# Optimizing a Trainium2 kernel written in Bass

```python
import numpy as np
import jax
import jax.numpy as jnp

def _softmax(x, axis=-1):
    return jax.nn.softmax(x, axis=axis)

def _gelu(x):
    return jax.nn.gelu(x, approximate=True)

def _silu(x):
    return jax.nn.silu(x)

def _sigmoid(x):
    return jax.nn.sigmoid(x)

def _layernorm(x, axis=-1, eps=1e-05):
    m = jnp.mean(x, axis=axis, keepdims=True)
    v = jnp.var(x, axis=axis, keepdims=True)
    return (x - m) / jnp.sqrt(v + eps)

def _scatter_add(tgt, idx, src, axis=0):
    return tgt.at[idx].add(src)

def _segment_sum(src, seg, n):
    return jax.ops.segment_sum(src, seg, n)
kernel_name = 'mk_lm_tower_d1_tok_ids1024_r4_458414'

def setup_inputs(seed: int=0):
    np.random.seed(seed)
    _w = jnp.asarray

    def _rec_inputs():
        import jax
        import jax.numpy as jnp
        _rk = jax.random.key(seed)
        x = jax.random.randint(jax.random.fold_in(_rk, 1), (16, 128), 0, 31983, jnp.int32)
        return x
    x = _rec_inputs()

    def _L0_tok_setup():
        import jax, jax.numpy as jnp
        import numpy as np
        L, D, H, B, S, V = (4, 256, 16, 8, 128, 8000)
        DK = D // H
        FF = 4 * D
        EPS = 0.001

        def _bn(x, gamma, beta, mean, var):
            return gamma * (x - mean) * jax.lax.rsqrt(var + EPS) + beta
        key = jax.random.key(seed)
        keys = iter(jax.random.split(key, 40))

        def rn(shape, scale=0.02):
            return jax.random.normal(next(keys), shape, jnp.float32) * scale
        sequence = jax.random.randint(next(keys), (B, S), 0, V, dtype=jnp.int32)
        pos = np.arange(S)[:, None].astype(np.float32)
        i = np.arange(D)[None, :]
        angle = pos / np.power(10000.0, 2 * (i // 2) / D).astype(np.float32)
        pes = np.where(i % 2 == 0, np.sin(angle), np.cos(angle)).astype(np.float32)
        return {'sequence': sequence, 'emb': rn((V, D)), 'pes': jnp.asarray(pes), 'wq': rn((L, D, DK)), 'bq': jnp.zeros((L, DK)), 'wk': rn((L, D, DK)), 'bk': jnp.zeros((L, DK)), 'wv': rn((L, D, DK)), 'bv': jnp.zeros((L, DK)), 'wo': rn((L, DK, D)), 'bo': jnp.zeros((L, D)), 'att_gamma': 1.0 + rn((L, D), 0.1), 'att_beta': rn((L, D), 0.1), 'att_mean': rn((L, D), 0.1), 'att_var': jnp.ones((L, D)), 'w1': rn((L, D, FF)), 'bff1': jnp.zeros((L, FF)), 'w2': rn((L, FF, D)), 'bff2': jnp.zeros((L, D)), 'ffn_gamma': 1.0 + rn((L, D), 0.1), 'ffn_beta': rn((L, D), 0.1), 'ffn_mean': rn((L, D), 0.1), 'ffn_var': jnp.ones((L, D))}
    _L0_tok_all = _L0_tok_setup()
    _L0_tok_in = {k: v for k, v in _L0_tok_all.items() if k in ('emb', 'pes', 'wq', 'bq', 'wk', 'bk', 'wv', 'bv', 'wo', 'bo', 'att_gamma', 'att_beta', 'att_mean', 'att_var', 'w1', 'bff1', 'w2', 'bff2', 'ffn_gamma', 'ffn_beta', 'ffn_mean', 'ffn_var')}
    del _L0_tok_all

    def _L0_attn_setup():
        import jax, jax.numpy as jnp
        import numpy as np
        D = 256
        H = 16
        N = D // H
        B = 4
        T = 512
        NLAYERS = 12
        LAYER_ID = 6
        EPS = 1e-05 * 64

        def _forward(x, w_r, w_k, w_v, w_g, w_o, time_maa_k, time_maa_v, time_maa_r, time_maa_g, time_decay, time_faaaa, ln_g, ln_b):
            Bs, Ts, C = x.shape
            if Ts % 64 == 0:
                Q = 64
            elif Ts % 128 == 0:
                Q = 128
            else:
                Q = Ts
            nC = Ts // Q
            xs = jnp.pad(x, ((0, 0), (1, 0), (0, 0)))[:, :-1]
            xx = xs - x
            xk = x + xx * time_maa_k
            xv = x + xx * time_maa_v
            xr = x + xx * time_maa_r
            xg = x + xx * time_maa_g
            r = (xr @ w_r.T).reshape(Bs, Ts, H, N).transpose(0, 2, 1, 3)
            k = (xk @ w_k.T).reshape(Bs, Ts, H, N).transpose(0, 2, 3, 1)
            v = (xv @ w_v.T).reshape(Bs, Ts, H, N).transpose(0, 2, 1, 3)
            g = jax.nn.silu(xg @ w_g.T)
            w = jnp.exp(-jnp.exp(time_decay))
            u = time_faaaa
            ws = (w ** Q)[None, :, None, None]
            q = jnp.arange(Q)
            wk = (w[:, None] ** (Q - 1 - q)[None, :])[None, :, None, :]
            wb = (w[:, None] ** q[None, :])[None, :, :, None]
            ii = q[:, None]
            jj = q[None, :]
            e = jnp.maximum(ii - jj - 1, 0)
            Wmat = jnp.where((jj < ii)[None], w[:, None, None] ** e[None], 0.0)
            Wmat = Wmat + jnp.eye(Q, dtype=x.dtype)[None] * u[:, None, None]
            Wmat = Wmat[None]
            rC = r.reshape(Bs, H, nC, Q, N).transpose(2, 0, 1, 3, 4)
            kC = k.reshape(Bs, H, N, nC, Q).transpose(3, 0, 1, 2, 4)
            vC = v.reshape(Bs, H, nC, Q, N).transpose(2, 0, 1, 3, 4)

            def step(state, inp):
                rr, kk, vv = inp
                y = rr @ kk * Wmat @ vv + rr @ state * wb
                state = ws * state + kk * wk @ vv
                return (state, y)
            state0 = jnp.zeros((Bs, H, N, N), x.dtype)
            _, yC = jax.lax.scan(step, state0, (rC, kC, vC))
            y = yC.transpose(1, 2, 0, 3, 4).reshape(Bs, H, Ts, N)
            y = y.transpose(0, 2, 1, 3).reshape(Bs * Ts, H, N)
            mu = y.mean(-1, keepdims=True)
            var = y.var(-1, keepdims=True)
            y = (y - mu) / jnp.sqrt(var + EPS)
            y = y.reshape(Bs, Ts, C) * ln_g + ln_b
            y = y * g
            return y @ w_o.T
        key = jax.random.key(seed)
        ks = jax.random.split(key, 6)
        r01 = LAYER_ID / (NLAYERS - 1)
        r10 = 1.0 - LAYER_ID / NLAYERS
        ddd = np.arange(D, dtype=np.float64) / D
        maa_k = (1.0 - ddd ** r10).astype(np.float32)
        maa_v = (1.0 - (ddd ** r10 + 0.3 * r01)).astype(np.float32)
        maa_r = (1.0 - ddd ** (0.5 * r10)).astype(np.float32)
        maa_g = maa_r.copy()
        hh = np.arange(H, dtype=np.float64)
        decay = (-6.0 + 5.0 * (hh / (H - 1)) ** (0.7 + 1.3 * r01)).astype(np.float32)
        faaaa = (r01 * (1.0 - hh / (H - 1))).astype(np.float32)
        s = 0.02
        return {'x': jax.random.normal(ks[0], (B, T, D), jnp.float32), 'w_r': jax.random.normal(ks[1], (D, D), jnp.float32) * s, 'w_k': jax.random.normal(ks[2], (D, D), jnp.float32) * s, 'w_v': jax.random.normal(ks[3], (D, D), jnp.float32) * s, 'w_g': jax.random.normal(ks[4], (D, D), jnp.float32) * s, 'w_o': jax.random.normal(ks[5], (D, D), jnp.float32) * s, 'time_maa_k': jnp.asarray(maa_k), 'time_maa_v': jnp.asarray(maa_v), 'time_maa_r': jnp.asarray(maa_r), 'time_maa_g': jnp.asarray(maa_g), 'time_decay': jnp.asarray(decay), 'time_faaaa': jnpp if False else jnp.asarray(faaaa), 'ln_g': jnp.ones((D,), jnp.float32), 'ln_b': jnp.zeros((D,), jnp.float32)}
    _L0_attn_all = _L0_attn_setup()
    _L0_attn_in = {k: v for k, v in _L0_attn_all.items() if k in ('w_r', 'w_k', 'w_v', 'w_g', 'w_o', 'time_maa_k', 'time_maa_v', 'time_maa_r', 'time_maa_g', 'time_decay', 'time_faaaa', 'ln_g', 'ln_b')}
    del _L0_attn_all

    def _L0_ffn_setup():
        import jax, jax.numpy as jnp
        import numpy as np
        K_TOP = 2
        key = jax.random.key(seed)
        k1, k2, k3 = jax.random.split(key, 3)
        B, S, H, E = (4, 512, 256, 8)
        hidden_states = jax.random.normal(k1, (B, S, H), dtype=jnp.float32)
        router_w = jax.random.normal(k2, (E, H), dtype=jnp.float32) * 0.02
        expert_weights = jax.random.normal(k3, (E, H, H), dtype=jnp.float32) * 0.02
        return {'hidden_states': hidden_states, 'router_w': router_w, 'expert_weights': expert_weights}
    _L0_ffn_all = _L0_ffn_setup()
    _L0_ffn_in = {k: v for k, v in _L0_ffn_all.items() if k in ('router_w', 'expert_weights')}
    del _L0_ffn_all
    return {'x': x, 'L0_tok_emb': _L0_tok_in['emb'], 'L0_tok_pes': _L0_tok_in['pes'], 'L0_tok_wq': _L0_tok_in['wq'], 'L0_tok_bq': _L0_tok_in['bq'], 'L0_tok_wk': _L0_tok_in['wk'], 'L0_tok_bk': _L0_tok_in['bk'], 'L0_tok_wv': _L0_tok_in['wv'], 'L0_tok_bv': _L0_tok_in['bv'], 'L0_tok_wo': _L0_tok_in['wo'], 'L0_tok_bo': _L0_tok_in['bo'], 'L0_tok_att_gamma': _L0_tok_in['att_gamma'], 'L0_tok_att_beta': _L0_tok_in['att_beta'], 'L0_tok_att_mean': _L0_tok_in['att_mean'], 'L0_tok_att_var': _L0_tok_in['att_var'], 'L0_tok_w1': _L0_tok_in['w1'], 'L0_tok_bff1': _L0_tok_in['bff1'], 'L0_tok_w2': _L0_tok_in['w2'], 'L0_tok_bff2': _L0_tok_in['bff2'], 'L0_tok_ffn_gamma': _L0_tok_in['ffn_gamma'], 'L0_tok_ffn_beta': _L0_tok_in['ffn_beta'], 'L0_tok_ffn_mean': _L0_tok_in['ffn_mean'], 'L0_tok_ffn_var': _L0_tok_in['ffn_var'], 'L0_attn_w_r': _L0_attn_in['w_r'], 'L0_attn_w_k': _L0_attn_in['w_k'], 'L0_attn_w_v': _L0_attn_in['w_v'], 'L0_attn_w_g': _L0_attn_in['w_g'], 'L0_attn_w_o': _L0_attn_in['w_o'], 'L0_attn_time_maa_k': _L0_attn_in['time_maa_k'], 'L0_attn_time_maa_v': _L0_attn_in['time_maa_v'], 'L0_attn_time_maa_r': _L0_attn_in['time_maa_r'], 'L0_attn_time_maa_g': _L0_attn_in['time_maa_g'], 'L0_attn_time_decay': _L0_attn_in['time_decay'], 'L0_attn_time_faaaa': _L0_attn_in['time_faaaa'], 'L0_attn_ln_g': _L0_attn_in['ln_g'], 'L0_attn_ln_b': _L0_attn_in['ln_b'], 'L0_ffn_router_w': _L0_ffn_in['router_w'], 'L0_ffn_expert_weights': _L0_ffn_in['expert_weights']}

def reference(x, L0_tok_emb, L0_tok_pes, L0_tok_wq, L0_tok_bq, L0_tok_wk, L0_tok_bk, L0_tok_wv, L0_tok_bv, L0_tok_wo, L0_tok_bo, L0_tok_att_gamma, L0_tok_att_beta, L0_tok_att_mean, L0_tok_att_var, L0_tok_w1, L0_tok_bff1, L0_tok_w2, L0_tok_bff2, L0_tok_ffn_gamma, L0_tok_ffn_beta, L0_tok_ffn_mean, L0_tok_ffn_var, L0_attn_w_r, L0_attn_w_k, L0_attn_w_v, L0_attn_w_g, L0_attn_w_o, L0_attn_time_maa_k, L0_attn_time_maa_v, L0_attn_time_maa_r, L0_attn_time_maa_g, L0_attn_time_decay, L0_attn_time_faaaa, L0_attn_ln_g, L0_attn_ln_b, L0_ffn_router_w, L0_ffn_expert_weights):
    import jax
    import jax.numpy as jnp

    def _L0_tok_ref(sequence, emb, pes, wq, bq, wk, bk, wv, bv, wo, bo, att_gamma, att_beta, att_mean, att_var, w1, bff1, w2, bff2, ffn_gamma, ffn_beta, ffn_mean, ffn_var):
        import jax, jax.numpy as jnp
        import numpy as np
        L, D, H, B, S, V = (4, 256, 16, 8, 128, 8000)
        DK = D // H
        FF = 4 * D
        EPS = 0.001

        def _bn(x, gamma, beta, mean, var):
            return gamma * (x - mean) * jax.lax.rsqrt(var + EPS) + beta
        x = emb[sequence] + pes[:S, 0:1][None]
        scale = 1.0 / jnp.sqrt(jnp.float32(DK))
        for l in range(L):
            q = x @ wq[l] + bq[l]
            k = x @ wk[l] + bk[l]
            v = x @ wv[l] + bv[l]
            score = jnp.einsum('bqd,bkd->bqk', q, k) * scale
            head = jax.nn.softmax(score, axis=-1) @ v
            att = head @ wo[l] + bo[l]
            x = _bn(x + att, att_gamma[l], att_beta[l], att_mean[l], att_var[l])
            ffn = jax.nn.relu(x @ w1[l] + bff1[l]) @ w2[l] + bff2[l]
            x = _bn(x + ffn, ffn_gamma[l], ffn_beta[l], ffn_mean[l], ffn_var[l])
        return x

    def _L0_attn_ref(x, w_r, w_k, w_v, w_g, w_o, time_maa_k, time_maa_v, time_maa_r, time_maa_g, time_decay, time_faaaa, ln_g, ln_b):
        import jax, jax.numpy as jnp
        import numpy as np
        D = 256
        H = 16
        N = D // H
        B = 4
        T = 512
        NLAYERS = 12
        LAYER_ID = 6
        EPS = 1e-05 * 64

        def _forward(x, w_r, w_k, w_v, w_g, w_o, time_maa_k, time_maa_v, time_maa_r, time_maa_g, time_decay, time_faaaa, ln_g, ln_b):
            Bs, Ts, C = x.shape
            if Ts % 64 == 0:
                Q = 64
            elif Ts % 128 == 0:
                Q = 128
            else:
                Q = Ts
            nC = Ts // Q
            xs = jnp.pad(x, ((0, 0), (1, 0), (0, 0)))[:, :-1]
            xx = xs - x
            xk = x + xx * time_maa_k
            xv = x + xx * time_maa_v
            xr = x + xx * time_maa_r
            xg = x + xx * time_maa_g
            r = (xr @ w_r.T).reshape(Bs, Ts, H, N).transpose(0, 2, 1, 3)
            k = (xk @ w_k.T).reshape(Bs, Ts, H, N).transpose(0, 2, 3, 1)
            v = (xv @ w_v.T).reshape(Bs, Ts, H, N).transpose(0, 2, 1, 3)
            g = jax.nn.silu(xg @ w_g.T)
            w = jnp.exp(-jnp.exp(time_decay))
            u = time_faaaa
            ws = (w ** Q)[None, :, None, None]
            q = jnp.arange(Q)
            wk = (w[:, None] ** (Q - 1 - q)[None, :])[None, :, None, :]
            wb = (w[:, None] ** q[None, :])[None, :, :, None]
            ii = q[:, None]
            jj = q[None, :]
            e = jnp.maximum(ii - jj - 1, 0)
            Wmat = jnp.where((jj < ii)[None], w[:, None, None] ** e[None], 0.0)
            Wmat = Wmat + jnp.eye(Q, dtype=x.dtype)[None] * u[:, None, None]
            Wmat = Wmat[None]
            rC = r.reshape(Bs, H, nC, Q, N).transpose(2, 0, 1, 3, 4)
            kC = k.reshape(Bs, H, N, nC, Q).transpose(3, 0, 1, 2, 4)
            vC = v.reshape(Bs, H, nC, Q, N).transpose(2, 0, 1, 3, 4)

            def step(state, inp):
                rr, kk, vv = inp
                y = rr @ kk * Wmat @ vv + rr @ state * wb
                state = ws * state + kk * wk @ vv
                return (state, y)
            state0 = jnp.zeros((Bs, H, N, N), x.dtype)
            _, yC = jax.lax.scan(step, state0, (rC, kC, vC))
            y = yC.transpose(1, 2, 0, 3, 4).reshape(Bs, H, Ts, N)
            y = y.transpose(0, 2, 1, 3).reshape(Bs * Ts, H, N)
            mu = y.mean(-1, keepdims=True)
            var = y.var(-1, keepdims=True)
            y = (y - mu) / jnp.sqrt(var + EPS)
            y = y.reshape(Bs, Ts, C) * ln_g + ln_b
            y = y * g
            return y @ w_o.T
        return _forward(x, w_r, w_k, w_v, w_g, w_o, time_maa_k, time_maa_v, time_maa_r, time_maa_g, time_decay, time_faaaa, ln_g, ln_b)

    def _L0_ffn_ref(hidden_states, router_w, expert_weights):
        import jax, jax.numpy as jnp
        import numpy as np
        K_TOP = 2
        B, S, H = hidden_states.shape
        x = hidden_states.reshape(-1, H)
        logits = x @ router_w.T
        probs = jax.nn.softmax(logits, axis=-1)
        topk_vals, topk_idx = jax.lax.top_k(probs, K_TOP)
        topk_w = topk_vals / (topk_vals.sum(-1, keepdims=True) + 1e-06)
        expert_out = jnp.einsum('nh,eho->eno', x, expert_weights)
        combined = jnp.take_along_axis(expert_out.transpose(1, 0, 2), topk_idx[:, :, None], axis=1)
        combined = combined.transpose(1, 0, 2)
        remap_bias = jnp.take_along_axis(probs, topk_idx, axis=1).T[:, :, None]
        weights = topk_w.T[:, :, None]
        out = ((combined + remap_bias) * weights).sum(axis=0)
        return out.reshape(B, S, H)
    h = _L0_tok_ref(x, L0_tok_emb, L0_tok_pes, L0_tok_wq, L0_tok_bq, L0_tok_wk, L0_tok_bk, L0_tok_wv, L0_tok_bv, L0_tok_wo, L0_tok_bo, L0_tok_att_gamma, L0_tok_att_beta, L0_tok_att_mean, L0_tok_att_var, L0_tok_w1, L0_tok_bff1, L0_tok_w2, L0_tok_bff2, L0_tok_ffn_gamma, L0_tok_ffn_beta, L0_tok_ffn_mean, L0_tok_ffn_var)
    h = h + _L0_attn_ref(_layernorm(h, axis=-1), L0_attn_w_r, L0_attn_w_k, L0_attn_w_v, L0_attn_w_g, L0_attn_w_o, L0_attn_time_maa_k, L0_attn_time_maa_v, L0_attn_time_maa_r, L0_attn_time_maa_g, L0_attn_time_decay, L0_attn_time_faaaa, L0_attn_ln_g, L0_attn_ln_b)
    h = h + _L0_ffn_ref(_layernorm(h, axis=-1), L0_ffn_router_w, L0_ffn_expert_weights)
    return h

_drawn_inputs = setup_inputs


def setup_inputs(seed=0):
    import zlib

    import numpy as np

    out = dict(_drawn_inputs(seed))
    spreads = {'L0_tok_bq': (0.0, 0.8),
     'L0_tok_bk': (0.0, 2.0),
     'L0_tok_bv': (0.0, 0.1),
     'L0_tok_bo': (0.0, 0.1),
     'L0_tok_att_var': (1.0, 0.2),
     'L0_tok_bff1': (0.0, 0.1),
     'L0_tok_bff2': (0.0, 0.1),
     'L0_tok_ffn_var': (1.0, 0.2),
     'L0_attn_ln_g': (1.0, 0.6),
     'L0_attn_ln_b': (0.0, 0.481)}
    factors = {'L0_tok_wq': 8.0,
     'L0_tok_wk': 8.0,
     'L0_attn_time_maa_k': 8.0,
     'L0_attn_time_maa_v': 8.0,
     'L0_attn_time_maa_r': 4.01,
     'L0_attn_time_maa_g': 8.0,
     'L0_attn_time_decay': 41.728,
     'L0_attn_time_faaaa': 28.26}
    for name, (base, spread) in spreads.items():
        noise = np.random.default_rng([zlib.crc32(name.encode()), seed]).standard_normal(out[name].shape)
        drawn = base * np.exp(spread * noise) if base else spread * noise
        out[name] = jnp.asarray(drawn.astype(out[name].dtype))
    for name, factor in factors.items():
        out[name] = (out[name] * factor).astype(out[name].dtype)
    return out
```

```python
import concourse.bass as bass
from concourse import mybir
from contextlib import ExitStack

L, D, DK, FF = 4, 256, 16, 1024
NSEQ, T = 16, 128
V = 8000
P = 128
KT = D // P
MT = FF // P
CHUNK = 4
CT = CHUNK * T
NCH = NSEQ // CHUNK
BN_EPS = 1e-3
QROW, KROW, VROW = 0, 32, 64
QKVROWS = 96
RING = 4
NH = 16
DH = D // NH
LN_EPS = 1e-5
GN_EPS = 1e-5 * 64
RATE_MAX = 200.0
NE, TOPK = 8, 2
TOP_EPS = 1e-6
QUAD = 4
WCOLS = KT * P + D


def tower(nc, ids, emb, pes, w_ffn, w_qkv, w_o, bn_raw, qkv_bias, ff_bias, ident_in, w_exp, w_mix, w_router,
          maa_in, decay, bonus, ln_affine, gap, later, even_odd, expert_no, out):
    fp32, fp32r = mybir.dt.float32, mybir.dt.float32r
    keep = ExitStack()
    with keep:
        def lasting(name, shape, dt=fp32):
            return keep.enter_context(nc.sbuf_tensor(name, shape, dt))

        xT = lasting("xT", [P, KT, NSEQ * T])
        ident = lasting("ident", [P, P])
        exp_hi = lasting("exp_hi", [P, KT, NE * D], fp32r)
        exp_lo = lasting("exp_lo", [P, KT, NE * D], fp32r)
        decays = lasting("decays", [P, NH, T])
        bank = [keep.enter_context(nc.psum_tensor(f"bank{i}", [P, 512], fp32)) for i in range(8)]
        transformer(nc, bank, xT, ident, exp_hi, exp_lo, decays, ids, emb, pes, w_ffn, w_qkv, w_o, bn_raw, qkv_bias,
                    ff_bias, ident_in, w_exp, decay, bonus, gap, later)
        mixer_and_experts(nc, bank, xT, ident, exp_hi, exp_lo, decays, w_mix, w_router, maa_in, ln_affine, even_odd,
                          expert_no, out)


def three(nc, out_, w, x, first, last):
    (wh, wl), (xh, xl) = w, x
    nc.tensor.matmul(out_, wh, xh, start=first, stop=False)
    nc.tensor.matmul(out_, wh, xl, start=False, stop=False)
    return nc.tensor.matmul(out_, wl, xh, start=False, stop=last)


def transformer(nc, bank, xT, ident, exp_hi, exp_lo, decays, ids, emb, pes, w_ffn, w_qkv, w_o, bn_raw, qkv_bias, ff_bias,
                ident_in, w_exp, decay, bonus, gap, later):
    fp32, fp32r, i32 = mybir.dt.float32, mybir.dt.float32r, mybir.dt.int32
    ALU, ACT, AX = mybir.AluOpType, mybir.ActivationFunctionType, mybir.AxisListType

    ctx = ExitStack()
    with ctx:
        def sb(name, shape, dt=fp32):
            return ctx.enter_context(nc.sbuf_tensor(name, shape, dt))

        def sem(name):
            return ctx.enter_context(nc.semaphore(name))

        ids_sb = sb("ids_sb", [P, NSEQ], i32)
        id_wrap = sb("id_wrap", [P, NSEQ], i32)
        id_row = sb("id_row", [P, NSEQ], i32)
        tok = sb("tok", [P, NSEQ, D])
        pes_sb = sb("pes_sb", [P, 1])

        w_raw = sb("w_raw", [P, MT, WCOLS])
        w_hi = sb("w_hi", [P, MT, WCOLS], fp32r)
        w_lo = sb("w_lo", [P, MT, WCOLS], fp32r)
        qkv_all = sb("qkv_all", [P, L, KT * QKVROWS])
        qkv_w = sb("qkv_w", [P, KT * QKVROWS])
        wo_all = sb("wo_all", [DK, L, D])
        wo_w = sb("wo_w", [DK, D])
        raw = sb("raw", [P, 5, 2, L, KT])
        norm_all = sb("norm_all", [P, 2, L, 2, KT])
        norm_tmp = sb("norm_tmp", [P, 2, L, KT])
        minus_half = sb("minus_half", [P, 2 * L * KT])
        qkvb_all = sb("qkvb_all", [QKVROWS, L])
        ffb_all = sb("ffb_all", [P, L, MT])
        qkvb = sb("qkvb", [QKVROWS, 1])
        ffb = sb("ffb", [P, MT])
        bn1 = sb("bn1", [P, 2, KT])
        bn2 = sb("bn2", [P, 2, KT])

        qT = sb("qT", [DK, CT])
        kT = sb("kT", [DK, CT])
        vT = sb("vT", [DK, CT])
        vtok = sb("vtok", [P, CHUNK, DK])
        smax = sb("smax", [P, CHUNK])
        nbias = sb("nbias", [P, CHUNK])
        ssum = sb("ssum", [P, CHUNK])
        rsum = sb("rsum", [P, CHUNK])
        prob = sb("prob", [P, CHUNK, T])
        probT = sb("probT", [P, CHUNK, T])
        headT = sb("headT", [DK, CT])
        z1 = sb("z1", [P, KT, CT])
        z2 = sb("z2", [P, KT, CT])
        x1 = sb("x1", [P, 2, KT, CT])
        x1_hi = sb("x1_hi", [P, 2, KT, CT], fp32r)
        x1_lo = sb("x1_lo", [P, 2, KT, CT], fp32r)
        hid = sb("hid", [P, 2, CT])
        hid_hi = sb("hid_hi", [P, RING, CT], fp32r)
        hid_lo = sb("hid_lo", [P, RING, CT], fp32r)

        H = [bank[0], bank[1]]
        Y = [bank[2], bank[3]]
        A = bank[4]
        S = bank[5]
        O = [bank[6], bank[7]]

        s_ids, s_misc, s_wl = sem("s_ids"), sem("s_misc"), sem("s_wl")
        s_gather = [sem(f"s_gather{c}") for c in range(NCH)]
        s_idx, s_pre, s_emb = sem("s_idx"), sem("s_pre"), sem("s_emb")
        s_w_lo, s_attw, s_attv, s_ffb, s_bn2 = sem("s_w_lo"), sem("s_attw"), sem("s_attv"), sem("s_ffb"), sem("s_bn2")
        s_wov = sem("s_wov")
        s_q, s_v, s_vtok, s_max, s_nb, s_rs, s_prob = (sem("s_q"), sem("s_v"), sem("s_vtok"), sem("s_max"),
                                                       sem("s_nb"), sem("s_rs"), sem("s_prob"))
        s_head, s_z1, s_x1lo, s_hlo, s_z2 = sem("s_head"), sem("s_z1"), sem("s_x1lo"), sem("s_hlo"), sem("s_z2")
        s_w_hi, s_k, s_exp, s_pT, s_x1, s_x1hi = (sem("s_w_hi"), sem("s_k"), sem("s_exp"), sem("s_pT"),
                                                  sem("s_x1"), sem("s_x1hi"))
        s_relu, s_hhi, s_x = sem("s_relu"), sem("s_hhi"), sem("s_x")
        s_eT, s_qkv, s_vt, s_sc, s_pt, s_pv, s_wo = (sem("s_eT"), sem("s_qkv"), sem("s_vt"), sem("s_sc"),
                                                     sem("s_pt"), sem("s_pv"), sem("s_wo"))
        s_h, s_y = sem("s_h"), sem("s_y")
        s_exp_raw, s_exp_hi, s_dec, s_rate, s_decay, s_masked = (sem("s_exp_raw"), sem("s_exp_hi"), sem("s_dec"), sem("s_rate"),
                                                       sem("s_decay"), sem("s_masked"))
        rate = sb("rate", [P, NH])
        bonus_sb = sb("bonus_sb", [P, NH])
        gap_sb = sb("gap_sb", [P, T])
        later_sb = sb("later_sb", [P, T])
        exp_raw = tok[:].rearrange("p n d -> p (n d)").rearrange("p (k e) -> p k e", k=KT)
        s_pow = sem("s_pow")
        CREDIT = {s_relu: 2, s_hlo: 2, s_y: RING, s_z2: KT}

        def after(s, n):
            return n + CREDIT.get(s, 0)

        def wait_after(eng, s, n):
            if not (isinstance(n, int) and after(s, n) <= 0):
                eng.wait_ge(s, after(s, n))

        def following(l, c):
            return (l, c + 1) if c < NCH - 1 else (l + 1, 0)

        block = ctx.enter_context(nc.Block())

        @block.sync
        def _(sp):
            sp.dma_start(ids_sb[:], ids).then_inc(s_ids, 16)
            sp.dma_start(pes_sb[:], pes).then_inc(s_misc, 16)
            sp.dma_start(ident[:], ident_in).then_inc(s_misc, 16)
            sp.dma_start(raw[:], bn_raw).then_inc(s_misc, 16)
            sp.dma_start(qkv_all[:], w_qkv).then_inc(s_misc, 16)
            sp.dma_start(wo_all[:], w_o).then_inc(s_misc, 16)
            sp.dma_start(qkvb_all[:], qkv_bias).then_inc(s_misc, 16)
            sp.dma_start(ffb_all[:], ff_bias).then_inc(s_misc, 16)
            sp.dma_start(w_raw[:], w_ffn[0]).then_inc(s_wl, 16)
            for dst, src in ((rate, decay), (bonus_sb, bonus), (gap_sb, gap), (later_sb, later)):
                sp.dma_start(dst[:], src).then_inc(s_dec, 16)
            sp.wait_ge(s_eT, NCH)
            sp.dma_start(exp_raw, w_exp).then_inc(s_exp_raw, 16)
            with sp.Fori(0, L - 1) as l:
                sp.wait_ge(s_w_lo, MT * l + MT)
                sp.dma_start(w_raw[:], w_ffn[bass.ds(l + 1, 1), :, :, :]).then_inc(s_wl, 16)

        @block.gpsimd
        def _(pool):
            pool.wait_ge(s_idx, 3)
            for n in range(NSEQ):
                pool.indirect_dma_start(tok[:, n, :], None, emb,
                                        bass.IndirectOffsetOnAxis(ap=id_row[:, n:n + 1], axis=0)).then_inc(s_gather[n // CHUNK], 16)
            pool.wait_ge(s_pre, 2)
            flat = norm_tmp[:].rearrange("p a l k -> p (a l k)")
            nc.gpsimd.tensor_tensor(flat, flat, minus_half[:], ALU.pow).then_inc(s_pow, 1)

        @block.tensor
        def _(pe):
            def qkv(l, c):
                a = NCH * l + c
                pe.wait_ge(s_attw, l + 1)
                pe.wait_ge(s_x, KT * (a + 1))
                wait_after(pe, s_pT, a)
                for kt in range(KT):
                    last = nc.tensor.matmul(A[0:QKVROWS, :], qkv_w[:, kt * QKVROWS:(kt + 1) * QKVROWS],
                                            xT[:, kt, c * CT:(c + 1) * CT], start=kt == 0, stop=kt == KT - 1)
                last.then_inc(s_qkv, 1)

            def scores(l, c):
                a = NCH * l + c
                pe.wait_ge(s_v, a + 1)
                wait_after(pe, s_z1, KT * a)
                pe.wait_ge(s_k, a + 1)
                wait_after(pe, s_head, a)
                pe.wait_ge(s_q, a + 1)
                for n in range(CHUNK):
                    last = nc.tensor.matmul(S[:, n * T:(n + 1) * T], qT[:, n * T:(n + 1) * T],
                                            kT[:, n * T:(n + 1) * T], start=True, stop=True)
                last.then_inc(s_sc, 1)
                for n in range(CHUNK):
                    last = nc.tensor.transpose(O[0][:, n * DK:(n + 1) * DK], vT[:, n * T:(n + 1) * T],
                                               ident[0:DK, 0:DK])
                last.then_inc(s_vt, 1)

            def turn_probs(l, c):
                pe.wait_ge(s_prob, NCH * l + c + 1)
                for n in range(CHUNK):
                    last = nc.tensor.transpose(A[:, n * T:(n + 1) * T], prob[:, n, :], ident[:])
                last.then_inc(s_pt, 1)

            def head(l, c):
                a = NCH * l + c
                pe.wait_ge(s_pT, a + 1)
                pe.wait_ge(s_vtok, a + 1)
                for n in range(CHUNK):
                    last = nc.tensor.matmul(S[0:DK, n * T:(n + 1) * T], vtok[:, n, :], probT[:, n, :],
                                            start=True, stop=True)
                last.then_inc(s_pv, 1)

            def project(l, c):
                pe.wait_ge(s_attv, l + 1)
                pe.wait_ge(s_head, NCH * l + c + 1)
                for kt in range(KT):
                    last = nc.tensor.matmul(O[kt][:], wo_w[:, kt * P:(kt + 1) * P], headT[:], start=True, stop=True)
                last.then_inc(s_wo, 1)

            def hidden(l, c, m):
                s = NCH * l + c
                if m == 0:
                    pe.wait_ge(s_x1lo, s + 1)
                if c == 0:
                    pe.wait_ge(s_w_lo, MT * l + m + 1)
                pe.wait_ge(s_relu, after(s_relu, MT * s + m - 1))
                for kt in range(KT):
                    w = [t[:, m, kt * P:(kt + 1) * P] for t in (w_hi, w_lo)]
                    last = three(nc, H[m % 2][:], w, [t[:, c % 2, kt, :] for t in (x1_hi, x1_lo)], kt == 0, kt == KT - 1)
                last.then_inc(s_h, 1)

            def second(l, c, m):
                s = NCH * l + c
                pe.wait_ge(s_hlo, after(s_hlo, MT * s + m + 1))
                if m == 0:
                    pe.wait_ge(s_z2, after(s_z2, KT * s))
                for kt in range(KT):
                    w = [t[:, m, KT * P + kt * P:KT * P + (kt + 1) * P] for t in (w_hi, w_lo)]
                    last = three(nc, Y[kt][:], w, [t[:, m % RING, :] for t in (hid_hi, hid_lo)], m == 0, m == MT - 1)
                last.then_inc(s_y, 1)

            def step(l, c, attend=True):
                nxt = following(l, c)
                for m in range(MT):
                    if attend and m == 0:
                        qkv(*nxt)
                    if attend and m == 4:
                        turn_probs(*nxt)
                    if attend and m == 5:
                        head(*nxt)
                    if attend and m == 6:
                        project(*nxt)
                    hidden(l, c, m)
                    if attend and m == 1:
                        scores(*nxt)
                    if m >= 2:
                        second(l, c, m - 2)
                second(l, c, MT - 2)
                second(l, c, MT - 1)

            pe.sem_inc(s_y, CREDIT[s_y])
            pe.wait_ge(s_misc, 7 * 16)
            for c in range(NCH):
                pe.wait_ge(s_emb, c + 1)
                if c >= 2:
                    pe.wait_ge(s_x, KT * (c - 1))
                for n in range(CHUNK):
                    for kt in range(KT):
                        last = nc.tensor.transpose((O, Y)[c % 2][kt][:, n * T:(n + 1) * T],
                                                   tok[:, c * CHUNK + n, kt * P:(kt + 1) * P], ident[:])
                last.then_inc(s_eT, 1)
            pe.wait_ge(s_x, KT * NCH)
            for part in (qkv, scores, turn_probs, head, project):
                part(0, 0)
            with pe.Fori(0, L - 1) as l:
                for c in range(NCH):
                    step(l, c)
            for c in range(NCH):
                step(L - 1, c, attend=c < NCH - 1)

        @block.scalar
        def _(act):
            def turn_k(l, c):
                act.wait_ge(s_qkv, NCH * l + c + 1)
                act.wait_ge(s_attv, l + 1)
                nc.scalar.activation(kT[:], A[KROW:KROW + DK, :], ACT.Identity,
                                     bias=qkvb[KROW:KROW + DK, :]).then_inc(s_k, 1)

            def exps(l, c):
                act.wait_ge(s_nb, NCH * l + c + 1)
                for n in range(CHUNK):
                    last = nc.scalar.activation(prob[:, n, :], S[:, n * T:(n + 1) * T], ACT.Exp, bias=nbias[:, n:n + 1],
                                                scale=DK ** -0.5, accum_out=ssum[:, n:n + 1])
                last.then_inc(s_exp, 1)

            def copy_probT(l, c):
                act.wait_ge(s_pt, NCH * l + c + 1)
                nc.scalar.copy(probT[:].rearrange("p n t -> p (n t)"), A[:]).then_inc(s_pT, 1)

            def norm1(l, c):
                a = NCH * l + c
                for kt in range(KT):
                    act.wait_ge(s_z1, KT * a + kt + 1)
                    nc.scalar.activation(x1[:, c % 2, kt, :], z1[:, kt, :], ACT.Identity, bias=bn1[:, 1, kt:kt + 1],
                                         scale=bn1[:, 0, kt:kt + 1]).then_inc(s_x1, 1)
                act.wait_ge(s_x1, KT * (a + 1))
                nc.scalar.copy(x1_hi[:, c % 2, :, :], x1[:, c % 2, :, :]).then_inc(s_x1hi, 1)

            def relu(l, c, m):
                n = MT * (NCH * l + c) + m
                if c == 0 and m == 0:
                    act.wait_ge(s_ffb, l + 1)
                act.wait_ge(s_h, n + 1)
                act.wait_ge(s_hlo, after(s_hlo, n - 1))
                nc.scalar.activation(hid[:, m % 2, :], H[m % 2][:], ACT.Relu, bias=ffb[:, m:m + 1]).then_inc(s_relu, 1)
                act.wait_ge(s_relu, after(s_relu, n + 1))
                act.wait_ge(s_y, after(s_y, n + 1 - RING))
                nc.scalar.copy(hid_hi[:, m % RING, :], hid[:, m % 2, :]).then_inc(s_hhi, 1)

            def norm2(l, c):
                for kt in range(KT):
                    if c == 0:
                        act.wait_ge(s_bn2, l + 1)
                    act.wait_ge(s_z2, after(s_z2, KT * (NCH * l + c) + kt + 1))
                    nc.scalar.activation(xT[:, kt, c * CT:(c + 1) * CT], z2[:, kt, :], ACT.Identity,
                                         bias=bn2[:, 1, kt:kt + 1], scale=bn2[:, 0, kt:kt + 1]).then_inc(s_x, 1)

            def split_high(l, m):
                act.wait_ge(s_wl, 16 * l + 16)
                if not isinstance(l, int):
                    act.wait_ge(s_y, after(s_y, MT * (NCH * l - 1) + m + 1))
                nc.scalar.copy(w_hi[:, m, :], w_raw[:, m, :]).then_inc(s_w_hi, 1)

            def step(l, c, attend=True, refresh=True):
                nxt = following(l, c)
                refresh = refresh and c == NCH - 1
                for m in range(MT):
                    if attend and m == 0:
                        turn_k(*nxt)
                    if attend and m == 4:
                        copy_probT(*nxt)
                    relu(l, c, m)
                    if attend and m == 2:
                        exps(*nxt)
                    if attend and m == 6:
                        norm1(*nxt)
                    if refresh and m >= 3:
                        split_high(l + 1, m - 3)
                norm2(l, c)
                if refresh:
                    for m in range(MT - 3, MT):
                        split_high(l + 1, m)

            def expert_high(i):
                if i == 0:
                    act.wait_ge(s_exp_raw, 16)
                cols = slice(i * D, (i + 1) * D)
                nc.scalar.copy(exp_hi[:, :, cols], exp_raw[:, :, cols]).then_inc(s_exp_hi, 1)

            def decay_rate():
                act.wait_ge(s_dec, 4 * 16)
                nc.scalar.activation(rate[:], rate[:], ACT.Exp).then_inc(s_rate, 1)

            def decay_row(h):
                if h == 0:
                    act.wait_ge(s_rate, 2)
                nc.scalar.activation(decays[:, h, :], gap_sb[:], ACT.Exp, scale=rate[:, h:h + 1]).then_inc(s_decay, 1)

            act.sem_inc(s_relu, CREDIT[s_relu])
            for c in range(NCH):
                act.wait_ge(s_eT, c + 1)
                for kt in range(KT):
                    nc.scalar.copy(xT[:, kt, c * CT:(c + 1) * CT], (O, Y)[c % 2][kt][:]).then_inc(s_x, 1)
            turn_k(0, 0)
            exps(0, 0)
            copy_probT(0, 0)
            norm1(0, 0)
            for m in range(MT):
                split_high(0, m)
            with act.Fori(0, L - 1) as l:
                for c in range(NCH):
                    step(l, c)
            decay_rate()
            for c in range(NCH):
                step(L - 1, c, attend=c < NCH - 1, refresh=False)
                for i in range(NE // NCH):
                    expert_high(NE // NCH * c + i)
                for i in range(NH // NCH):
                    decay_row(NH // NCH * c + i)

        @block.vector
        def _(dve):
            def turn_qv(l, c):
                a = NCH * l + c
                dve.wait_ge(s_qkv, a + 1)
                dve.wait_ge(s_attv, l + 1)
                nc.vector.tensor_scalar(qT[:], A[QROW:QROW + DK, :], qkvb[QROW:QROW + DK, :], None, ALU.add).then_inc(s_q, 1)
                nc.vector.tensor_scalar(vT[:], A[VROW:VROW + DK, :], qkvb[VROW:VROW + DK, :], None, ALU.add).then_inc(s_v, 1)

            def softmax_max(l, c):
                a = NCH * l + c
                dve.wait_ge(s_sc, a + 1)
                nc.vector.reduce_max(smax[:], S[:].rearrange("p (n t) -> p n t", n=CHUNK), AX.X).then_inc(s_max, 1)
                dve.wait_ge(s_max, a + 1)
                nc.vector.tensor_scalar(nbias[:], smax[:], -DK ** -0.5, None, ALU.mult).then_inc(s_nb, 1)
                dve.wait_ge(s_vt, a + 1)
                nc.vector.tensor_copy(vtok[:].rearrange("p n d -> p (n d)"), O[0][:, 0:CHUNK * DK]).then_inc(s_vtok, 1)

            def softmax_norm(l, c):
                a = NCH * l + c
                dve.wait_ge(s_exp, a + 1)
                nc.vector.reciprocal(rsum[:], ssum[:]).then_inc(s_rs, 1)
                dve.wait_ge(s_rs, a + 1)
                nc.vector.tensor_tensor(prob[:], prob[:], rsum[:].unsqueeze(2).to_broadcast([P, CHUNK, T]),
                                        ALU.mult).then_inc(s_prob, 1)

            def turn_head(l, c):
                dve.wait_ge(s_pv, NCH * l + c + 1)
                nc.vector.tensor_copy(headT[:], S[0:DK, :]).then_inc(s_head, 1)

            def residual1(l, c):
                a = NCH * l + c
                dve.wait_ge(s_wo, a + 1)
                wait_after(dve, s_x1, KT * a)
                for kt in range(KT):
                    nc.vector.tensor_tensor(z1[:, kt, :], O[kt][:], xT[:, kt, c * CT:(c + 1) * CT], ALU.add).then_inc(s_z1, 1)

            def split_x1(l, c):
                dve.wait_ge(s_x1hi, NCH * l + c + 1)
                nc.vector.tensor_tensor(x1_lo[:, c % 2, :, :], x1[:, c % 2, :, :], x1_hi[:, c % 2, :, :].bitcast(fp32),
                                        ALU.subtract).then_inc(s_x1lo, 1)

            def split_hidden(l, c, m):
                dve.wait_ge(s_hhi, MT * (NCH * l + c) + m + 1)
                nc.vector.tensor_tensor(hid_lo[:, m % RING, :], hid[:, m % 2, :], hid_hi[:, m % RING, :].bitcast(fp32),
                                        ALU.subtract).then_inc(s_hlo, 1)

            def residual2(l, c):
                s = NCH * l + c
                dve.wait_ge(s_y, after(s_y, MT * (s + 1)))
                dve.wait_ge(s_x, KT * (NCH + s))
                for kt in range(KT):
                    nc.vector.tensor_tensor(z2[:, kt, :], Y[kt][:], x1[:, c % 2, kt, :], ALU.add).then_inc(s_z2, 1)

            def split_low(l, m):
                dve.wait_ge(s_w_hi, MT * l + m + 1)
                nc.vector.tensor_tensor(w_lo[:, m, :], w_raw[:, m, :], w_hi[:, m, :].bitcast(fp32),
                                        ALU.subtract).then_inc(s_w_lo, 1)

            def layer(t, l):
                return t[:, bass.ds(l, 1), :]

            def place_qkv(l):
                if not isinstance(l, int):
                    dve.wait_ge(s_qkv, NCH * l)
                nc.vector.tensor_copy(qkv_w[:].unsqueeze(1), layer(qkv_all, l)).then_inc(s_attw, 1)

            def place_attention(l):
                if not isinstance(l, int):
                    dve.wait_ge(s_x1, KT * NCH * l)
                nc.vector.tensor_copy(wo_w[:].unsqueeze(1), layer(wo_all, l))
                nc.vector.tensor_copy(qkvb[:], qkvb_all[:, bass.ds(l, 1)])
                nc.vector.tensor_copy(bn1[:].rearrange("p k t -> p (k t)").unsqueeze(1), layer(norm1_all, l)).then_inc(s_attv, 1)

            def place_ffb(l):
                if not isinstance(l, int):
                    dve.wait_ge(s_relu, after(s_relu, MT * NCH * l))
                nc.vector.tensor_copy(ffb[:].unsqueeze(1), layer(ffb_all, l)).then_inc(s_ffb, 1)

            def place_bn2(l):
                dve.wait_ge(s_x, KT * NCH * (l + 1))
                nc.vector.tensor_copy(bn2[:].rearrange("p k t -> p (k t)").unsqueeze(1), layer(norm2_all, l)).then_inc(s_bn2, 1)

            def expert_low(i):
                dve.wait_ge(s_exp_hi, i + 1)
                cols = slice(i * D, (i + 1) * D)
                nc.vector.tensor_tensor(exp_lo[:, :, cols], exp_raw[:, :, cols], exp_hi[:, :, cols].bitcast(fp32), ALU.subtract)

            def decay_mask(h):
                dve.wait_ge(s_decay, h + 1)
                nc.vector.tensor_tensor(decays[:, h, :], decays[:, h, :], later_sb[:], ALU.mult).then_inc(s_masked, 1)
                dve.wait_ge(s_masked, h + 1)
                nc.vector.scalar_tensor_tensor(decays[:, h, :], ident[:], bonus_sb[:, h:h + 1], decays[:, h, :],
                                               ALU.mult, ALU.add)

            norm1_all = norm_all[:, 0, :, :, :].rearrange("p l k t -> p l (k t)")
            norm2_all = norm_all[:, 1, :, :, :].rearrange("p l k t -> p l (k t)")

            def step(l, c, attend=True, refresh=True):
                nxt = following(l, c)
                if refresh and c == NCH - 1:
                    place_attention(l + 1)
                for m in range(MT):
                    if attend and m == 0:
                        turn_qv(*nxt)
                    if c == 0 and m == 2:
                        place_bn2(l)
                    if attend and m == 4:
                        softmax_norm(*nxt)
                    if attend and m == 5:
                        turn_head(*nxt)
                    if attend and m == 6:
                        residual1(*nxt)
                    split_hidden(l, c, m)
                    if attend and m == 1:
                        softmax_max(*nxt)
                    if refresh and c == NCH - 1 and m >= 3:
                        split_low(l + 1, m - 3)
                if attend:
                    split_x1(*nxt)
                if refresh and c == NCH - 1:
                    place_ffb(l + 1)
                if refresh and c == NCH - 2:
                    place_qkv(l + 1)
                residual2(l, c)
                if refresh and c == NCH - 1:
                    for m in range(MT - 3, MT):
                        split_low(l + 1, m)

            for s in (s_hlo, s_z2):
                dve.sem_inc(s, CREDIT[s])
            dve.wait_ge(s_ids, 16)
            nc.vector.tensor_scalar(id_wrap[:], ids_sb[:], 0, V, ALU.is_lt, ALU.mult).then_inc(s_idx, 1)
            dve.wait_ge(s_idx, 1)
            nc.vector.tensor_tensor(id_wrap[:], id_wrap[:], ids_sb[:], ALU.add).then_inc(s_idx, 1)
            dve.wait_ge(s_idx, 2)
            nc.vector.tensor_scalar(id_row[:], id_wrap[:], 0, V - 1, ALU.max, ALU.min).then_inc(s_idx, 1)
            dve.wait_ge(s_misc, 7 * 16)
            nc.vector.memset(minus_half[:], -0.5).then_inc(s_pre, 1)
            nc.vector.tensor_scalar(norm_tmp[:], raw[:, 3], BN_EPS, None, ALU.add).then_inc(s_pre, 1)
            for c in range(NCH):
                dve.wait_ge(s_gather[c], 16 * CHUNK)
                rows = tok[:, c * CHUNK:(c + 1) * CHUNK, :]
                nc.vector.tensor_scalar(rows, rows, pes_sb[:, 0:1], None, ALU.add).then_inc(s_emb, 1)
            dve.wait_ge(s_pow, 1)
            for w in range(2):
                nc.vector.tensor_tensor(norm_all[:, w, :, 0, :], raw[:, 0, w], norm_tmp[:, w], ALU.mult)
            nc.vector.tensor_tensor(raw[:, 4], raw[:, 4], raw[:, 2], ALU.subtract).then_inc(s_pre, 1)
            dve.wait_ge(s_pre, 3)
            for w in range(2):
                last = nc.vector.tensor_tensor(raw[:, 4, w], raw[:, 4, w], norm_all[:, w, :, 0, :], ALU.mult)
            last.then_inc(s_pre, 1)
            dve.wait_ge(s_pre, 4)
            for w in range(2):
                last = nc.vector.tensor_tensor(norm_all[:, w, :, 1, :], raw[:, 4, w], raw[:, 1, w], ALU.add)
            last.then_inc(s_pre, 1)
            dve.wait_ge(s_pre, 5)
            place_qkv(0)
            place_attention(0)
            place_ffb(0)
            turn_qv(0, 0)
            softmax_max(0, 0)
            softmax_norm(0, 0)
            turn_head(0, 0)
            residual1(0, 0)
            split_x1(0, 0)
            for m in range(MT):
                split_low(0, m)
            with dve.Fori(0, L - 1) as l:
                for c in range(NCH):
                    step(l, c)
            dve.wait_ge(s_rate, 1)
            nc.vector.tensor_scalar(rate[:], rate[:], RATE_MAX, -1.0, ALU.min, ALU.mult).then_inc(s_rate, 1)
            for c in range(NCH):
                step(L - 1, c, attend=c < NCH - 1, refresh=False)
                for i in range(NE // NCH):
                    expert_low(NE // NCH * c + i)
                for i in range(NH // NCH):
                    decay_mask(NH // NCH * c + i)


EVENTS = dict(
    xs=1, h=2, hnT=2, mix_hi=4, r=4, vg=4, eg=4, sq=2, y_hi=2, h2_hi=2, rexp=1,
    hT_t=2, hnT_t=2, r_t=2, k_t=2, vg_t=4, s_t=16, y_t=4, yT_t=2, o_t=2, h2T_t=2, lg_t=1, moe_t=16,
    st1=4, mv1=4, hn=4, xx=2, mix=8, mix_lo=4, k=2, wide=16, gate1=1, gate2=1, silu=1, gsum=2, gmean=2, yc=2, gsq=2, yn=4, yg=2,
    y_lo=2, h2=2, st2=4, mv2=4, hn2=4, h2_lo=2, rt=16, coef=1, acc0=4, moe=32,
    v1=1, rstd1=1, v2=1, rstd2=1, gv=2, grstd=2, g1=1, g2=1,
)


def mixer_and_experts(nc, bank, xT, ident, exp_hi, exp_lo, decays, w_mix, w_router, maa_in, ln_affine, even_odd,
                      expert_no, out):
    fp32, fp32r, u32 = mybir.dt.float32, mybir.dt.float32r, mybir.dt.uint32
    ALU, ACT, AX = mybir.AluOpType, mybir.ActivationFunctionType, mybir.AxisListType
    R, K, VV, G = range(4)
    PAIR = 2
    UNITS = CHUNK * NE // 2

    ctx = ExitStack()
    with ctx:
        def sb(name, shape, dt=fp32):
            return ctx.enter_context(nc.sbuf_tensor(name, shape, dt))

        E = {name: ctx.enter_context(nc.semaphore("e_" + name)) for name in EVENTS}
        s_in, s_split, s_out = [ctx.enter_context(nc.semaphore(n)) for n in ("s_in", "s_split", "s_out")]
        MOE_CREDIT = 4

        def wait(eng, name, c, k):
            n = EVENTS[name] * c + k + (MOE_CREDIT if name == "moe" else 0)
            if not (isinstance(n, int) and n <= 0):
                eng.wait_ge(E[name], n)

        mixw_hi = sb("mixw_hi", [P, KT, 5 * D], fp32r)
        mixw_lo = sb("mixw_lo", [P, KT, 5 * D], fp32r)
        router = sb("router", [P, KT, NE])
        router_hi = sb("router_hi", [P, KT, NE], fp32r)
        router_lo = sb("router_lo", [P, KT, NE], fp32r)
        maa = sb("maa", [P, 4, KT])
        affine = sb("affine", [P, 2, D])
        parity = sb("parity", [P, 2])
        expno = sb("expno", [P, NE])
        minus_half = sb("minus_half2", [P, PAIR * NH])
        ln_eps = sb("ln_eps", [P, CHUNK])
        gn_eps = sb("gn_eps", [P, PAIR * NH])

        held = sb("held", [P, 1])
        xs = sb("xs", [P, KT, CT])
        h = sb("h", [P, CHUNK, D])
        stats = sb("stats", [P, CHUNK, 6])
        mv = sb("mv", [P, CHUNK, 2])
        var = sb("var", [P, CHUNK])
        rstd = sb("rstd", [P, CHUNK])
        hn = sb("hn", [P, CHUNK, D])
        hnT = sb("hnT", [P, KT, CHUNK, T + 1])
        xx = sb("xx", [P, KT, CHUNK, T])
        mix = sb("mix", [P, 2, KT, CT])
        mix_hi = sb("mix_hi", [P, 4, KT, CT], fp32r)
        mix_lo = sb("mix_lo", [P, 4, KT, CT], fp32r)
        r_eo = sb("r_eo", [P, KT, 2, CT])
        kT = sb("kT2", [P, KT, CT])
        vg = sb("vg", [P, CHUNK, 2, D])
        gate = sb("gate", [P, CHUNK, D])
        gain = gate
        offs = sb("offs", [P, CHUNK, D])
        weighed = sb("weighed", [P, 2, NH, T])
        mixw = weighed[:].rearrange("p b h t -> p (b h t)")[:, 0:KT * 5 * D].rearrange("p (k n) -> p k n", k=KT)
        gsum = sb("gsum", [P, 2, PAIR * NH])
        gmean = sb("gmean", [P, 2, PAIR * NH])
        gvar = sb("gvar", [P, 2, PAIR * NH])
        grstd = sb("grstd", [P, 2, PAIR * NH])
        yc = hn
        ysq = xx[:].rearrange("p k n t -> p (k n t)").rearrange("p (n d) -> p n d", n=CHUNK)
        yT_hi = sb("yT_hi", [P, KT, CT], fp32r)
        yT_lo = sb("yT_lo", [P, KT, CT], fp32r)
        h2T_hi = sb("h2T_hi", [P, KT, CT], fp32r)
        h2T_lo = sb("h2T_lo", [P, KT, CT], fp32r)
        acc = sb("acc", [P, CHUNK, D])
        lg = sb("lg", [P, CHUNK, NE])
        lmax = sb("lmax", [P, CHUNK])
        psm = sb("psm", [P, CHUNK, NE])
        psum_ = sb("psum_", [P, CHUNK])
        top = sb("top", [P, CHUNK, NE])
        topi = sb("topi", [P, CHUNK, NE], u32)
        topf = sb("topf", [P, CHUNK, TOPK])
        tsum = sb("tsum", [P, CHUNK])
        wtop = sb("wtop", [P, CHUNK, TOPK])
        wprod = sb("wprod", [P, CHUNK, TOPK])
        ebias = sb("ebias", [P, CHUNK])
        pick = sb("pick", [P, TOPK, CHUNK, NE])
        coef = sb("coef", [P, CHUNK, NE])

        M = [bank[0], bank[1]]
        B = bank[2:8]
        SC = [B[0], B[1], B[4], B[5]]
        VG = [B[2], B[3], B[0], B[1]]

        def seq(t, n):
            return t[..., n * T:(n + 1) * T]

        block = ctx.enter_context(nc.Block())

        @block.sync
        def _(sp):
            for dst, src in ((mixw, w_mix), (maa[:], maa_in), (affine[:], ln_affine), (parity[:], even_odd),
                             (expno[:], expert_no), (router[:], w_router)):
                sp.dma_start(dst, src).then_inc(s_in, 16)

            def store(c):
                for n in range(CHUNK):
                    wait(sp, "moe", c, NE * (n + 1))
                    sp.dma_start(out[bass.ds(c * CHUNK + n, 1), :, :].rearrange("s t d -> (s t) d"),
                                 acc[:, n, :]).then_inc(s_out, 16)

            with sp.Fori(0, NCH - 1) as c:
                store(c)
            store(NCH - 1)
            sp.wait_ge(s_out, 16 * NSEQ)

        @block.gpsimd
        def _(pool):
            def root(c, which):
                wait(pool, f"mv{which}", c, CHUNK)
                nc.gpsimd.tensor_tensor(var[:], mv[:, :, 1], ln_eps[:], ALU.add).then_inc(E[f"v{which}"], 1)
                wait(pool, f"v{which}", c, 1)
                nc.gpsimd.tensor_tensor(rstd[:], var[:], minus_half[:, 0:CHUNK], ALU.pow).then_inc(E[f"rstd{which}"], 1)

            def gates(c):
                wait(pool, "silu", c, 1)
                for k, t, name in ((1, offs, "g2"), (0, gain, "g1")):
                    nc.gpsimd.tensor_tensor(t[:], gate[:], affine[:, k, :].unsqueeze(1).to_broadcast([P, CHUNK, D]),
                                            ALU.mult).then_inc(E[name], 1)

            def group_root(c, p):
                wait(pool, "gsq", c, p + 1)
                nc.gpsimd.tensor_tensor(gvar[:, p, :], gvar[:, p, :], gn_eps[:], ALU.add).then_inc(E["gv"], 1)
                wait(pool, "gv", c, p + 1)
                nc.gpsimd.tensor_tensor(grstd[:, p, :], gvar[:, p, :], minus_half[:], ALU.pow).then_inc(E["grstd"], 1)

            def chunk(c):
                root(c, 1)
                gates(c)
                group_root(c, 0)
                group_root(c, 1)
                root(c, 2)

            pool.memset(ln_eps[:], LN_EPS)
            pool.memset(gn_eps[:], GN_EPS)
            pool.memset(minus_half[:], -0.5).then_inc(s_split, 1)
            pool.wait_ge(s_split, 1)
            chunk(0)
            with pool.Fori(1, NCH) as c:
                chunk(c)

        @block.tensor
        def _(pe):
            def moe(c, units):
                for u in units:
                    n, pair = divmod(u, NE // 2)
                    wait(pe, "moe", c, 2 * (u - 1))
                    for kt in range(KT):
                        last = three(nc, M[u % 2][:], [seq(t[:, kt, :], n) for t in (h2T_hi, h2T_lo)],
                                     [t[:, kt, pair * 2 * D:(pair + 1) * 2 * D] for t in (exp_hi, exp_lo)],
                                     kt == 0, kt == KT - 1)
                    last.then_inc(E["moe_t"], 1)

            def turn_x(c):
                wait(pe, "h2", c, 0)
                wait(pe, "xs", c, 1)
                for n in range(CHUNK):
                    for kt in range(KT):
                        at = (n % PAIR) * D + kt * P
                        last = nc.tensor.transpose(B[n // PAIR][:, at:at + P], seq(xs[:, kt, :], n), ident[:])
                    if n % PAIR == 1:
                        last.then_inc(E["hT_t"], 1)

            def turn_tokens(c, src, banks, ready, done):
                wait(pe, ready, c, EVENTS[ready])
                for kt in range(KT):
                    for n in range(CHUNK):
                        last = nc.tensor.transpose(seq(banks[kt], n), src[:, n, kt * P:(kt + 1) * P], ident[:])
                    last.then_inc(E[done], 1)

            def weights(i, cols):
                return lambda kt: [t[:, kt, i * D + cols.start:i * D + cols.stop] for t in (mixw_hi, mixw_lo)]

            def project_rk(c):
                for i, banks, done in ((R, B[0:2], "r_t"), (K, B[4:6], "k_t")):
                    wait(pe, "mix_lo", c, i + 1)
                    for mt in range(KT):
                        w = weights(i, slice(mt * P, (mt + 1) * P))
                        for kt in range(KT):
                            last = three(nc, banks[mt][:], w(kt), [t[:, i, kt, :] for t in (mix_hi, mix_lo)],
                                         kt == 0, kt == KT - 1)
                        last.then_inc(E[done], 1)

            def project_vg(c):
                for n in range(CHUNK):
                    if n == 2:
                        wait(pe, "r", c, 4)
                    for j, i in enumerate((VV, G)):
                        wait(pe, "mix_lo", c, i + 1)
                        for kt in range(KT):
                            last = three(nc, VG[n][:, j * D:(j + 1) * D], [seq(t[:, i, kt, :], n) for t in (mix_hi, mix_lo)],
                                         weights(i, slice(0, D))(kt), kt == 0, kt == KT - 1)
                    last.then_inc(E["vg_t"], 1)

            def scores(c, n):
                if n == 0:
                    wait(pe, "r", c, 4)
                    wait(pe, "k", c, 2)
                    wait(pe, "vg", c, 4)
                else:
                    wait(pe, "wide", c, QUAD * n)
                for mt in range(KT):
                    for q in range(QUAD):
                        rows = slice(32 * q, 32 * q + 32)
                        last = nc.tensor.matmul(SC[q][:, mt * 2 * T:(mt + 1) * 2 * T], seq(kT[rows, mt, :], n),
                                                seq(r_eo[rows, mt, :, :], n), start=True, stop=True)
                        if mt == KT - 1:
                            last.then_inc(E["s_t"], 1)

            def values(c, n):
                wait(pe, "wide", c, QUAD * (n + 1))
                for head in range(NH):
                    mt, q, e = head // 8, head % 8 // 2, head % 2
                    at = (n % PAIR) * D + head * DH
                    last = nc.tensor.matmul(B[2 + n // PAIR][:, at:at + DH], weighed[:, n % 2, q * 4 + mt * 2 + e, :],
                                            vg[:, n, 0, head * DH:(head + 1) * DH], start=True, stop=True)
                last.then_inc(E["y_t"], 1)

            def project_out(c):
                wait(pe, "y_lo", c, 2)
                for n in range(CHUNK):
                    at = (n % PAIR) * D
                    for kt in range(KT):
                        last = three(nc, B[n // PAIR][:, at:at + D], [seq(t[:, kt, :], n) for t in (yT_hi, yT_lo)],
                                     weights(4, slice(0, D))(kt), kt == 0, kt == KT - 1)
                    if n % PAIR == 1:
                        last.then_inc(E["o_t"], 1)

            def route(c):
                wait(pe, "h2_lo", c, 2)
                for n in range(CHUNK):
                    for kt in range(KT):
                        last = three(nc, B[4][:, n * NE:(n + 1) * NE], [seq(t[:, kt, :], n) for t in (h2T_hi, h2T_lo)],
                                     [t[:, kt, :] for t in (router_hi, router_lo)], kt == 0, kt == KT - 1)
                last.then_inc(E["lg_t"], 1)

            def step(c, experts=True):
                def fill(first, last):
                    if experts:
                        moe(c - 1, range(first, last))
                turn_x(c)
                fill(0, 3)
                turn_tokens(c, hn, B[2:4], "hn", "hnT_t")
                fill(3, 7)
                project_rk(c)
                project_vg(c)
                scores(c, 0)
                for n in range(1, CHUNK):
                    scores(c, n)
                    values(c, n - 1)
                values(c, CHUNK - 1)
                fill(7, 11)
                turn_tokens(c, yc, B[4:6], "yg", "yT_t")
                fill(11, 13)
                project_out(c)
                fill(13, 16)
                turn_tokens(c, hn, B[2:4], "hn2", "h2T_t")
                route(c)

            pe.wait_ge(s_split, 1 + 4)
            step(0, experts=False)
            with pe.Fori(1, NCH) as c:
                step(c)
            moe(NCH - 1, range(UNITS))

        @block.scalar
        def _(act):
            def step(c):
                nc.scalar.copy(xs[:], xT[:, :, bass.ds(c * CT, CT)]).then_inc(E["xs"], 1)
                wait(act, "acc0", c, 0)
                for p in range(2):
                    wait(act, "hT_t", c, p + 1)
                    nc.scalar.copy(h[:, PAIR * p:PAIR * (p + 1), :], B[p][:].rearrange("p (n d) -> p n d", n=PAIR)).then_inc(E["h"], 1)
                for kt in range(KT):
                    wait(act, "hnT_t", c, kt + 1)
                    nc.scalar.copy(hnT[:, kt, :, 1:T + 1], B[2 + kt][:].rearrange("p (n t) -> p n t", n=CHUNK)).then_inc(E["hnT"], 1)
                for i in range(4):
                    wait(act, "mix", c, KT * (i + 1))
                    nc.scalar.copy(mix_hi[:, i], mix[:, i % 2]).then_inc(E["mix_hi"], 1)
                for mt in range(KT):
                    wait(act, "r_t", c, mt + 1)
                    for e in range(2):
                        nc.scalar.mul(r_eo[:, mt, e, :], B[mt][:], parity[:, e:e + 1]).then_inc(E["r"], 1)
                for n in range(CHUNK):
                    wait(act, "vg_t", c, n + 1)
                    nc.scalar.activation(gate[:, n, :], VG[n][:, D:2 * D], ACT.Exp, scale=-1.0).then_inc(E["eg"], 1)
                    nc.scalar.copy(vg[:, n].rearrange("p j d -> p (j d)"), VG[n][:]).then_inc(E["vg"], 1)
                for p in range(2):
                    wait(act, "yc", c, p + 1)
                    nc.scalar.activation(ysq[:, PAIR * p:PAIR * (p + 1), :], yc[:, PAIR * p:PAIR * (p + 1), :], ACT.Square,
                                         scale=DH ** -0.5).then_inc(E["sq"], 1)
                for kt in range(KT):
                    wait(act, "yT_t", c, kt + 1)
                    nc.scalar.copy(yT_hi[:, kt, :], B[4 + kt][:]).then_inc(E["y_hi"], 1)
                for kt in range(KT):
                    wait(act, "h2T_t", c, kt + 1)
                    nc.scalar.copy(h2T_hi[:, kt, :], B[2 + kt][:]).then_inc(E["h2_hi"], 1)
                wait(act, "rt", c, 2)
                nc.scalar.activation(psm[:], lg[:], ACT.Exp).then_inc(E["rexp"], 1)

            act.wait_ge(s_in, 6 * 16)
            nc.scalar.copy(mixw_hi[:], mixw).then_inc(s_split, 1)
            nc.scalar.copy(router_hi[:], router[:]).then_inc(s_split, 1)
            step(0)
            with act.Fori(1, NCH) as c:
                step(c)

        @block.vector
        def _(dve):
            def hold():
                nc.vector.memset(held[:], 0.0)

            def norm(c, src, which):
                for n in range(CHUNK):
                    if which == 1:
                        wait(dve, "h", c, n // PAIR + 1)
                    nc.vector.bn_stats(stats[:, n, :], src[:, n, :]).then_inc(E[f"st{which}"], 1)
                wait(dve, f"st{which}", c, CHUNK)
                hold()
                for n in range(CHUNK):
                    nc.vector.bn_aggr(mv[:, n, :], stats[:, n, :]).then_inc(E[f"mv{which}"], 1)

            def normed(c, src, which, done):
                wait(dve, f"rstd{which}", c, 1)
                for n in range(CHUNK):
                    nc.vector.tensor_scalar(hn[:, n, :], src[:, n, :], mv[:, n, 0:1], rstd[:, n:n + 1],
                                            ALU.subtract, ALU.mult).then_inc(E[done], 1)

            def mixes(c):
                for kt in range(KT):
                    wait(dve, "hnT", c, kt + 1)
                    nc.vector.tensor_tensor(xx[:, kt], hnT[:, kt, :, 0:T], hnT[:, kt, :, 1:T + 1], ALU.subtract).then_inc(E["xx"], 1)
                for i in range(4):
                    if i >= 2:
                        wait(dve, "mix_lo", c, i - 1)
                    for kt in range(KT):
                        wait(dve, "xx", c, kt + 1)
                        nc.vector.scalar_tensor_tensor(mix[:, i % 2, kt].rearrange("p (n t) -> p n t", n=CHUNK), xx[:, kt],
                                                       maa[:, i, kt:kt + 1], hnT[:, kt, :, 1:T + 1],
                                                       ALU.mult, ALU.add).then_inc(E["mix"], 1)
                    if i:
                        mix_low(c, i - 1)
                mix_low(c, 3)

            def mix_low(c, i):
                wait(dve, "mix_hi", c, i + 1)
                nc.vector.tensor_tensor(mix_lo[:, i], mix[:, i % 2], mix_hi[:, i].bitcast(fp32), ALU.subtract).then_inc(E["mix_lo"], 1)

            def keys(c):
                for mt in range(KT):
                    wait(dve, "k_t", c, mt + 1)
                    nc.vector.tensor_copy(kT[:, mt, :], B[4 + mt][:]).then_inc(E["k"], 1)

            def weigh(c, n):
                if n >= 2:
                    wait(dve, "y_t", c, n - 1)
                for q in range(QUAD):
                    wait(dve, "s_t", c, QUAD * n + q + 1)
                    nc.vector.tensor_tensor(weighed[:, n % 2, 4 * q:4 * q + 4, :], SC[q][:].rearrange("p (h t) -> p h t", t=T),
                                            decays[:, 4 * q:4 * q + 4, :], ALU.mult).then_inc(E["wide"], 1)

            def silu(c):
                wait(dve, "vg", c, CHUNK)
                nc.vector.tensor_scalar(gate[:], gate[:], 1.0, None, ALU.add).then_inc(E["gate1"], 1)
                wait(dve, "gate1", c, 1)
                nc.vector.reciprocal(gate[:], gate[:]).then_inc(E["gate2"], 1)
                wait(dve, "gate2", c, 1)
                nc.vector.tensor_tensor(gate[:], gate[:], vg[:, :, 1, :], ALU.mult).then_inc(E["silu"], 1)

            def heads(t):
                return t.rearrange("p n (h d) -> p (n h) d", d=DH)

            def of_pair(t, p):
                return t[:, PAIR * p:PAIR * (p + 1), :]

            def group_centre(c, p):
                y = B[2 + p][:].rearrange("p (h d) -> p h d", d=DH)
                wait(dve, "y_t", c, PAIR * (p + 1))
                nc.vector.reduce_sum(gsum[:, p, :], y, AX.X).then_inc(E["gsum"], 1)
                wait(dve, "gsum", c, p + 1)
                nc.vector.tensor_scalar(gmean[:, p, :], gsum[:, p, :], 1.0 / DH, None, ALU.mult).then_inc(E["gmean"], 1)
                wait(dve, "gmean", c, p + 1)
                nc.vector.tensor_tensor(heads(of_pair(yc, p)), y, gmean[:, p, :].unsqueeze(2).to_broadcast([P, PAIR * NH, DH]),
                                        ALU.subtract).then_inc(E["yc"], 1)

            def group_var(c, p):
                wait(dve, "sq", c, p + 1)
                nc.vector.reduce_sum(gvar[:, p, :], heads(of_pair(ysq, p)), AX.X).then_inc(E["gsq"], 1)

            def group_out(c, p):
                t = of_pair(yc, p)
                wait(dve, "grstd", c, p + 1)
                nc.vector.tensor_tensor(heads(t), heads(t), grstd[:, p, :].unsqueeze(2).to_broadcast([P, PAIR * NH, DH]),
                                        ALU.mult).then_inc(E["yn"], 1)
                wait(dve, "yn", c, 2 * p + 1)
                wait(dve, "g1", c, 1)
                nc.vector.tensor_tensor(t, t, of_pair(gain, p), ALU.mult).then_inc(E["yn"], 1)
                wait(dve, "yn", c, 2 * p + 2)
                wait(dve, "g2", c, 1)
                nc.vector.tensor_tensor(t, t, of_pair(offs, p), ALU.add).then_inc(E["yg"], 1)

            def low(c, name, banks, hi, lo):
                for kt in range(KT):
                    wait(dve, name + "_hi", c, kt + 1)
                    nc.vector.tensor_tensor(lo[:, kt, :], banks[kt][:], hi[:, kt, :].bitcast(fp32), ALU.subtract).then_inc(E[name + "_lo"], 1)

            def residual(c):
                for p in range(2):
                    wait(dve, "o_t", c, p + 1)
                    nc.vector.tensor_tensor(of_pair(h, p), B[p][:].rearrange("p (n d) -> p n d", n=PAIR), of_pair(h, p),
                                            ALU.add).then_inc(E["h2"], 1)
                wait(dve, "h2", c, 2)

            def route(c):
                k = [0]

                def did(ins):
                    k[0] += 1
                    ins.then_inc(E["rt"], 1)
                    wait(dve, "rt", c, k[0])
                wait(dve, "lg_t", c, 1)
                logits = B[4][:, 0:CHUNK * NE].rearrange("p (n e) -> p n e", n=CHUNK)

                def wide(t):
                    return t.to_broadcast([P, CHUNK, NE])
                did(nc.vector.reduce_max(lmax[:], logits, AX.X))
                did(nc.vector.tensor_tensor(lg[:], logits, wide(lmax[:].unsqueeze(2)), ALU.subtract))
                wait(dve, "rexp", c, 1)
                did(nc.vector.reduce_sum(psum_[:], psm[:], AX.X))
                did(nc.vector.reciprocal(psum_[:], psum_[:]))
                did(nc.vector.tensor_tensor(psm[:], psm[:], wide(psum_[:].unsqueeze(2)), ALU.mult))
                hold()
                for n in range(CHUNK):
                    last = nc.vector.max(top[:, n, :], psm[:, n, :])
                did(last)
                hold()
                for n in range(CHUNK):
                    last = nc.vector.max_index(topi[:, n, :], top[:, n, :], psm[:, n, :])
                did(last)
                nc.vector.tensor_tensor(tsum[:], top[:, :, 0], top[:, :, 1], ALU.add)
                did(nc.vector.tensor_copy(topf[:], topi[:, :, 0:TOPK]))
                did(nc.vector.tensor_scalar(tsum[:], tsum[:], TOP_EPS, None, ALU.add))
                did(nc.vector.reciprocal(tsum[:], tsum[:]))
                did(nc.vector.tensor_tensor(wtop[:], top[:, :, 0:TOPK], tsum[:].unsqueeze(2).to_broadcast([P, CHUNK, TOPK]), ALU.mult))
                for j in range(TOPK):
                    nc.vector.tensor_tensor(pick[:, j], wide(topf[:, :, j:j + 1]), expno[:].unsqueeze(1).to_broadcast([P, CHUNK, NE]),
                                            ALU.is_equal)
                did(nc.vector.tensor_tensor(wprod[:], wtop[:], top[:, :, 0:TOPK], ALU.mult))
                for j in range(TOPK):
                    nc.vector.tensor_tensor(pick[:, j], pick[:, j], wide(wtop[:, :, j:j + 1]), ALU.mult)
                did(nc.vector.tensor_tensor(ebias[:], wprod[:, :, 0], wprod[:, :, 1], ALU.add))
                did(nc.vector.tensor_tensor(coef[:], pick[:, 0], pick[:, 1], ALU.add))
                for n in range(CHUNK):
                    if n == 0 and not (isinstance(c, int) and c == 0):
                        dve.wait_ge(s_out, 16 * CHUNK * c)
                    last = nc.vector.tensor_scalar(acc[:, n, :], h[:, n, :], ebias[:, n:n + 1], None, ALU.add)
                    last.then_inc(E["acc0"], 1)
                k[0] += 2
                nc.vector.tensor_copy(lmax[:], tsum[:]).then_inc(E["rt"], 2)
                assert k[0] == EVENTS["rt"], k

            def add_experts(c, units):
                for u in units:
                    n, pair = divmod(u, NE // 2)
                    wait(dve, "moe_t", c, u + 1)
                    for j in range(2):
                        if pair + j == 0:
                            wait(dve, "acc0", c, n + 1)
                        else:
                            wait(dve, "moe", c, 2 * u + j)
                        nc.vector.scalar_tensor_tensor(acc[:, n, :], M[u % 2][:, j * D:(j + 1) * D],
                                                       coef[:, n, 2 * pair + j:2 * pair + j + 1], acc[:, n, :],
                                                       ALU.mult, ALU.add).then_inc(E["moe"], 1)

            def step(c, experts=True):
                def fill(first, last):
                    if experts:
                        add_experts(c - 1, range(first, last))
                norm(c, h, 1)
                fill(0, 1)
                normed(c, h, 1, "hn")
                fill(1, 3)
                mixes(c)
                fill(3, 7)
                keys(c)
                weigh(c, 0)
                weigh(c, 1)
                silu(c)
                weigh(c, 2)
                weigh(c, 3)
                group_centre(c, 0)
                group_centre(c, 1)
                group_var(c, 0)
                group_var(c, 1)
                fill(7, 9)
                group_out(c, 0)
                group_out(c, 1)
                fill(9, 11)
                low(c, "y", B[4:6], yT_hi, yT_lo)
                fill(11, 13)
                residual(c)
                norm(c, h, 2)
                fill(13, 14)
                normed(c, h, 2, "hn2")
                fill(14, 16)
                low(c, "h2", B[2:4], h2T_hi, h2T_lo)
                route(c)

            dve.sem_inc(E["moe"], MOE_CREDIT)
            nc.vector.memset(hnT[:, :, :, 0:1], 0.0)
            dve.wait_ge(s_split, 1 + 2)
            nc.vector.tensor_tensor(mixw_lo[:], mixw, mixw_hi[:].bitcast(fp32), ALU.subtract).then_inc(s_split, 1)
            nc.vector.tensor_tensor(router_lo[:], router[:], router_hi[:].bitcast(fp32), ALU.subtract).then_inc(s_split, 1)
            step(0, experts=False)
            with dve.Fori(1, NCH) as c:
                step(c)
            add_experts(NCH - 1, range(UNITS))


def kernel(x, L0_tok_emb, L0_tok_pes, L0_tok_wq, L0_tok_bq, L0_tok_wk, L0_tok_bk, L0_tok_wv, L0_tok_bv, L0_tok_wo, L0_tok_bo, L0_tok_att_gamma, L0_tok_att_beta, L0_tok_att_mean, L0_tok_att_var, L0_tok_w1, L0_tok_bff1, L0_tok_w2, L0_tok_bff2, L0_tok_ffn_gamma, L0_tok_ffn_beta, L0_tok_ffn_mean, L0_tok_ffn_var,
           L0_attn_w_r, L0_attn_w_k, L0_attn_w_v, L0_attn_w_g, L0_attn_w_o, L0_attn_time_maa_k, L0_attn_time_maa_v,
           L0_attn_time_maa_r, L0_attn_time_maa_g, L0_attn_time_decay, L0_attn_time_faaaa, L0_attn_ln_g, L0_attn_ln_b,
           L0_ffn_router_w, L0_ffn_expert_weights):
    import numpy as np
    import concourse.bacc as bacc
    from concourse.bass_utils import run_bass_kernel_spmd
    A = np.asarray
    w1 = A(L0_tok_w1).reshape(L, KT, P, MT, P).transpose(0, 2, 3, 1, 4).reshape(L, P, MT, KT * P)
    w2 = A(L0_tok_w2).reshape(L, MT, P, D).transpose(0, 2, 1, 3)
    w_ffn = np.concatenate([w1, w2], axis=3)
    w_qkv = np.zeros((P, L, KT, QKVROWS), np.float32)
    qkv_bias = np.zeros((QKVROWS, L), np.float32)
    for row, w, b in ((QROW, L0_tok_wq, L0_tok_bq), (KROW, L0_tok_wk, L0_tok_bk), (VROW, L0_tok_wv, L0_tok_bv)):
        w_qkv[:, :, :, row:row + DK] = A(w).reshape(L, KT, P, DK).transpose(2, 0, 1, 3)
        qkv_bias[row:row + DK] = A(b).T
    w_o = A(L0_tok_wo).transpose(1, 0, 2)
    kinds = [(L0_tok_att_gamma, L0_tok_ffn_gamma), (L0_tok_att_beta, L0_tok_ffn_beta), (L0_tok_att_mean, L0_tok_ffn_mean),
             (L0_tok_att_var, L0_tok_ffn_var), (L0_tok_bo, L0_tok_bff2)]
    bn_raw = np.stack([np.stack([A(v).reshape(L, KT, P).transpose(2, 0, 1) for v in two], 1) for two in kinds], 1)
    ins = dict(ids=A(x).T, emb=A(L0_tok_emb), pes=A(L0_tok_pes)[:T, 0:1], w_ffn=w_ffn,
               w_qkv=w_qkv.reshape(P, L, KT * QKVROWS), w_o=w_o, bn_raw=bn_raw, qkv_bias=qkv_bias,
               ff_bias=A(L0_tok_bff1).reshape(L, MT, P).transpose(2, 0, 1), ident_in=np.eye(P, dtype=np.float32))
    def feature_rows(w):
        return A(w).T.reshape(KT, P, -1).transpose(1, 0, 2)

    def to_all(v):
        return np.broadcast_to(A(v), (P,) + A(v).shape)

    order = [mt * 8 + q * 2 + e for q in range(QUAD) for mt in range(KT) for e in range(2)]
    key, query = np.arange(T)[:, None], np.arange(T)[None, :]
    ins.update(
        w_exp=A(L0_ffn_expert_weights).reshape(NE, KT, P, D).transpose(2, 1, 0, 3).reshape(P, KT, NE * D),
        w_mix=np.concatenate([feature_rows(w) for w in (L0_attn_w_r, L0_attn_w_k, L0_attn_w_v, L0_attn_w_g, L0_attn_w_o)], 2),
        w_router=feature_rows(L0_ffn_router_w),
        maa_in=np.stack([A(m).reshape(KT, P).T for m in (L0_attn_time_maa_r, L0_attn_time_maa_k, L0_attn_time_maa_v,
                                                         L0_attn_time_maa_g)], 1),
        decay=to_all(A(L0_attn_time_decay)[order]), bonus=to_all(A(L0_attn_time_faaaa)[order]),
        ln_affine=to_all(np.stack([A(L0_attn_ln_g), A(L0_attn_ln_b)])),
        gap=np.maximum(query - key - 1, 0).astype(np.float32), later=(query > key).astype(np.float32),
        even_odd=np.stack([np.arange(P) // DH % 2 == e for e in range(2)], 1).astype(np.float32),
        expert_no=to_all(np.arange(NE, dtype=np.float32)))
    nc = bacc.Bacc("TRN2", target_bir_lowering=False, num_devices=1)
    arrays = {k: np.ascontiguousarray(v) for k, v in ins.items()}
    args = {k: nc.dram_tensor(k, v.shape, mybir.dt.from_np(v.dtype), kind="ExternalInput").ap() for k, v in arrays.items()}
    args["out"] = nc.dram_tensor("out", [NSEQ, T, D], mybir.dt.float32, kind="ExternalOutput").ap()
    tower(nc, **args)
    return run_bass_kernel_spmd(nc, [arrays], core_ids=[0]).results[0]["out"]
```

```python
import concourse.bass as bass
from concourse import mybir
from contextlib import ExitStack

L, D, DK, FF = 4, 256, 16, 1024
NSEQ, T = 16, 128
V = 8000
P = 128
KT = D // P
MT = FF // P
CHUNK = 4
CT = CHUNK * T
NCH = NSEQ // CHUNK
BN_EPS = 1e-3
QROW, KROW, VROW = 0, 32, 64
QKVROWS = 96
STACK = 96
RING = 4
NH = 16
DH = D // NH
LN_EPS = 1e-5
GN_EPS = 1e-5 * 64
RATE_MAX = 200.0
NE, TOPK = 8, 2
TOP_EPS = 1e-6
QUAD = 4
WCOLS = KT * P + D


def tower(nc, ids, emb, pes, w_ffn, w_qkv, w_o, bn_raw, qkv_bias, ff_bias, ident_in, w_exp, w_mix, w_router,
          maa_in, decay, bonus, ln_affine, gap, later, even_odd, expert_no, out):
    fp32, fp32r = mybir.dt.float32, mybir.dt.float32r
    keep = ExitStack()
    with keep:
        def lasting(name, shape, dt=fp32):
            return keep.enter_context(nc.sbuf_tensor(name, shape, dt))

        h = lasting("h", [P, NSEQ, D])
        ident = lasting("ident", [P, P])
        mixw = [lasting(f"mixw_{part}", [P, KT, 5 * D], fp32r) for part in ("hi", "lo")]
        decays = lasting("decays", [P, NH, T])
        bank = [keep.enter_context(nc.psum_tensor(f"bank{i}", [P, 512], fp32)) for i in range(8)]
        transformer(nc, bank, h, ident, mixw, decays, ids, emb, pes, w_ffn, w_qkv, w_o, bn_raw, qkv_bias,
                    ff_bias, ident_in, w_mix, decay, bonus, gap, later)
        mixer_and_experts(nc, bank, h, ident, mixw, decays, w_exp, w_router, maa_in, ln_affine, even_odd, expert_no, out)


def three(nc, out_, w, x, first, last):
    (wh, wl), (xh, xl) = w, x
    nc.tensor.matmul(out_, wh, xh, start=first, stop=False)
    nc.tensor.matmul(out_, wh, xl, start=False, stop=False)
    return nc.tensor.matmul(out_, wl, xh, start=False, stop=last)


def transformer(nc, bank, h, ident, mixw, decays, ids, emb, pes, w_ffn, w_qkv, w_o, bn_raw, qkv_bias,
                ff_bias, ident_in, w_mix, decay, bonus, gap, later):
    fp32, fp32r, i32 = mybir.dt.float32, mybir.dt.float32r, mybir.dt.int32
    ALU, ACT, AX = mybir.AluOpType, mybir.ActivationFunctionType, mybir.AxisListType

    ctx = ExitStack()
    with ctx:
        def sb(name, shape, dt=fp32):
            return ctx.enter_context(nc.sbuf_tensor(name, shape, dt))

        def sem(name):
            return ctx.enter_context(nc.semaphore(name))

        ids_sb = sb("ids_sb", [P, NSEQ], i32)
        id_wrap = sb("id_wrap", [P, NSEQ], i32)
        id_row = sb("id_row", [P, NSEQ], i32)
        tok = h
        mixw_raw = h[:, NSEQ - 10:, :].rearrange("p n d -> p (n d)").rearrange("p (k n) -> p k n", k=KT)
        pes_sb = sb("pes_sb", [P, 1])

        xT = sb("xT", [P, KT, NSEQ * T])
        w_raw = sb("w_raw", [P, MT, WCOLS])
        w_hi = sb("w_hi", [P, MT, WCOLS], fp32r)
        w_lo = sb("w_lo", [P, MT, WCOLS], fp32r)
        qkv_all = sb("qkv_all", [P, L, KT * QKVROWS])
        qkv_w = sb("qkv_w", [P, KT * QKVROWS])
        wo_all = sb("wo_all", [STACK, L, D])
        wo_w = sb("wo_w", [STACK, D], fp32r)
        raw = sb("raw", [P, 5, 2, L, KT])
        norm_all = sb("norm_all", [P, 2, L, 2, KT])
        norm_tmp = sb("norm_tmp", [P, 2, L, KT])
        minus_half = sb("minus_half", [P, 2 * L * KT])
        qkvb_all = sb("qkvb_all", [QKVROWS, L])
        ffb_all = sb("ffb_all", [P, L, MT])
        qkvb = sb("qkvb", [QKVROWS, 1])
        ffb = sb("ffb", [P, MT])
        bn1 = sb("bn1", [P, 2, KT])
        bn2 = sb("bn2", [P, 2, KT])

        qT = sb("qT", [DK, CT])
        kT = sb("kT", [DK, CT])
        vT = sb("vT", [DK, CT])
        vtok = sb("vtok", [P, CHUNK, STACK])
        smax = sb("smax", [P, CHUNK])
        nbias = sb("nbias", [P, CHUNK])
        ssum = sb("ssum", [P, CHUNK])
        rsum = sb("rsum", [P, CHUNK])
        prob = sb("prob", [P, CHUNK, T])
        probT = sb("probT", [P, CHUNK, T])
        headT = sb("headT", [STACK, CT], fp32r)
        z1 = sb("z1", [P, KT, CT])
        z2 = sb("z2", [P, KT, CT])
        x1 = sb("x1", [P, 2, KT, CT])
        x1_hi = sb("x1_hi", [P, 2, KT, CT], fp32r)
        x1_lo = sb("x1_lo", [P, 2, KT, CT], fp32r)
        hid = sb("hid", [P, 2, CT])
        hid_hi = sb("hid_hi", [P, RING, CT], fp32r)
        hid_lo = sb("hid_lo", [P, RING, CT], fp32r)

        H = [bank[0], bank[1]]
        Y = [bank[2], bank[3]]
        A = bank[4]
        S = bank[5]
        O = [bank[6], bank[7]]

        s_ids, s_misc, s_wl = sem("s_ids"), sem("s_misc"), sem("s_wl")
        s_gather = [sem(f"s_gather{c}") for c in range(NCH)]
        s_idx, s_pre, s_emb = sem("s_idx"), sem("s_pre"), sem("s_emb")
        s_w_lo, s_attw, s_attv, s_ffb, s_bn2 = sem("s_w_lo"), sem("s_attw"), sem("s_attv"), sem("s_ffb"), sem("s_bn2")
        s_wov = sem("s_wov")
        s_q, s_v, s_vtok, s_max, s_nb, s_rs, s_prob = (sem("s_q"), sem("s_v"), sem("s_vtok"), sem("s_max"),
                                                       sem("s_nb"), sem("s_rs"), sem("s_prob"))
        s_head, s_z1, s_x1lo, s_hlo, s_z2 = sem("s_head"), sem("s_z1"), sem("s_x1lo"), sem("s_hlo"), sem("s_z2")
        s_w_hi, s_k, s_exp, s_pT, s_x1, s_x1hi = (sem("s_w_hi"), sem("s_k"), sem("s_exp"), sem("s_pT"),
                                                  sem("s_x1"), sem("s_x1hi"))
        s_relu, s_hhi, s_x = sem("s_relu"), sem("s_hhi"), sem("s_x")
        s_eT, s_qkv, s_vt, s_sc, s_pt, s_pv, s_wo = (sem("s_eT"), sem("s_qkv"), sem("s_vt"), sem("s_sc"),
                                                     sem("s_pt"), sem("s_pv"), sem("s_wo"))
        s_h, s_y = sem("s_h"), sem("s_y")
        s_dec, s_rate, s_decay, s_masked = sem("s_dec"), sem("s_rate"), sem("s_decay"), sem("s_masked")
        s_mixw, s_mixw_hi, s_mixw_lo, s_hturn, s_hout = (sem("s_mixw"), sem("s_mixw_hi"), sem("s_mixw_lo"), sem("s_hturn"),
                                                         sem("s_hout"))
        s_head_hi, s_wo_hi, s_zero = sem("s_head_hi"), sem("s_wo_hi"), sem("s_zero")
        s_pow = sem("s_pow")
        rate = sb("rate", [P, NH])
        bonus_sb = sb("bonus_sb", [P, NH])
        gap_sb = sb("gap_sb", [P, T])
        later_sb = sb("later_sb", [P, T])
        CREDIT = {s_relu: 2, s_hlo: 2, s_y: RING, s_z2: KT}

        def after(s, n):
            return n + CREDIT.get(s, 0)

        def wait_after(eng, s, n):
            if not (isinstance(n, int) and after(s, n) <= 0):
                eng.wait_ge(s, after(s, n))

        def following(l, c):
            return (l, c + 1) if c < NCH - 1 else (l + 1, 0)

        block = ctx.enter_context(nc.Block())

        @block.sync
        def _(sp):
            sp.dma_start(ids_sb[:], ids).then_inc(s_ids, 16)
            sp.dma_start(pes_sb[:], pes).then_inc(s_misc, 16)
            sp.dma_start(ident[:], ident_in).then_inc(s_misc, 16)
            sp.dma_start(raw[:], bn_raw).then_inc(s_misc, 16)
            sp.dma_start(qkv_all[:], w_qkv).then_inc(s_misc, 16)
            sp.dma_start(wo_all[:], w_o).then_inc(s_misc, 16)
            sp.dma_start(qkvb_all[:], qkv_bias).then_inc(s_misc, 16)
            sp.dma_start(ffb_all[:], ff_bias).then_inc(s_misc, 16)
            sp.dma_start(w_raw[:], w_ffn[0]).then_inc(s_wl, 16)
            for dst, src in ((rate, decay), (bonus_sb, bonus), (gap_sb, gap), (later_sb, later)):
                sp.dma_start(dst[:], src).then_inc(s_dec, 16)
            sp.wait_ge(s_eT, NCH)
            sp.dma_start(mixw_raw, w_mix).then_inc(s_mixw, 16)
            with sp.Fori(0, L - 1) as l:
                sp.wait_ge(s_w_lo, MT * l + MT)
                sp.dma_start(w_raw[:], w_ffn[bass.ds(l + 1, 1), :, :, :]).then_inc(s_wl, 16)

        @block.gpsimd
        def _(pool):
            pool.wait_ge(s_idx, 3)
            for n in range(NSEQ):
                pool.indirect_dma_start(tok[:, n, :], None, emb,
                                        bass.IndirectOffsetOnAxis(ap=id_row[:, n:n + 1], axis=0)).then_inc(s_gather[n // CHUNK], 16)
            pool.wait_ge(s_pre, 2)
            flat = norm_tmp[:].rearrange("p a l k -> p (a l k)")
            nc.gpsimd.tensor_tensor(flat, flat, minus_half[:], ALU.pow).then_inc(s_pow, 1)

        @block.tensor
        def _(pe):
            def qkv(l, c):
                a = NCH * l + c
                pe.wait_ge(s_attw, l + 1)
                pe.wait_ge(s_x, KT * (a + 1))
                wait_after(pe, s_pT, a)
                for kt in range(KT):
                    last = nc.tensor.matmul(A[0:QKVROWS, :], qkv_w[:, kt * QKVROWS:(kt + 1) * QKVROWS],
                                            xT[:, kt, c * CT:(c + 1) * CT], start=kt == 0, stop=kt == KT - 1)
                last.then_inc(s_qkv, 1)

            def scores(l, c):
                a = NCH * l + c
                pe.wait_ge(s_v, a + 1)
                pe.wait_ge(s_k, a + 1)
                wait_after(pe, s_head, a)
                pe.wait_ge(s_q, a + 1)
                for n in range(CHUNK):
                    last = nc.tensor.matmul(S[:, n * T:(n + 1) * T], qT[:, n * T:(n + 1) * T],
                                            kT[:, n * T:(n + 1) * T], start=True, stop=True)
                last.then_inc(s_sc, 1)
                for n in range(CHUNK):
                    last = nc.tensor.transpose(A[:, n * DK:(n + 1) * DK], vT[:, n * T:(n + 1) * T],
                                               ident[0:DK, 0:DK])
                last.then_inc(s_vt, 1)

            def turn_probs(l, c):
                pe.wait_ge(s_vtok, NCH * l + c + 1)
                pe.wait_ge(s_prob, NCH * l + c + 1)
                for n in range(CHUNK):
                    last = nc.tensor.transpose(A[:, n * T:(n + 1) * T], prob[:, n, :], ident[:])
                last.then_inc(s_pt, 1)

            def head(l, c):
                a = NCH * l + c
                pe.wait_ge(s_pT, a + 1)
                for n in range(CHUNK):
                    last = nc.tensor.matmul(S[0:STACK, n * T:(n + 1) * T], vtok[:, n, :], probT[:, n, :],
                                            start=True, stop=True)
                last.then_inc(s_pv, 1)

            def project(l, c):
                pe.wait_ge(s_attv, l + 1)
                pe.wait_ge(s_head, NCH * l + c + 1)
                wait_after(pe, s_z1, KT * (NCH * l + c))
                if isinstance(l, int) and l == L - 1 and c >= 3:
                    pe.wait_ge(s_hout, KT * (c - 2))
                for kt in range(KT):
                    last = nc.tensor.matmul(O[kt][:], wo_w[:, kt * P:(kt + 1) * P], headT[:], start=True, stop=True)
                last.then_inc(s_wo, 1)

            def hidden(l, c, m):
                s = NCH * l + c
                if c == 0:
                    pe.wait_ge(s_w_lo, MT * l + m + 1)
                pe.wait_ge(s_relu, after(s_relu, MT * s + m - 1))
                for kt in range(KT):
                    if m == 0:
                        pe.wait_ge(s_x1lo, KT * s + kt + 1)
                    w = [t[:, m, kt * P:(kt + 1) * P] for t in (w_hi, w_lo)]
                    last = three(nc, H[m % 2][:], w, [t[:, c % 2, kt, :] for t in (x1_hi, x1_lo)], kt == 0, kt == KT - 1)
                last.then_inc(s_h, 1)

            def second(l, c, m):
                s = NCH * l + c
                pe.wait_ge(s_hlo, after(s_hlo, MT * s + m + 1))
                if m == 0:
                    pe.wait_ge(s_z2, after(s_z2, KT * s))
                for kt in range(KT):
                    w = [t[:, m, KT * P + kt * P:KT * P + (kt + 1) * P] for t in (w_hi, w_lo)]
                    last = three(nc, Y[kt][:], w, [t[:, m % RING, :] for t in (hid_hi, hid_lo)], m == 0, m == MT - 1)
                last.then_inc(s_y, 1)

            def turn_out(c):
                pe.wait_ge(s_x, KT * (NCH * L + c + 1))
                pe.wait_ge(s_z1, KT * min(NCH * (L - 1) + c + 3, NCH * L))
                if c >= 1:
                    pe.wait_ge(s_hout, KT * c)
                for n in range(CHUNK):
                    for kt in range(KT):
                        at = n % 2 * D + kt * P
                        last = nc.tensor.transpose(O[n // 2][:, at:at + P], xT[:, kt, c * CT + n * T:c * CT + (n + 1) * T], ident[:])
                    if n % 2:
                        last.then_inc(s_hturn, 1)

            def step(l, c, attend=True):
                nxt = following(l, c)
                for m in range(MT):
                    if attend and m == 0:
                        qkv(*nxt)
                    if attend and m == 5:
                        turn_probs(*nxt)
                    if attend and m == 6:
                        head(*nxt)
                    if attend and m == 7:
                        project(*nxt)
                    hidden(l, c, m)
                    if attend and m == 1:
                        scores(*nxt)
                    if m >= 2:
                        second(l, c, m - 2)
                second(l, c, MT - 2)
                second(l, c, MT - 1)

            pe.sem_inc(s_y, CREDIT[s_y])
            pe.wait_ge(s_misc, 7 * 16)
            for c in range(NCH):
                pe.wait_ge(s_emb, c + 1)
                if c >= 2:
                    pe.wait_ge(s_x, KT * (c - 1))
                for n in range(CHUNK):
                    for kt in range(KT):
                        last = nc.tensor.transpose((O, Y)[c % 2][kt][:, n * T:(n + 1) * T],
                                                   tok[:, c * CHUNK + n, kt * P:(kt + 1) * P], ident[:])
                last.then_inc(s_eT, 1)
            pe.wait_ge(s_x, KT * NCH)
            for part in (qkv, scores, turn_probs, head, project):
                part(0, 0)
            with pe.Fori(0, L - 1) as l:
                for c in range(NCH):
                    step(l, c)
            for c in range(NCH):
                step(L - 1, c, attend=c < NCH - 1)
                if c >= 1:
                    turn_out(c - 1)
            turn_out(NCH - 1)

        @block.scalar
        def _(act):
            def turn_k(l, c):
                act.wait_ge(s_qkv, NCH * l + c + 1)
                act.wait_ge(s_attv, l + 1)
                nc.scalar.activation(kT[:], A[KROW:KROW + DK, :], ACT.Identity,
                                     bias=qkvb[KROW:KROW + DK, :]).then_inc(s_k, 1)

            def exps(l, c):
                act.wait_ge(s_nb, NCH * l + c + 1)
                for n in range(CHUNK):
                    last = nc.scalar.activation(prob[:, n, :], S[:, n * T:(n + 1) * T], ACT.Exp, bias=nbias[:, n:n + 1],
                                                scale=DK ** -0.5, accum_out=ssum[:, n:n + 1])
                last.then_inc(s_exp, 1)

            def copy_probT(l, c):
                act.wait_ge(s_pt, NCH * l + c + 1)
                nc.scalar.copy(probT[:].rearrange("p n t -> p (n t)"), A[:]).then_inc(s_pT, 1)

            def norm1(l, c):
                a = NCH * l + c
                for kt in range(KT):
                    act.wait_ge(s_z1, KT * a + kt + 1)
                    nc.scalar.activation(x1[:, c % 2, kt, :], z1[:, kt, :], ACT.Identity, bias=bn1[:, 1, kt:kt + 1],
                                         scale=bn1[:, 0, kt:kt + 1]).then_inc(s_x1, 1)
                    act.wait_ge(s_x1, KT * a + kt + 1)
                    nc.scalar.copy(x1_hi[:, c % 2, kt, :], x1[:, c % 2, kt, :]).then_inc(s_x1hi, 1)

            def relu(l, c, m):
                n = MT * (NCH * l + c) + m
                if c == 0 and m == 0:
                    act.wait_ge(s_ffb, l + 1)
                act.wait_ge(s_h, n + 1)
                act.wait_ge(s_hlo, after(s_hlo, n - 1))
                nc.scalar.activation(hid[:, m % 2, :], H[m % 2][:], ACT.Relu, bias=ffb[:, m:m + 1]).then_inc(s_relu, 1)
                act.wait_ge(s_relu, after(s_relu, n + 1))
                act.wait_ge(s_y, after(s_y, n + 1 - RING))
                nc.scalar.copy(hid_hi[:, m % RING, :], hid[:, m % 2, :]).then_inc(s_hhi, 1)

            def norm2(l, c):
                for kt in range(KT):
                    if c == 0:
                        act.wait_ge(s_bn2, l + 1)
                    act.wait_ge(s_z2, after(s_z2, KT * (NCH * l + c) + kt + 1))
                    nc.scalar.activation(xT[:, kt, c * CT:(c + 1) * CT], z2[:, kt, :], ACT.Identity,
                                         bias=bn2[:, 1, kt:kt + 1], scale=bn2[:, 0, kt:kt + 1]).then_inc(s_x, 1)

            def split_high(l, m):
                act.wait_ge(s_wl, 16 * l + 16)
                if not isinstance(l, int):
                    act.wait_ge(s_y, after(s_y, MT * (NCH * l - 1) + m + 1))
                nc.scalar.copy(w_hi[:, m, :], w_raw[:, m, :]).then_inc(s_w_hi, 1)

            def step(l, c, attend=True, refresh=True, extra=None):
                nxt = following(l, c)
                refresh = refresh and c == NCH - 1
                for m in range(MT):
                    if attend and m == 0:
                        turn_k(*nxt)
                    if attend and m == 5:
                        copy_probT(*nxt)
                    relu(l, c, m)
                    if attend and m == 2:
                        exps(*nxt)
                    if attend and m == 7:
                        norm1(*nxt)
                    if extra:
                        extra(c, m)
                    if refresh and m >= 3:
                        split_high(l + 1, m - 3)
                norm2(l, c)
                if refresh:
                    for m in range(MT - 3, MT):
                        split_high(l + 1, m)

            def mixw_high(i):
                if i == 0:
                    act.wait_ge(s_mixw, 16)
                cols = slice(i * D, (i + 1) * D)
                nc.scalar.copy(mixw[0][:, :, cols], mixw_raw[:, :, cols]).then_inc(s_mixw_hi, 1)

            def decay_rate():
                act.wait_ge(s_dec, 4 * 16)
                nc.scalar.activation(rate[:], rate[:], ACT.Exp).then_inc(s_rate, 1)

            def decay_row(h):
                if h == 0:
                    act.wait_ge(s_rate, 2)
                nc.scalar.activation(decays[:, h, :], gap_sb[:], ACT.Exp, scale=rate[:, h:h + 1]).then_inc(s_decay, 1)

            act.sem_inc(s_relu, CREDIT[s_relu])
            for c in range(NCH):
                act.wait_ge(s_eT, c + 1)
                for kt in range(KT):
                    nc.scalar.copy(xT[:, kt, c * CT:(c + 1) * CT], (O, Y)[c % 2][kt][:]).then_inc(s_x, 1)
            turn_k(0, 0)
            exps(0, 0)
            copy_probT(0, 0)
            norm1(0, 0)
            for m in range(MT):
                split_high(0, m)
            with act.Fori(0, L - 1) as l:
                for c in range(NCH):
                    step(l, c)
            decay_rate()

            def extra(c, m):
                if m % 2:
                    decay_row(c * (MT // 2) + m // 2)
                elif 3 * c + m // 2 < 5 and m < 6:
                    mixw_high(3 * c + m // 2)
            for c in range(NCH):
                step(L - 1, c, attend=c < NCH - 1, refresh=False, extra=extra)

        @block.vector
        def _(dve):
            def turn_qv(l, c):
                a = NCH * l + c
                dve.wait_ge(s_qkv, a + 1)
                dve.wait_ge(s_attv, l + 1)
                nc.vector.tensor_scalar(qT[:], A[QROW:QROW + DK, :], qkvb[QROW:QROW + DK, :], None, ALU.add).then_inc(s_q, 1)
                nc.vector.tensor_scalar(vT[:], A[VROW:VROW + DK, :], qkvb[VROW:VROW + DK, :], None, ALU.add).then_inc(s_v, 1)

            def softmax_max(l, c):
                a = NCH * l + c
                dve.wait_ge(s_sc, a + 1)
                nc.vector.reduce_max(smax[:], S[:].rearrange("p (n t) -> p n t", n=CHUNK), AX.X).then_inc(s_max, 1)
                dve.wait_ge(s_max, a + 1)
                nc.vector.tensor_scalar(nbias[:], smax[:], -DK ** -0.5, None, ALU.mult).then_inc(s_nb, 1)
                dve.wait_ge(s_vt, a + 1)
                nc.vector.tensor_copy(vtok[:].rearrange("p n (j d) -> p n j d", j=3)[:, :, :, 0:DK],
                                      A[:, 0:CHUNK * DK].rearrange("p (n d) -> p n d", n=CHUNK).unsqueeze(2)
                                      .to_broadcast([P, CHUNK, 3, DK])).then_inc(s_vtok, 1)

            def softmax_norm(l, c):
                a = NCH * l + c
                dve.wait_ge(s_exp, a + 1)
                nc.vector.reciprocal(rsum[:], ssum[:]).then_inc(s_rs, 1)
                dve.wait_ge(s_rs, a + 1)
                nc.vector.tensor_tensor(prob[:], prob[:], rsum[:].unsqueeze(2).to_broadcast([P, CHUNK, T]),
                                        ALU.mult).then_inc(s_prob, 1)

            def turn_head(l, c):
                dve.wait_ge(s_pv, NCH * l + c + 1)
                nc.vector.tensor_copy(headT[:], S[0:STACK, :]).then_inc(s_head_hi, 1)
                dve.wait_ge(s_head_hi, NCH * l + c + 1)
                low = headT[32:32 + DK, :]
                nc.vector.tensor_tensor(low, S[32:32 + DK, :], low.bitcast(fp32), ALU.subtract).then_inc(s_head, 1)

            def residual1(l, c):
                a = NCH * l + c
                dve.wait_ge(s_wo, a + 1)
                wait_after(dve, s_x1, KT * a)
                for kt in range(KT):
                    nc.vector.tensor_tensor(z1[:, kt, :], O[kt][:], xT[:, kt, c * CT:(c + 1) * CT], ALU.add).then_inc(s_z1, 1)

            def split_x1(l, c):
                for kt in range(KT):
                    dve.wait_ge(s_x1hi, KT * (NCH * l + c) + kt + 1)
                    nc.vector.tensor_tensor(x1_lo[:, c % 2, kt, :], x1[:, c % 2, kt, :], x1_hi[:, c % 2, kt, :].bitcast(fp32),
                                            ALU.subtract).then_inc(s_x1lo, 1)

            def split_hidden(l, c, m):
                dve.wait_ge(s_hhi, MT * (NCH * l + c) + m + 1)
                nc.vector.tensor_tensor(hid_lo[:, m % RING, :], hid[:, m % 2, :], hid_hi[:, m % RING, :].bitcast(fp32),
                                        ALU.subtract).then_inc(s_hlo, 1)

            def residual2(l, c):
                s = NCH * l + c
                dve.wait_ge(s_y, after(s_y, MT * (s + 1)))
                dve.wait_ge(s_x, KT * (NCH + s))
                for kt in range(KT):
                    nc.vector.tensor_tensor(z2[:, kt, :], Y[kt][:], x1[:, c % 2, kt, :], ALU.add).then_inc(s_z2, 1)

            def split_low(l, m):
                dve.wait_ge(s_w_hi, MT * l + m + 1)
                nc.vector.tensor_tensor(w_lo[:, m, :], w_raw[:, m, :], w_hi[:, m, :].bitcast(fp32),
                                        ALU.subtract).then_inc(s_w_lo, 1)

            def layer(t, l):
                return t[:, bass.ds(l, 1), :]

            def place_qkv(l):
                if not isinstance(l, int):
                    dve.wait_ge(s_qkv, NCH * l)
                nc.vector.tensor_copy(qkv_w[:].unsqueeze(1), layer(qkv_all, l)).then_inc(s_attw, 1)

            def place_attention(l):
                if not isinstance(l, int):
                    dve.wait_ge(s_x1, KT * NCH * l)
                nc.vector.tensor_copy(wo_w[:].unsqueeze(1), layer(wo_all, l)).then_inc(s_wo_hi, 1)
                dve.wait_ge(s_wo_hi, l + 1)
                low = wo_w[64:64 + DK, :]
                nc.vector.tensor_tensor(low.unsqueeze(1), wo_all[64:64 + DK, bass.ds(l, 1), :], low.bitcast(fp32).unsqueeze(1), ALU.subtract)
                nc.vector.tensor_copy(qkvb[:], qkvb_all[:, bass.ds(l, 1)])
                nc.vector.tensor_copy(bn1[:].rearrange("p k t -> p (k t)").unsqueeze(1), layer(norm1_all, l)).then_inc(s_attv, 1)

            def place_ffb(l):
                if not isinstance(l, int):
                    dve.wait_ge(s_relu, after(s_relu, MT * NCH * l))
                nc.vector.tensor_copy(ffb[:].unsqueeze(1), layer(ffb_all, l)).then_inc(s_ffb, 1)

            def place_bn2(l):
                dve.wait_ge(s_x, KT * NCH * (l + 1))
                nc.vector.tensor_copy(bn2[:].rearrange("p k t -> p (k t)").unsqueeze(1), layer(norm2_all, l)).then_inc(s_bn2, 1)

            def mixw_low(i):
                dve.wait_ge(s_mixw_hi, i + 1)
                hi, lo = [t[:, :, i * D:(i + 1) * D] for t in mixw]
                nc.vector.tensor_tensor(lo, mixw_raw[:, :, i * D:(i + 1) * D], hi.bitcast(fp32), ALU.subtract).then_inc(s_mixw_lo, 1)

            def take_h(c):
                if c == 1:
                    dve.wait_ge(s_mixw_lo, 5)
                for i in range(2):
                    dve.wait_ge(s_hturn, 2 * c + i + 1)
                    nc.vector.tensor_copy(h[:, c * CHUNK + 2 * i:c * CHUNK + 2 * i + 2, :].rearrange("p n d -> p (n d)"),
                                          O[i][:]).then_inc(s_hout, 1)

            def decay_mask(i):
                dve.wait_ge(s_decay, i + 1)
                nc.vector.tensor_tensor(decays[:, i, :], decays[:, i, :], later_sb[:], ALU.mult).then_inc(s_masked, 1)
                dve.wait_ge(s_masked, i + 1)
                nc.vector.scalar_tensor_tensor(decays[:, i, :], ident[:], bonus_sb[:, i:i + 1], decays[:, i, :],
                                               ALU.mult, ALU.add)

            norm1_all = norm_all[:, 0, :, :, :].rearrange("p l k t -> p l (k t)")
            norm2_all = norm_all[:, 1, :, :, :].rearrange("p l k t -> p l (k t)")

            def step(l, c, attend=True, refresh=True, extra=None):
                nxt = following(l, c)
                if refresh and c == NCH - 1:
                    place_attention(l + 1)
                for m in range(MT):
                    if attend and m == 0:
                        turn_qv(*nxt)
                    if c == 0 and m == 2:
                        place_bn2(l)
                    if attend and m == 4:
                        softmax_norm(*nxt)
                    if attend and m == 6:
                        turn_head(*nxt)
                    if attend and m == 7:
                        residual1(*nxt)
                    split_hidden(l, c, m)
                    if extra:
                        extra(c, m)
                    if attend and m == 1:
                        softmax_max(*nxt)
                    if refresh and c == NCH - 1 and m >= 3:
                        split_low(l + 1, m - 3)
                if attend:
                    split_x1(*nxt)
                if refresh and c == NCH - 1:
                    place_ffb(l + 1)
                if refresh and c == NCH - 2:
                    place_qkv(l + 1)
                residual2(l, c)
                if refresh and c == NCH - 1:
                    for m in range(MT - 3, MT):
                        split_low(l + 1, m)

            for s in (s_hlo, s_z2):
                dve.sem_inc(s, CREDIT[s])
            nc.vector.memset(vtok[:], 0.0).then_inc(s_zero, 1)
            dve.wait_ge(s_zero, 1)
            dve.wait_ge(s_ids, 16)
            nc.vector.tensor_scalar(id_wrap[:], ids_sb[:], 0, V, ALU.is_lt, ALU.mult).then_inc(s_idx, 1)
            dve.wait_ge(s_idx, 1)
            nc.vector.tensor_tensor(id_wrap[:], id_wrap[:], ids_sb[:], ALU.add).then_inc(s_idx, 1)
            dve.wait_ge(s_idx, 2)
            nc.vector.tensor_scalar(id_row[:], id_wrap[:], 0, V - 1, ALU.max, ALU.min).then_inc(s_idx, 1)
            dve.wait_ge(s_misc, 7 * 16)
            nc.vector.memset(minus_half[:], -0.5).then_inc(s_pre, 1)
            nc.vector.tensor_scalar(norm_tmp[:], raw[:, 3], BN_EPS, None, ALU.add).then_inc(s_pre, 1)
            for c in range(NCH):
                dve.wait_ge(s_gather[c], 16 * CHUNK)
                rows = tok[:, c * CHUNK:(c + 1) * CHUNK, :]
                nc.vector.tensor_scalar(rows, rows, pes_sb[:, 0:1], None, ALU.add).then_inc(s_emb, 1)
            dve.wait_ge(s_pow, 1)
            for w in range(2):
                nc.vector.tensor_tensor(norm_all[:, w, :, 0, :], raw[:, 0, w], norm_tmp[:, w], ALU.mult)
            nc.vector.tensor_tensor(raw[:, 4], raw[:, 4], raw[:, 2], ALU.subtract).then_inc(s_pre, 1)
            dve.wait_ge(s_pre, 3)
            for w in range(2):
                last = nc.vector.tensor_tensor(raw[:, 4, w], raw[:, 4, w], norm_all[:, w, :, 0, :], ALU.mult)
            last.then_inc(s_pre, 1)
            dve.wait_ge(s_pre, 4)
            for w in range(2):
                last = nc.vector.tensor_tensor(norm_all[:, w, :, 1, :], raw[:, 4, w], raw[:, 1, w], ALU.add)
            last.then_inc(s_pre, 1)
            dve.wait_ge(s_pre, 5)
            place_qkv(0)
            place_attention(0)
            place_ffb(0)
            turn_qv(0, 0)
            softmax_max(0, 0)
            softmax_norm(0, 0)
            turn_head(0, 0)
            residual1(0, 0)
            split_x1(0, 0)
            for m in range(MT):
                split_low(0, m)
            with dve.Fori(0, L - 1) as l:
                for c in range(NCH):
                    step(l, c)
            dve.wait_ge(s_rate, 1)
            nc.vector.tensor_scalar(rate[:], rate[:], RATE_MAX, -1.0, ALU.min, ALU.mult).then_inc(s_rate, 1)

            def extra(c, m):
                if m % 2:
                    decay_mask(c * (MT // 2) + m // 2)
                elif 3 * c + m // 2 < 5 and m < 6:
                    mixw_low(3 * c + m // 2)
            for c in range(NCH):
                step(L - 1, c, attend=c < NCH - 1, refresh=False, extra=extra)
                if c >= 1:
                    take_h(c - 1)
            take_h(NCH - 1)


EVENTS = dict(
    hnT=2, mix_hi=4, r=4, k=2, tanh=4, vg=4, sq=2, yT_hi=2, h2T_hi=2, rexp=1, hn=4, hn2=4,
    hnT_t=2, r_t=2, k_t=2, vg_t=4, s_t=16, y_t=4, yT_t=2, o_t=2, h2T_t=2, lg_t=1, moe_t=16,
    st1=4, mv1=4, wide=16, gsum=2, gmean=2, yc=2, gsq=2, yn=4, yg=2,
    xx=2, mix=4, last_lo=1, bias1=1, bias2=1, yT_lo=2, h2T_lo=2, h2=2, st2=4, mv2=4, rt=16, coef=1, acc0=4, moe=32,
    v1=1, rstd1=1, v2=1, rstd2=1, gv=2, grstd=2, mix_lo=3, silu=4, goff=2, gates=2,
)


def mixer_and_experts(nc, bank, h, ident, mixw, decays, w_exp, w_router, maa_in, ln_affine, even_odd, expert_no, out):
    fp32, fp32r, u32 = mybir.dt.float32, mybir.dt.float32r, mybir.dt.uint32
    ALU, ACT, AX = mybir.AluOpType, mybir.ActivationFunctionType, mybir.AxisListType
    R, K, VV, G, O = range(5)
    PAIR = 2
    UNITS = CHUNK * NE // 2

    ctx = ExitStack()
    with ctx:
        def sb(name, shape, dt=fp32):
            return ctx.enter_context(nc.sbuf_tensor(name, shape, dt))

        E = {name: ctx.enter_context(nc.semaphore("e_" + name)) for name in EVENTS}
        s_in, s_const, s_halved, s_out, s_exp_in, s_e_hi, s_e_lo, s_router_hi, s_router_lo = [ctx.enter_context(nc.semaphore(n)) for n in (
            "s_in", "s_const", "s_halved", "s_out", "s_exp_in", "s_e_hi", "s_e_lo", "s_router_hi", "s_router_lo")]

        def wait(eng, name, c, k):
            n = EVENTS[name] * c + k
            if not (isinstance(n, int) and n <= 0):
                eng.wait_ge(E[name], n)

        experts = [sb(f"experts_{part}", [P, KT, NE * D], fp32r) for part in ("hi", "lo")]
        router = [sb(f"router_{part}", [P, KT, NE], fp32r) for part in ("hi", "lo")]
        router_raw = sb("router_raw", [P, KT, NE])
        maa = sb("maa", [P, 4, KT])
        affine = sb("affine", [P, 2, D])
        parity = sb("parity", [P, 2])
        expno = sb("expno", [P, NE])
        minus_half = sb("minus_half2", [P, PAIR * NH])
        ln_eps = sb("ln_eps", [P, CHUNK])
        gn_eps = sb("gn_eps", [P, PAIR * NH])
        held = sb("held", [P, 1])

        stats = sb("stats", [P, 2, CHUNK, 6])
        mv = sb("mv", [P, 2, CHUNK, 2])
        var = sb("var", [P, 2, CHUNK])
        rstd = sb("rstd", [P, 2, CHUNK])
        hn = sb("hn", [P, CHUNK, D])
        hnT = sb("hnT", [P, KT, CHUNK, T + 1])
        xx = sb("xx", [P, KT, CHUNK, T])
        mix_whole = sb("mix_whole", [P, 2, KT, CT])
        mix = [sb(f"mix_{part}", [P, 4, KT, CT], fp32r) for part in ("hi", "lo")]
        r_eo = sb("r_eo", [P, KT, 2, CT])
        kT = sb("kT2", [P, KT, CT])
        vg = sb("vg", [P, CHUNK, 2, D])
        gate = sb("gate", [P, CHUNK, D])
        offs = sb("offs", [P, CHUNK, D])
        weighed = sb("weighed", [P, 2, NH, T])
        experts_raw = weighed[:].rearrange("p b h t -> p (b h t)").rearrange("p (k e) -> p k e", k=KT)
        gsum = sb("gsum", [P, 2, PAIR * NH])
        gmean = sb("gmean", [P, 2, PAIR * NH])
        gvar = sb("gvar", [P, 2, PAIR * NH])
        grstd = sb("grstd", [P, 2, PAIR * NH])
        yc = sb("yc", [P, CHUNK, D])
        yT = [sb(f"yT_{part}", [P, KT, CT], fp32r) for part in ("hi", "lo")]
        hn2 = sb("hn2", [P, CHUNK, D])
        ysq = hn2
        nbias = sb("nbias2", [P, 2, CHUNK])
        h2T = [sb(f"h2T_{part}", [P, KT, CT], fp32r) for part in ("hi", "lo")]
        lg = sb("lg", [P, CHUNK, NE])
        lmax = sb("lmax", [P, CHUNK])
        psm = sb("psm", [P, CHUNK, NE])
        psum_ = sb("psum_", [P, CHUNK])
        top = sb("top", [P, CHUNK, NE])
        topi = sb("topi", [P, CHUNK, NE], u32)
        topf = sb("topf", [P, CHUNK, TOPK])
        tsum = sb("tsum", [P, CHUNK])
        wtop = sb("wtop", [P, CHUNK, TOPK])
        wprod = sb("wprod", [P, CHUNK, TOPK])
        ebias = sb("ebias", [P, CHUNK])
        pick = sb("pick", [P, TOPK, CHUNK, NE])
        coef = sb("coef", [P, CHUNK, NE])

        M = [bank[0], bank[1]]
        B = bank[2:8]
        R_BANKS = B[0:2]
        K_BANKS = B[4:6]
        Y_BANKS = B[2:4]
        SC = [B[0], B[1], B[4], B[5]]
        VG = [M[0], M[1], B[2], B[3]]
        LG = M[1]

        def seq(t, n):
            return t[..., n * T:(n + 1) * T]

        def rows(c, n, count=1):
            return h[:, bass.ds(c * CHUNK + n, count), :]

        def of_pair(t, p):
            return t[:, PAIR * p:PAIR * (p + 1), :]

        block = ctx.enter_context(nc.Block())

        @block.sync
        def _(sp):
            for dst, src in ((affine[:], ln_affine), (parity[:], even_odd), (maa[:], maa_in), (expno[:], expert_no),
                             (router_raw[:], w_router)):
                sp.dma_start(dst, src).then_inc(s_in, 16)
            sp.dma_start(experts_raw, w_exp).then_inc(s_exp_in, 16)

            def store(c):
                for n in range(CHUNK):
                    wait(sp, "moe", c, NE * (n + 1))
                    sp.dma_start(out[bass.ds(c * CHUNK + n, 1), :, :].rearrange("s t d -> (s t) d"),
                                 rows(c, n).rearrange("p n d -> p (n d)")).then_inc(s_out, 16)

            with sp.Fori(0, NCH) as c:
                store(c)
            sp.wait_ge(s_out, 16 * NSEQ)

        @block.gpsimd
        def _(pool):
            def root(c, which):
                w = which - 1
                wait(pool, f"mv{which}", c, CHUNK)
                nc.gpsimd.tensor_tensor(var[:, w, :], mv[:, w, :, 1], ln_eps[:], ALU.add).then_inc(E[f"v{which}"], 1)
                wait(pool, f"v{which}", c, 1)
                nc.gpsimd.tensor_tensor(rstd[:, w, :], var[:, w, :], minus_half[:, 0:CHUNK], ALU.pow).then_inc(E[f"rstd{which}"], 1)

            def gates(c):
                for p in range(2):
                    wait(pool, "vg", c, PAIR * (p + 1))
                    wait(pool, "tanh", c, PAIR * (p + 1))
                    g, t, o = vg[:, PAIR * p:PAIR * (p + 1), 1, :], of_pair(gate, p), of_pair(offs, p)
                    nc.gpsimd.tensor_tensor(o, t, g, ALU.mult).then_inc(E["silu"], 1)
                    wait(pool, "silu", c, 2 * p + 1)
                    nc.gpsimd.tensor_tensor(t, o, g, ALU.add).then_inc(E["silu"], 1)
                    wait(pool, "silu", c, 2 * p + 2)
                    nc.gpsimd.tensor_tensor(o, t, affine[:, 1, :].unsqueeze(1).to_broadcast([P, PAIR, D]), ALU.mult).then_inc(E["goff"], 1)
                    wait(pool, "goff", c, p + 1)
                    nc.gpsimd.tensor_tensor(t, t, affine[:, 0, :].unsqueeze(1).to_broadcast([P, PAIR, D]), ALU.mult).then_inc(E["gates"], 1)

            def group_root(c, p):
                wait(pool, "gsq", c, p + 1)
                nc.gpsimd.tensor_tensor(gvar[:, p, :], gvar[:, p, :], gn_eps[:], ALU.add).then_inc(E["gv"], 1)
                wait(pool, "gv", c, p + 1)
                nc.gpsimd.tensor_tensor(grstd[:, p, :], gvar[:, p, :], minus_half[:], ALU.pow).then_inc(E["grstd"], 1)

            def mix_low(c, i):
                wait(pool, "mix_hi", c, i + 1)
                hi, lo = [t[:, i] for t in mix]
                nc.gpsimd.tensor_tensor(lo, mix_whole[:, i % 2], hi.bitcast(fp32), ALU.subtract).then_inc(E["mix_lo"], 1)

            def step(c, front=True, back=True, more=True):
                if front and more:
                    root(c + 1, 1)
                if back:
                    root(c - 1, 2)
                if front:
                    gates(c)
                    if more:
                        mix_low(c + 1, 0)
                    group_root(c, 0)
                    if more:
                        mix_low(c + 1, 1)
                        mix_low(c + 1, 2)
                    group_root(c, 1)

            pool.memset(ln_eps[:], LN_EPS)
            pool.memset(gn_eps[:], GN_EPS)
            pool.memset(minus_half[:], -0.5).then_inc(s_const, 1)
            pool.wait_ge(s_const, 1)
            root(0, 1)
            for i in range(3):
                mix_low(0, i)
            pool.wait_ge(s_halved, 1)
            step(0, back=False)
            with pool.Fori(1, NCH - 1) as c:
                step(c)
            step(NCH - 1, more=False)
            step(NCH, front=False)

        @block.tensor
        def _(pe):
            def turn_tokens(c, src, ready, banks, done):
                for n in range(CHUNK):
                    if ready:
                        wait(pe, ready, c, n + 1)
                    for kt in range(KT):
                        last = nc.tensor.transpose(seq(banks[kt], n), src[:, n, kt * P:(kt + 1) * P], ident[:])
                        if n == CHUNK - 1:
                            last.then_inc(E[done], 1)

            def turn_normed(c):
                wait(pe, "vg", c - 1, 2)
                turn_tokens(c, hn, "hn", M, "hnT_t")

            def weights(i, cols):
                return lambda kt: [t[:, kt, i * D + cols.start:i * D + cols.stop] for t in mixw]

            def project_rk(c):
                wait(pe, "wide", c, 0)
                for i, banks, done in ((R, R_BANKS, "r_t"), (K, K_BANKS, "k_t")):
                    wait(pe, "mix_lo", c, i + 1)
                    for mt in range(KT):
                        w = weights(i, slice(mt * P, (mt + 1) * P))
                        for kt in range(KT):
                            last = three(nc, banks[mt][:], w(kt), [t[:, i, kt, :] for t in mix], kt == 0, kt == KT - 1)
                        last.then_inc(E[done], 1)

            def project_vg(c, n):
                if n < 2:
                    wait(pe, "moe", c - 1, 0)
                else:
                    wait(pe, "yc", c, 0)
                for j, i in enumerate((VV, G)):
                    wait(pe, *(("last_lo", c, 1) if i == G else ("mix_lo", c, i + 1)))
                    for kt in range(KT):
                        last = three(nc, VG[n][:, j * D:(j + 1) * D], [seq(t[:, i, kt, :], n) for t in mix],
                                     weights(i, slice(0, D))(kt), kt == 0, kt == KT - 1)
                last.then_inc(E["vg_t"], 1)

            def scores(c, n, mt):
                if n == 0 and mt == 0:
                    wait(pe, "r", c, 4)
                    wait(pe, "k", c, 2)
                    wait(pe, "yT_lo", c - 1, 2)
                    wait(pe, "h2", c - 1, 2)
                elif mt == 0:
                    wait(pe, "wide", c, QUAD * n)
                for q in range(QUAD):
                    at = slice(32 * q, 32 * q + 32)
                    last = nc.tensor.matmul(SC[q][:, mt * 2 * T:(mt + 1) * 2 * T], seq(kT[at, mt, :], n),
                                            seq(r_eo[at, mt, :, :], n), start=True, stop=True)
                    if mt == KT - 1:
                        last.then_inc(E["s_t"], 1)

            def values(c, n, half):
                if half == 0:
                    wait(pe, "wide", c, QUAD * (n + 1))
                if n == 0:
                    wait(pe, "vg", c, CHUNK)
                for head in range(half * NH // 2, (half + 1) * NH // 2):
                    mt, q, e = head // 8, head % 8 // 2, head % 2
                    at = (n % PAIR) * D + head * DH
                    last = nc.tensor.matmul(Y_BANKS[n // PAIR][:, at:at + DH], weighed[:, n % 2, q * 4 + mt * 2 + e, :],
                                            vg[:, n, 0, head * DH:(head + 1) * DH], start=True, stop=True)
                if half:
                    last.then_inc(E["y_t"], 1)

            def turn_y(c):
                wait(pe, "yg", c, 2)
                turn_tokens(c, yc, None, R_BANKS, "yT_t")

            def project_out(c):
                wait(pe, "yT_lo", c, 2)
                for n in range(CHUNK):
                    at = (n % PAIR) * D
                    for kt in range(KT):
                        last = three(nc, K_BANKS[n // PAIR][:, at:at + D], [seq(t[:, kt, :], n) for t in yT],
                                     weights(O, slice(0, D))(kt), kt == 0, kt == KT - 1)
                    if n % PAIR == 1:
                        last.then_inc(E["o_t"], 1)

            def turn_h2(c):
                turn_tokens(c, hn2, "hn2", M, "h2T_t")

            def route(c):
                wait(pe, "h2T_lo", c, 2)
                for n in range(CHUNK):
                    for kt in range(KT):
                        last = three(nc, LG[:, n * NE:(n + 1) * NE], [seq(t[:, kt, :], n) for t in h2T],
                                     [t[:, kt, :] for t in router], kt == 0, kt == KT - 1)
                last.then_inc(E["lg_t"], 1)

            def moe(c, first, last_):
                for u in range(first, last_):
                    n, pair = divmod(u, NE // 2)
                    if u == 1:
                        wait(pe, "rt", c, 3)
                    if u >= 2:
                        wait(pe, "moe", c, 2 * (u - 1))
                    for kt in range(KT):
                        last = three(nc, M[u % 2][:], [seq(t[:, kt, :], n) for t in h2T],
                                     [t[:, kt, pair * 2 * D:(pair + 1) * 2 * D] for t in experts], kt == 0, kt == KT - 1)
                    last.then_inc(E["moe_t"], 1)

            def step(c, front=True, back=True, more=True):
                p = c - 1
                if front:
                    project_rk(c)
                    project_vg(c, 0)
                    project_vg(c, 1)
                if back:
                    if front:
                        wait(pe, "r", c, 4)
                    turn_y(p)
                if front:
                    project_vg(c, 2)
                if back:
                    if front:
                        wait(pe, "k", c, 2)
                    project_out(p)
                if front:
                    project_vg(c, 3)
                    if more:
                        turn_normed(c + 1)
                    scores(c, 0, 0)
                    scores(c, 0, 1)
                if back:
                    if front:
                        wait(pe, *(("hnT", c + 1, KT) if more else ("vg", c, 2)))
                    turn_h2(p)
                    route(p)

                def fill(*units):
                    if back:
                        moe(p, *units)
                if not front:
                    fill(0, UNITS)
                    return
                for n in range(1, CHUNK):
                    u = 4 * (n - 1)
                    scores(c, n, 0)
                    fill(u, u + 1)
                    scores(c, n, 1)
                    fill(u + 1, u + 2)
                    values(c, n - 1, 0)
                    fill(u + 2, u + 3)
                    values(c, n - 1, 1)
                    fill(u + 3, u + 4)
                values(c, CHUNK - 1, 0)
                fill(12, 13)
                values(c, CHUNK - 1, 1)
                fill(13, 16)

            pe.wait_ge(s_in, 5 * 16)
            turn_normed(0)
            wait(pe, "hnT", 0, KT)
            step(0, back=False)
            pe.wait_ge(s_router_lo, 1)
            pe.wait_ge(s_e_lo, NE)
            with pe.Fori(1, NCH - 1) as c:
                step(c)
            step(NCH - 1, more=False)
            step(NCH, front=False)

        @block.scalar
        def _(act):
            def turned(c, name, dst, banks):
                for kt in range(KT):
                    wait(act, name.removesuffix("_hi") + "_t", c, kt + 1)
                    nc.scalar.copy(dst[:, kt, :], banks[kt][:]).then_inc(E[name], 1)

            def vg_out(c, n):
                wait(act, "vg_t", c, n + 1)
                if n == 0:
                    wait(act, "yg", c - 1, 2)
                    wait(act, "gates", c - 1, 2)
                nc.scalar.activation(gate[:, n, :], VG[n][:, D:2 * D], ACT.Tanh, scale=0.5).then_inc(E["tanh"], 1)
                nc.scalar.copy(vg[:, n].rearrange("p j d -> p (j d)"), VG[n][:]).then_inc(E["vg"], 1)

            def normed(c, dst, which, done):
                w = which - 1
                wait(act, f"bias{which}", c, 1)
                for n in range(CHUNK):
                    nc.scalar.activation(dst[:, n, :], rows(c, n).rearrange("p n d -> p (n d)"), ACT.Identity,
                                         bias=nbias[:, w, n:n + 1], scale=rstd[:, w, n:n + 1]).then_inc(E[done], 1)

            def normed_out(c):
                for kt in range(KT):
                    wait(act, "hnT_t", c, kt + 1)
                    nc.scalar.copy(hnT[:, kt, :, 1:T + 1], M[kt][:].rearrange("p (n t) -> p n t", n=CHUNK)).then_inc(E["hnT"], 1)

            def mix_high(c, i):
                wait(act, "mix", c, i + 1)
                nc.scalar.copy(mix[0][:, i], mix_whole[:, i % 2]).then_inc(E["mix_hi"], 1)

            def step(c, front=True, back=True, more=True):
                p = c - 1
                if front:
                    for mt in range(KT):
                        wait(act, "r_t", c, mt + 1)
                        for e in range(2):
                            nc.scalar.mul(r_eo[:, mt, e, :], R_BANKS[mt][:], parity[:, e:e + 1]).then_inc(E["r"], 1)
                    turned(c, "k", kT, K_BANKS)
                    if more:
                        normed(c + 1, hn, 1, "hn")
                    vg_out(c, 0)
                    vg_out(c, 1)
                if back:
                    turned(p, "yT_hi", yT[0], R_BANKS)
                if front:
                    vg_out(c, 2)
                    vg_out(c, 3)
                    if more:
                        normed_out(c + 1)
                if back:
                    normed(p, hn2, 2, "hn2")
                    turned(p, "h2T_hi", h2T[0], M)
                    wait(act, "rt", p, 2)
                    nc.scalar.activation(psm[:], lg[:], ACT.Exp).then_inc(E["rexp"], 1)

                def square(q):
                    wait(act, "yc", c, q + 1)
                    nc.scalar.activation(of_pair(ysq, q), of_pair(yc, q), ACT.Square, scale=DH ** -0.5).then_inc(E["sq"], 1)
                if front:
                    if more:
                        mix_high(c + 1, 0)
                    square(0)
                    if more:
                        mix_high(c + 1, 1)
                        mix_high(c + 1, 2)
                        mix_high(c + 1, 3)
                    square(1)

            act.wait_ge(s_in, 5 * 16)
            normed(0, hn, 1, "hn")
            normed_out(0)
            for i in range(4):
                mix_high(0, i)
            nc.scalar.copy(router[0][:], router_raw[:]).then_inc(s_router_hi, 1)
            act.wait_ge(s_exp_in, 16)
            for i in range(NE):
                cols = slice(i * D, (i + 1) * D)
                nc.scalar.copy(experts[0][:, :, cols], experts_raw[:, :, cols]).then_inc(s_e_hi, 1)
            step(0, back=False)
            with act.Fori(1, NCH - 1) as c:
                step(c)
            step(NCH - 1, more=False)
            step(NCH, front=False)

        @block.vector
        def _(dve):
            def hold():
                nc.vector.memset(held[:], 0.0)

            def low(c, name, banks, parts):
                for kt in range(KT):
                    wait(dve, name + "_hi", c, kt + 1)
                    hi, lo = [t[:, kt] for t in parts]
                    nc.vector.tensor_tensor(lo, banks[kt][:], hi.bitcast(fp32), ALU.subtract).then_inc(E[name + "_lo"], 1)

            def norm(c, which):
                w = which - 1
                for n in range(CHUNK):
                    nc.vector.bn_stats(stats[:, w, n, :], rows(c, n).rearrange("p n d -> p (n d)")).then_inc(E[f"st{which}"], 1)
                wait(dve, f"st{which}", c, CHUNK)
                hold()
                for n in range(CHUNK):
                    nc.vector.bn_aggr(mv[:, w, n, :], stats[:, w, n, :]).then_inc(E[f"mv{which}"], 1)

            def norm_bias(c, which):
                w = which - 1
                wait(dve, f"rstd{which}", c, 1)
                nc.vector.scalar_tensor_tensor(nbias[:, w, :], mv[:, w, :, 0], -1.0, rstd[:, w, :], ALU.mult,
                                               ALU.mult).then_inc(E[f"bias{which}"], 1)

            def mixes(c):
                for kt in range(KT):
                    wait(dve, "hnT", c, kt + 1)
                    nc.vector.tensor_tensor(xx[:, kt], hnT[:, kt, :, 0:T], hnT[:, kt, :, 1:T + 1], ALU.subtract).then_inc(E["xx"], 1)
                wait(dve, "xx", c, KT)

            def mix_of(c, i):
                if i == 2:
                    wait(dve, "mix_lo", c, 1)
                if i == 3:
                    wait(dve, "mix_lo", c, 2)
                for kt in range(KT):
                    last = nc.vector.scalar_tensor_tensor(
                        mix_whole[:, i % 2, kt].rearrange("p (n t) -> p n t", n=CHUNK), xx[:, kt], maa[:, i, kt:kt + 1],
                        hnT[:, kt, :, 1:T + 1], ALU.mult, ALU.add)
                last.then_inc(E["mix"], 1)

            def mix_low(c, i):
                wait(dve, "mix_hi", c, i + 1)
                hi, lo = [t[:, i] for t in mix]
                nc.vector.tensor_tensor(lo, mix_whole[:, i % 2], hi.bitcast(fp32), ALU.subtract).then_inc(E["last_lo"], 1)

            def weigh(c, n):
                if n >= 2:
                    wait(dve, "y_t", c, n - 1)
                for q in range(QUAD):
                    wait(dve, "s_t", c, QUAD * n + q + 1)
                    nc.vector.tensor_tensor(weighed[:, n % 2, 4 * q:4 * q + 4, :], SC[q][:].rearrange("p (h t) -> p h t", t=T),
                                            decays[:, 4 * q:4 * q + 4, :], ALU.mult).then_inc(E["wide"], 1)

            def heads(t):
                return t.rearrange("p n (h d) -> p (n h) d", d=DH)

            def group_centre(c, p):
                y = Y_BANKS[p][:].rearrange("p (h d) -> p h d", d=DH)
                wait(dve, "y_t", c, PAIR * (p + 1))
                nc.vector.reduce_sum(gsum[:, p, :], y, AX.X).then_inc(E["gsum"], 1)
                wait(dve, "gsum", c, p + 1)
                nc.vector.tensor_scalar(gmean[:, p, :], gsum[:, p, :], 1.0 / DH, None, ALU.mult).then_inc(E["gmean"], 1)
                wait(dve, "gmean", c, p + 1)
                nc.vector.tensor_tensor(heads(of_pair(yc, p)), y, gmean[:, p, :].unsqueeze(2).to_broadcast([P, PAIR * NH, DH]),
                                        ALU.subtract).then_inc(E["yc"], 1)

            def group_var(c, p):
                wait(dve, "sq", c, p + 1)
                nc.vector.reduce_sum(gvar[:, p, :], heads(of_pair(ysq, p)), AX.X).then_inc(E["gsq"], 1)

            def group_out(c, p):
                t = of_pair(yc, p)
                wait(dve, "grstd", c, p + 1)
                nc.vector.tensor_tensor(heads(t), heads(t), grstd[:, p, :].unsqueeze(2).to_broadcast([P, PAIR * NH, DH]),
                                        ALU.mult).then_inc(E["yn"], 1)
                wait(dve, "yn", c, 2 * p + 1)
                wait(dve, "gates", c, p + 1)
                nc.vector.tensor_tensor(t, t, of_pair(gate, p), ALU.mult).then_inc(E["yn"], 1)
                wait(dve, "yn", c, 2 * p + 2)
                nc.vector.tensor_tensor(t, t, of_pair(offs, p), ALU.add).then_inc(E["yg"], 1)

            def residual(c):
                for p in range(2):
                    wait(dve, "o_t", c, p + 1)
                    t = rows(c, PAIR * p, PAIR)
                    nc.vector.tensor_tensor(t, K_BANKS[p][:].rearrange("p (n d) -> p n d", n=PAIR), t, ALU.add).then_inc(E["h2"], 1)
                wait(dve, "h2", c, 2)
                hold()

            def route(c):
                k = [0]

                def did(ins):
                    k[0] += 1
                    ins.then_inc(E["rt"], 1)
                    wait(dve, "rt", c, k[0])
                wait(dve, "lg_t", c, 1)
                logits = LG[:, 0:CHUNK * NE].rearrange("p (n e) -> p n e", n=CHUNK)

                def wide(t):
                    return t.to_broadcast([P, CHUNK, NE])
                did(nc.vector.reduce_max(lmax[:], logits, AX.X))
                did(nc.vector.tensor_tensor(lg[:], logits, wide(lmax[:].unsqueeze(2)), ALU.subtract))
                wait(dve, "rexp", c, 1)
                did(nc.vector.reduce_sum(psum_[:], psm[:], AX.X))
                did(nc.vector.reciprocal(psum_[:], psum_[:]))
                did(nc.vector.tensor_tensor(psm[:], psm[:], wide(psum_[:].unsqueeze(2)), ALU.mult))
                hold()
                for n in range(CHUNK):
                    last = nc.vector.max(top[:, n, :], psm[:, n, :])
                did(last)
                hold()
                for n in range(CHUNK):
                    last = nc.vector.max_index(topi[:, n, :], top[:, n, :], psm[:, n, :])
                did(last)
                nc.vector.tensor_tensor(tsum[:], top[:, :, 0], top[:, :, 1], ALU.add)
                did(nc.vector.tensor_copy(topf[:], topi[:, :, 0:TOPK]))
                did(nc.vector.tensor_scalar(tsum[:], tsum[:], TOP_EPS, None, ALU.add))
                did(nc.vector.reciprocal(tsum[:], tsum[:]))
                did(nc.vector.tensor_tensor(wtop[:], top[:, :, 0:TOPK], tsum[:].unsqueeze(2).to_broadcast([P, CHUNK, TOPK]), ALU.mult))
                for j in range(TOPK):
                    nc.vector.tensor_tensor(pick[:, j], wide(topf[:, :, j:j + 1]), expno[:].unsqueeze(1).to_broadcast([P, CHUNK, NE]),
                                            ALU.is_equal)
                did(nc.vector.tensor_tensor(wprod[:], wtop[:], top[:, :, 0:TOPK], ALU.mult))
                for j in range(TOPK):
                    nc.vector.tensor_tensor(pick[:, j], pick[:, j], wide(wtop[:, :, j:j + 1]), ALU.mult)
                did(nc.vector.tensor_tensor(ebias[:], wprod[:, :, 0], wprod[:, :, 1], ALU.add))
                did(nc.vector.tensor_tensor(coef[:], pick[:, 0], pick[:, 1], ALU.add))
                for n in range(CHUNK):
                    t = rows(c, n).rearrange("p n d -> p (n d)")
                    nc.vector.tensor_scalar(t, t, ebias[:, n:n + 1], None, ALU.add).then_inc(E["acc0"], 1)
                k[0] += 2
                nc.vector.tensor_copy(lmax[:], tsum[:]).then_inc(E["rt"], 2)
                assert k[0] == EVENTS["rt"], k

            def add_experts(c, first, last):
                for u in range(first, last):
                    n, pair = divmod(u, NE // 2)
                    wait(dve, "moe_t", c, u + 1)
                    acc = rows(c, n).rearrange("p n d -> p (n d)")
                    for j in range(2):
                        if pair + j == 0:
                            wait(dve, "acc0", c, n + 1)
                        else:
                            wait(dve, "moe", c, 2 * u + j)
                        nc.vector.scalar_tensor_tensor(acc, M[u % 2][:, j * D:(j + 1) * D],
                                                       coef[:, n, 2 * pair + j:2 * pair + j + 1], acc,
                                                       ALU.mult, ALU.add).then_inc(E["moe"], 1)

            def step(c, front=True, back=True, more=True):
                p = c - 1

                def fill(first, last):
                    if back:
                        add_experts(p, first, last)
                if front and more:
                    norm(c + 1, 1)
                if back:
                    group_out(p, 0)
                if front and more:
                    norm_bias(c + 1, 1)
                if back:
                    group_out(p, 1)
                    low(p, "yT", R_BANKS, yT)
                    residual(p)
                    norm(p, 2)
                    norm_bias(p, 2)
                if front:
                    weigh(c, 0)
                if back:
                    low(p, "h2T", M, h2T)
                    route(p)
                if not front:
                    fill(0, UNITS)
                    return
                weigh(c, 1)
                fill(0, 2)
                if more:
                    mixes(c + 1)
                    mix_of(c + 1, 0)
                fill(2, 4)
                weigh(c, 2)
                fill(4, 7)
                group_centre(c, 0)
                fill(7, 8)
                if more:
                    mix_of(c + 1, 1)
                weigh(c, 3)
                group_var(c, 0)
                fill(8, 12)
                if more:
                    mix_of(c + 1, 2)
                fill(12, 13)
                if more:
                    mix_of(c + 1, 3)
                    mix_low(c + 1, 3)
                group_centre(c, 1)
                fill(13, 14)
                group_var(c, 1)
                fill(14, 16)

            nc.vector.memset(hnT[:, :, :, 0:1], 0.0)
            norm(0, 1)
            norm_bias(0, 1)
            dve.wait_ge(s_in, 5 * 16)
            nc.vector.tensor_scalar(affine[:], affine[:], 0.5, None, ALU.mult).then_inc(s_halved, 1)
            mixes(0)
            for i in range(4):
                mix_of(0, i)
            mix_low(0, 3)
            dve.wait_ge(s_router_hi, 1)
            nc.vector.tensor_tensor(router[1][:], router_raw[:], router[0][:].bitcast(fp32), ALU.subtract).then_inc(s_router_lo, 1)
            for i in range(NE):
                dve.wait_ge(s_e_hi, i + 1)
                hi, lo = [t[:, :, i * D:(i + 1) * D] for t in experts]
                nc.vector.tensor_tensor(lo, experts_raw[:, :, i * D:(i + 1) * D], hi.bitcast(fp32), ALU.subtract).then_inc(s_e_lo, 1)
            dve.wait_ge(s_e_lo, NE)
            step(0, back=False)
            with dve.Fori(1, NCH - 1) as c:
                step(c)
            step(NCH - 1, more=False)
            step(NCH, front=False)


def kernel(x, L0_tok_emb, L0_tok_pes, L0_tok_wq, L0_tok_bq, L0_tok_wk, L0_tok_bk, L0_tok_wv, L0_tok_bv, L0_tok_wo, L0_tok_bo, L0_tok_att_gamma, L0_tok_att_beta, L0_tok_att_mean, L0_tok_att_var, L0_tok_w1, L0_tok_bff1, L0_tok_w2, L0_tok_bff2, L0_tok_ffn_gamma, L0_tok_ffn_beta, L0_tok_ffn_mean, L0_tok_ffn_var,
           L0_attn_w_r, L0_attn_w_k, L0_attn_w_v, L0_attn_w_g, L0_attn_w_o, L0_attn_time_maa_k, L0_attn_time_maa_v,
           L0_attn_time_maa_r, L0_attn_time_maa_g, L0_attn_time_decay, L0_attn_time_faaaa, L0_attn_ln_g, L0_attn_ln_b,
           L0_ffn_router_w, L0_ffn_expert_weights):
    import numpy as np
    import concourse.bacc as bacc
    from concourse.bass_utils import run_bass_kernel_spmd
    A = np.asarray
    w1 = A(L0_tok_w1).reshape(L, KT, P, MT, P).transpose(0, 2, 3, 1, 4).reshape(L, P, MT, KT * P)
    w2 = A(L0_tok_w2).reshape(L, MT, P, D).transpose(0, 2, 1, 3)
    w_ffn = np.concatenate([w1, w2], axis=3)
    w_qkv = np.zeros((P, L, KT, QKVROWS), np.float32)
    qkv_bias = np.zeros((QKVROWS, L), np.float32)
    for row, w, b in ((QROW, L0_tok_wq, L0_tok_bq), (KROW, L0_tok_wk, L0_tok_bk), (VROW, L0_tok_wv, L0_tok_bv)):
        w_qkv[:, :, :, row:row + DK] = A(w).reshape(L, KT, P, DK).transpose(2, 0, 1, 3)
        qkv_bias[row:row + DK] = A(b).T
    w_o = np.zeros((STACK, L, D), np.float32)
    for row in range(0, STACK, 32):
        w_o[row:row + DK] = A(L0_tok_wo).transpose(1, 0, 2)
    kinds = [(L0_tok_att_gamma, L0_tok_ffn_gamma), (L0_tok_att_beta, L0_tok_ffn_beta), (L0_tok_att_mean, L0_tok_ffn_mean),
             (L0_tok_att_var, L0_tok_ffn_var), (L0_tok_bo, L0_tok_bff2)]
    bn_raw = np.stack([np.stack([A(v).reshape(L, KT, P).transpose(2, 0, 1) for v in two], 1) for two in kinds], 1)
    ins = dict(ids=A(x).T, emb=A(L0_tok_emb), pes=A(L0_tok_pes)[:T, 0:1], w_ffn=w_ffn,
               w_qkv=w_qkv.reshape(P, L, KT * QKVROWS), w_o=w_o, bn_raw=bn_raw, qkv_bias=qkv_bias,
               ff_bias=A(L0_tok_bff1).reshape(L, MT, P).transpose(2, 0, 1), ident_in=np.eye(P, dtype=np.float32))
    def feature_rows(w):
        return A(w).T.reshape(KT, P, -1).transpose(1, 0, 2)

    def to_all(v):
        return np.broadcast_to(A(v), (P,) + A(v).shape)

    order = [mt * 8 + q * 2 + e for q in range(QUAD) for mt in range(KT) for e in range(2)]
    key, query = np.arange(T)[:, None], np.arange(T)[None, :]
    ins.update(
        w_exp=A(L0_ffn_expert_weights).reshape(NE, KT, P, D).transpose(2, 1, 0, 3).reshape(P, KT, NE * D),
        w_mix=np.concatenate([feature_rows(w) for w in (L0_attn_w_r, L0_attn_w_k, L0_attn_w_v, L0_attn_w_g, L0_attn_w_o)], 2),
        w_router=feature_rows(L0_ffn_router_w),
        maa_in=np.stack([A(m).reshape(KT, P).T for m in (L0_attn_time_maa_r, L0_attn_time_maa_k, L0_attn_time_maa_v,
                                                         L0_attn_time_maa_g)], 1),
        decay=to_all(A(L0_attn_time_decay)[order]), bonus=to_all(A(L0_attn_time_faaaa)[order]),
        ln_affine=to_all(np.stack([A(L0_attn_ln_g), A(L0_attn_ln_b)])),
        gap=np.maximum(query - key - 1, 0).astype(np.float32), later=(query > key).astype(np.float32),
        even_odd=np.stack([np.arange(P) // DH % 2 == e for e in range(2)], 1).astype(np.float32),
        expert_no=to_all(np.arange(NE, dtype=np.float32)))
    nc = bacc.Bacc("TRN2", target_bir_lowering=False, num_devices=1)
    arrays = {k: np.ascontiguousarray(v) for k, v in ins.items()}
    args = {k: nc.dram_tensor(k, v.shape, mybir.dt.from_np(v.dtype), kind="ExternalInput").ap() for k, v in arrays.items()}
    args["out"] = nc.dram_tensor("out", [NSEQ, T, D], mybir.dt.float32, kind="ExternalOutput").ap()
    tower(nc, **args)
    return run_bass_kernel_spmd(nc, [arrays], core_ids=[0]).results[0]["out"]
```

```python
import concourse.bass as bass
from concourse import mybir
from contextlib import ExitStack

L, D, DK, FF = 4, 256, 16, 1024
NSEQ, T = 16, 128
V = 8000
P = 128
KT = D // P
MT = FF // P
CHUNK = 4
CT = CHUNK * T
NCH = NSEQ // CHUNK
BN_EPS = 1e-3
QROW, KROW, VROW = 0, 32, 64
QKVROWS = 96
STACK = 96
RING = 4
NH = 16
DH = D // NH
LN_EPS = 1e-5
GN_EPS = 1e-5 * 64
RATE_MAX = 200.0
NE, TOPK = 8, 2
TOP_EPS = 1e-6
QUAD = 4
WCOLS = KT * P + D


def tower(nc, ids, emb, pes, w_ffn, w_qkv, w_o, bn_raw, qkv_bias, ff_bias, ident_in, w_exp, w_mix, w_router,
          maa_in, decay, bonus, ln_affine, gap, later, even_odd, expert_no, out):
    fp32, fp32r = mybir.dt.float32, mybir.dt.float32r
    keep = ExitStack()
    with keep:
        def lasting(name, shape, dt=fp32):
            return keep.enter_context(nc.sbuf_tensor(name, shape, dt))

        h = lasting("h", [P, NSEQ, D])
        ident = lasting("ident", [P, P])
        mixw = [lasting(f"mixw_{part}", [P, KT, 5 * D], fp32r) for part in ("hi", "lo")]
        decays = lasting("decays", [P, NH, T])
        hnT = lasting("hnT", [P, KT, CHUNK, T + 1])
        maa = lasting("maa", [P, 4, KT])
        bank = [keep.enter_context(nc.psum_tensor(f"bank{i}", [P, 512], fp32)) for i in range(8)]
        transformer(nc, bank, h, ident, mixw, decays, hnT, maa, ids, emb, pes, w_ffn, w_qkv, w_o, bn_raw, qkv_bias,
                    ff_bias, ident_in, w_mix, maa_in, decay, bonus, gap, later)
        mixer_and_experts(nc, bank, h, ident, mixw, decays, hnT, maa, w_exp, w_router, ln_affine, even_odd, expert_no, out)


def three(nc, out_, w, x, first, last):
    (wh, wl), (xh, xl) = w, x
    nc.tensor.matmul(out_, wh, xh, start=first, stop=False)
    nc.tensor.matmul(out_, wh, xl, start=False, stop=False)
    return nc.tensor.matmul(out_, wl, xh, start=False, stop=last)


def transformer(nc, bank, h, ident, mixw, decays, hnT, maa, ids, emb, pes, w_ffn, w_qkv, w_o, bn_raw, qkv_bias,
                ff_bias, ident_in, w_mix, maa_in, decay, bonus, gap, later):
    fp32, fp32r, i32 = mybir.dt.float32, mybir.dt.float32r, mybir.dt.int32
    ALU, ACT, AX = mybir.AluOpType, mybir.ActivationFunctionType, mybir.AxisListType

    ctx = ExitStack()
    with ctx:
        def sb(name, shape, dt=fp32):
            return ctx.enter_context(nc.sbuf_tensor(name, shape, dt))

        def sem(name):
            return ctx.enter_context(nc.semaphore(name))

        ids_sb = sb("ids_sb", [P, NSEQ], i32)
        id_wrap = sb("id_wrap", [P, NSEQ], i32)
        id_row = sb("id_row", [P, NSEQ], i32)
        tok = h
        mixw_raw = h[:, NSEQ - 10:, :].rearrange("p n d -> p (n d)").rearrange("p (k n) -> p k n", k=KT)
        pes_sb = sb("pes_sb", [P, 1])

        xT = sb("xT", [P, KT, NSEQ * T])
        w_raw = sb("w_raw", [P, MT, WCOLS])
        w_hi = sb("w_hi", [P, MT, WCOLS], fp32r)
        w_lo = sb("w_lo", [P, MT, WCOLS], fp32r)
        qkv_all = sb("qkv_all", [P, L, KT * QKVROWS])
        qkv_w = sb("qkv_w", [P, KT * QKVROWS])
        wo_all = sb("wo_all", [STACK, L, D])
        wo_w = sb("wo_w", [STACK, D], fp32r)
        raw = sb("raw", [P, 5, 2, L, KT])
        norm_all = sb("norm_all", [P, 2, L, 2, KT])
        norm_tmp = sb("norm_tmp", [P, 2, L, KT])
        minus_half = sb("minus_half", [P, 2 * L * KT])
        qkvb_all = sb("qkvb_all", [QKVROWS, L])
        ffb_all = sb("ffb_all", [P, L, MT])
        qkvb = sb("qkvb", [QKVROWS, 1])
        ffb = sb("ffb", [P, MT])
        bn1 = sb("bn1", [P, 2, KT])
        bn2 = sb("bn2", [P, 2, KT])

        qT = sb("qT", [DK, CT])
        kT = sb("kT", [DK, CT])
        vT = sb("vT", [DK, CT])
        vtok = sb("vtok", [P, CHUNK, STACK])
        smax = sb("smax", [P, CHUNK])
        nbias = sb("nbias", [P, CHUNK])
        ssum = sb("ssum", [P, CHUNK])
        rsum = sb("rsum", [P, CHUNK])
        prob = sb("prob", [P, CHUNK, T])
        probT = sb("probT", [P, CHUNK, T])
        headT = sb("headT", [STACK, CT], fp32r)
        z1 = sb("z1", [P, KT, CT])
        z2 = sb("z2", [P, KT, CT])
        x1 = sb("x1", [P, 2, KT, CT])
        x1_hi = sb("x1_hi", [P, 2, KT, CT], fp32r)
        x1_lo = sb("x1_lo", [P, 2, KT, CT], fp32r)
        hid = sb("hid", [P, 2, CT])
        hid_hi = sb("hid_hi", [P, RING, CT], fp32r)
        hid_lo = sb("hid_lo", [P, RING, CT], fp32r)

        H = [bank[0], bank[1]]
        Y = [bank[2], bank[3]]
        A = bank[4]
        S = bank[5]
        O = [bank[6], bank[7]]

        s_ids, s_pes, s_ident, s_bn, s_ffb_in = sem("s_ids"), sem("s_pes"), sem("s_ident"), sem("s_bn"), sem("s_ffb_in")
        s_maa = sem("s_maa")
        s_attn_in, s_wo_in, s_wl = sem("s_attn_in"), sem("s_wo_in"), sem("s_wl")
        s_gather = [sem(f"s_gather{c}") for c in range(NCH)]
        s_idx, s_pre, s_emb = sem("s_idx"), sem("s_pre"), sem("s_emb")
        s_w_lo, s_attw, s_attv, s_ffb, s_bn2 = sem("s_w_lo"), sem("s_attw"), sem("s_attv"), sem("s_ffb"), sem("s_bn2")
        s_q, s_v, s_vtok, s_max, s_nb, s_rs, s_prob = (sem("s_q"), sem("s_v"), sem("s_vtok"), sem("s_max"),
                                                       sem("s_nb"), sem("s_rs"), sem("s_prob"))
        s_head, s_z1, s_x1lo, s_hlo, s_z2 = sem("s_head"), sem("s_z1"), sem("s_x1lo"), sem("s_hlo"), sem("s_z2")
        s_w_hi, s_k, s_exp, s_pT, s_x1, s_x1hi = (sem("s_w_hi"), sem("s_k"), sem("s_exp"), sem("s_pT"),
                                                  sem("s_x1"), sem("s_x1hi"))
        s_relu, s_hhi, s_x = sem("s_relu"), sem("s_hhi"), sem("s_x")
        s_eT, s_qkv, s_vt, s_sc, s_pt, s_pv, s_wo = (sem("s_eT"), sem("s_qkv"), sem("s_vt"), sem("s_sc"),
                                                     sem("s_pt"), sem("s_pv"), sem("s_wo"))
        s_h, s_y = sem("s_h"), sem("s_y")
        s_dec, s_rate, s_decay, s_masked = sem("s_dec"), sem("s_rate"), sem("s_decay"), sem("s_masked")
        s_mixw, s_mixw_hi, s_mixw_lo, s_hturn, s_hout = (sem("s_mixw"), sem("s_mixw_hi"), sem("s_mixw_lo"), sem("s_hturn"),
                                                         sem("s_hout"))
        s_head_hi, s_wo_hi, s_zero = sem("s_head_hi"), sem("s_wo_hi"), sem("s_zero")
        n_stats, n_mean, n_var, n_root, n_bias, n_out, n_turned, n_taken = [
            sem(n) for n in ("n_stats", "n_mean", "n_var", "n_root", "n_bias", "n_out", "n_turned", "n_taken")]
        stats0 = sb("stats0", [P, CHUNK, 6])
        mv0 = sb("mv0", [P, CHUNK, 2])
        var0 = sb("var0", [P, CHUNK])
        rstd0 = sb("rstd0", [P, CHUNK])
        bias0 = sb("bias0", [P, CHUNK])
        hn0 = sb("hn0", [P, CHUNK, D])
        eps0 = sb("eps0", [P, CHUNK])
        s_pow = sem("s_pow")
        rate = sb("rate", [P, NH])
        bonus_sb = sb("bonus_sb", [P, NH])
        gap_sb = sb("gap_sb", [P, T])
        later_sb = sb("later_sb", [P, T])
        CREDIT = {s_relu: 2, s_hlo: 2, s_y: RING, s_z2: KT}

        def after(s, n):
            return n + CREDIT.get(s, 0)

        def wait_after(eng, s, n):
            if not (isinstance(n, int) and after(s, n) <= 0):
                eng.wait_ge(s, after(s, n))

        def following(l, c):
            return (l, c + 1) if c < NCH - 1 else (l + 1, 0)

        block = ctx.enter_context(nc.Block())

        @block.sync
        def _(sp):
            sp.dma_start(ids_sb[:], ids).then_inc(s_ids, 16)
            sp.dma_start(pes_sb[:], pes).then_inc(s_pes, 16)
            sp.dma_start(qkv_all[:], w_qkv).then_inc(s_attn_in, 16)
            sp.dma_start(qkvb_all[:], qkv_bias).then_inc(s_attn_in, 16)
            sp.dma_start(wo_all[:], w_o).then_inc(s_wo_in, 16)
            sp.wait_ge(s_gather[1], 16 * CHUNK)
            sp.dma_start(w_raw[:], w_ffn[0]).then_inc(s_wl, 16)
            for dst, src in ((rate, decay), (bonus_sb, bonus), (gap_sb, gap), (later_sb, later)):
                sp.dma_start(dst[:], src).then_inc(s_dec, 16)
            sp.wait_ge(s_eT, NCH)
            sp.dma_start(mixw_raw, w_mix).then_inc(s_mixw, 16)
            sp.dma_start(maa[:], maa_in).then_inc(s_maa, 16)
            sp.wait_ge(s_maa, 16)
            with sp.Fori(0, L - 1) as l:
                sp.wait_ge(s_w_lo, MT * l + MT)
                sp.dma_start(w_raw[:], w_ffn[bass.ds(l + 1, 1), :, :, :]).then_inc(s_wl, 16)

        @block.gpsimd
        def _(pool):
            pool.wait_ge(s_idx, 3)
            for n in range(NSEQ):
                if n == 3 * CHUNK:
                    pool.wait_ge(s_pre, 2)
                    flat = norm_tmp[:].rearrange("p a l k -> p (a l k)")
                    nc.gpsimd.tensor_tensor(flat, flat, minus_half[:], ALU.pow).then_inc(s_pow, 1)
                pool.indirect_dma_start(tok[:, n, :], None, emb,
                                        bass.IndirectOffsetOnAxis(ap=id_row[:, n:n + 1], axis=0)).then_inc(s_gather[n // CHUNK], 16)

            pool.memset(eps0[:], LN_EPS).then_inc(n_var, 1)
            pool.wait_ge(n_var, 1)
            pool.wait_ge(n_mean, 1)
            nc.gpsimd.tensor_tensor(var0[:], mv0[:, :, 1], eps0[:], ALU.add).then_inc(n_var, 1)
            pool.wait_ge(n_var, 2)
            nc.gpsimd.tensor_tensor(rstd0[:], var0[:], minus_half[:, 0:CHUNK], ALU.pow).then_inc(n_root, 1)

        @block.tensor
        def _(pe):
            def qkv(l, c):
                a = NCH * l + c
                pe.wait_ge(s_attw, l + 1)
                pe.wait_ge(s_x, KT * (a + 1))
                wait_after(pe, s_pT, a)
                for kt in range(KT):
                    last = nc.tensor.matmul(A[0:QKVROWS, :], qkv_w[:, kt * QKVROWS:(kt + 1) * QKVROWS],
                                            xT[:, kt, c * CT:(c + 1) * CT], start=kt == 0, stop=kt == KT - 1)
                last.then_inc(s_qkv, 1)

            def scores(l, c):
                a = NCH * l + c
                pe.wait_ge(s_v, a + 1)
                pe.wait_ge(s_k, a + 1)
                wait_after(pe, s_head, a)
                pe.wait_ge(s_q, a + 1)
                for n in range(CHUNK):
                    last = nc.tensor.matmul(S[:, n * T:(n + 1) * T], qT[:, n * T:(n + 1) * T],
                                            kT[:, n * T:(n + 1) * T], start=True, stop=True)
                last.then_inc(s_sc, 1)
                for n in range(CHUNK):
                    last = nc.tensor.transpose(A[:, n * DK:(n + 1) * DK], vT[:, n * T:(n + 1) * T],
                                               ident[0:DK, 0:DK])
                last.then_inc(s_vt, 1)

            def turn_probs(l, c):
                pe.wait_ge(s_vtok, NCH * l + c + 1)
                pe.wait_ge(s_prob, NCH * l + c + 1)
                for n in range(CHUNK):
                    last = nc.tensor.transpose(A[:, n * T:(n + 1) * T], prob[:, n, :], ident[:])
                last.then_inc(s_pt, 1)

            def head(l, c):
                a = NCH * l + c
                pe.wait_ge(s_pT, a + 1)
                for n in range(CHUNK):
                    last = nc.tensor.matmul(S[0:STACK, n * T:(n + 1) * T], vtok[:, n, :], probT[:, n, :],
                                            start=True, stop=True)
                last.then_inc(s_pv, 1)

            def project(l, c):
                pe.wait_ge(s_attv, l + 1)
                pe.wait_ge(s_head, NCH * l + c + 1)
                wait_after(pe, s_z1, KT * (NCH * l + c))
                if isinstance(l, int) and l == L - 1 and c >= 3:
                    pe.wait_ge(s_hout, KT * (c - 2))
                for kt in range(KT):
                    last = nc.tensor.matmul(O[kt][:], wo_w[:, kt * P:(kt + 1) * P], headT[:], start=True, stop=True)
                last.then_inc(s_wo, 1)

            def hidden(l, c, m):
                s = NCH * l + c
                if c == 0:
                    pe.wait_ge(s_w_lo, MT * l + m + 1)
                pe.wait_ge(s_relu, after(s_relu, MT * s + m - 1))
                for kt in range(KT):
                    if m == 0:
                        pe.wait_ge(s_x1lo, KT * s + kt + 1)
                    w = [t[:, m, kt * P:(kt + 1) * P] for t in (w_hi, w_lo)]
                    last = three(nc, H[m % 2][:], w, [t[:, c % 2, kt, :] for t in (x1_hi, x1_lo)], kt == 0, kt == KT - 1)
                last.then_inc(s_h, 1)

            def second(l, c, m):
                s = NCH * l + c
                pe.wait_ge(s_hlo, after(s_hlo, MT * s + m + 1))
                if m == 0:
                    pe.wait_ge(s_z2, after(s_z2, KT * s))
                for kt in range(KT):
                    w = [t[:, m, KT * P + kt * P:KT * P + (kt + 1) * P] for t in (w_hi, w_lo)]
                    last = three(nc, Y[kt][:], w, [t[:, m % RING, :] for t in (hid_hi, hid_lo)], m == 0, m == MT - 1)
                last.then_inc(s_y, 1)

            def turn_out(c):
                pe.wait_ge(s_x, KT * (NCH * L + c + 1))
                pe.wait_ge(s_z1, KT * min(NCH * (L - 1) + c + 3, NCH * L))
                if c >= 1:
                    pe.wait_ge(s_hout, KT * c)
                for n in range(CHUNK):
                    for kt in range(KT):
                        at = n % 2 * D + kt * P
                        last = nc.tensor.transpose(O[n // 2][:, at:at + P], xT[:, kt, c * CT + n * T:c * CT + (n + 1) * T], ident[:])
                    if n % 2:
                        last.then_inc(s_hturn, 1)

            def step(l, c, attend=True):
                nxt = following(l, c)
                for m in range(MT):
                    if attend and m == 0:
                        qkv(*nxt)
                    if attend and m == 5:
                        turn_probs(*nxt)
                    if attend and m == 6:
                        head(*nxt)
                    if attend and m == 7:
                        project(*nxt)
                    hidden(l, c, m)
                    if attend and m == 1:
                        scores(*nxt)
                    if m >= 2:
                        second(l, c, m - 2)
                second(l, c, MT - 2)
                second(l, c, MT - 1)

            pe.sem_inc(s_y, CREDIT[s_y])

            def turn_in(c):
                pe.wait_ge(s_emb, c + 1)
                if c >= 2:
                    pe.wait_ge(s_x, KT * (c - 1))
                for n in range(CHUNK):
                    for kt in range(KT):
                        last = nc.tensor.transpose((O, Y)[c % 2][kt][:, n * T:(n + 1) * T],
                                                   tok[:, c * CHUNK + n, kt * P:(kt + 1) * P], ident[:])
                last.then_inc(s_eT, 1)

            pe.wait_ge(s_ident, 16)
            turn_in(0)
            turn_in(1)
            qkv(0, 0)
            scores(0, 0)
            turn_in(2)
            turn_probs(0, 0)
            turn_in(3)
            head(0, 0)
            pe.wait_ge(s_x, KT * NCH)
            project(0, 0)
            with pe.Fori(0, L - 1) as l:
                for c in range(NCH):
                    step(l, c)
            for c in range(NCH):
                step(L - 1, c, attend=c < NCH - 1)
                if c == NCH - 1:
                    pe.wait_ge(n_out, CHUNK)
                    for n in range(CHUNK):
                        for kt in range(KT):
                            last = nc.tensor.transpose((A, S)[kt][:, n * T:(n + 1) * T], hn0[:, n, kt * P:(kt + 1) * P], ident[:])
                    last.then_inc(n_turned, 1)
                if c >= 1:
                    turn_out(c - 1)
            turn_out(NCH - 1)

        @block.scalar
        def _(act):
            def turn_k(l, c):
                act.wait_ge(s_qkv, NCH * l + c + 1)
                nc.scalar.activation(kT[:], A[KROW:KROW + DK, :], ACT.Identity,
                                     bias=qkvb[KROW:KROW + DK, :]).then_inc(s_k, 1)

            def exps(l, c):
                act.wait_ge(s_nb, NCH * l + c + 1)
                for n in range(CHUNK):
                    last = nc.scalar.activation(prob[:, n, :], S[:, n * T:(n + 1) * T], ACT.Exp, bias=nbias[:, n:n + 1],
                                                scale=DK ** -0.5, accum_out=ssum[:, n:n + 1])
                last.then_inc(s_exp, 1)

            def copy_probT(l, c):
                act.wait_ge(s_pt, NCH * l + c + 1)
                nc.scalar.copy(probT[:].rearrange("p n t -> p (n t)"), A[:]).then_inc(s_pT, 1)

            def norm1(l, c):
                a = NCH * l + c
                for kt in range(KT):
                    act.wait_ge(s_z1, KT * a + kt + 1)
                    nc.scalar.activation(x1[:, c % 2, kt, :], z1[:, kt, :], ACT.Identity, bias=bn1[:, 1, kt:kt + 1],
                                         scale=bn1[:, 0, kt:kt + 1]).then_inc(s_x1, 1)
                    act.wait_ge(s_x1, KT * a + kt + 1)
                    nc.scalar.copy(x1_hi[:, c % 2, kt, :], x1[:, c % 2, kt, :]).then_inc(s_x1hi, 1)

            def relu(l, c, m):
                n = MT * (NCH * l + c) + m
                if c == 0 and m == 0:
                    act.wait_ge(s_ffb, l + 1)
                act.wait_ge(s_h, n + 1)
                act.wait_ge(s_hlo, after(s_hlo, n - 1))
                nc.scalar.activation(hid[:, m % 2, :], H[m % 2][:], ACT.Relu, bias=ffb[:, m:m + 1]).then_inc(s_relu, 1)
                act.wait_ge(s_relu, after(s_relu, n + 1))
                act.wait_ge(s_y, after(s_y, n + 1 - RING))
                nc.scalar.copy(hid_hi[:, m % RING, :], hid[:, m % 2, :]).then_inc(s_hhi, 1)

            def norm2(l, c):
                for kt in range(KT):
                    if c == 0:
                        act.wait_ge(s_bn2, l + 1)
                    act.wait_ge(s_z2, after(s_z2, KT * (NCH * l + c) + kt + 1))
                    nc.scalar.activation(xT[:, kt, c * CT:(c + 1) * CT], z2[:, kt, :], ACT.Identity,
                                         bias=bn2[:, 1, kt:kt + 1], scale=bn2[:, 0, kt:kt + 1]).then_inc(s_x, 1)

            def split_high(l, m):
                act.wait_ge(s_wl, 16 * l + 16)
                if not (isinstance(l, int) and l == 0):
                    act.wait_ge(s_y, after(s_y, MT * (NCH * l - 1) + m + 1))
                nc.scalar.copy(w_hi[:, m, :], w_raw[:, m, :]).then_inc(s_w_hi, 1)

            def step(l, c, attend=True, refresh=True, extra=None):
                nxt = following(l, c)
                refresh = refresh and c == NCH - 1
                for m in range(MT):
                    if attend and m == 0:
                        turn_k(*nxt)
                    if attend and m == 5:
                        copy_probT(*nxt)
                    relu(l, c, m)
                    if attend and m == 2:
                        exps(*nxt)
                    if attend and m == 7:
                        norm1(*nxt)
                    if extra:
                        extra(c, m)
                    if c == 0 and m < 3:
                        split_high(l, MT - 3 + m)
                    if refresh and m >= 3:
                        split_high(l + 1, m - 3)
                norm2(l, c)

            def mixw_high(i):
                if i == 0:
                    act.wait_ge(s_mixw, 16)
                cols = slice(i * D, (i + 1) * D)
                nc.scalar.copy(mixw[0][:, :, cols], mixw_raw[:, :, cols]).then_inc(s_mixw_hi, 1)

            def decay_rate():
                act.wait_ge(s_dec, 4 * 16)
                nc.scalar.activation(rate[:], rate[:], ACT.Exp).then_inc(s_rate, 1)

            def decay_row(h):
                if h == 0:
                    act.wait_ge(s_rate, 2)
                nc.scalar.activation(decays[:, h, :], gap_sb[:], ACT.Exp, scale=rate[:, h:h + 1]).then_inc(s_decay, 1)

            def take_x(c):
                act.wait_ge(s_eT, c + 1)
                for kt in range(KT):
                    nc.scalar.copy(xT[:, kt, c * CT:(c + 1) * CT], (O, Y)[c % 2][kt][:]).then_inc(s_x, 1)

            act.dma_start(ident[:], ident_in).then_inc(s_ident, 16)
            act.dma_start(raw[:], bn_raw).then_inc(s_bn, 16)
            act.dma_start(ffb_all[:], ff_bias).then_inc(s_ffb_in, 16)
            act.sem_inc(s_relu, CREDIT[s_relu])
            take_x(0)
            take_x(1)
            turn_k(0, 0)
            exps(0, 0)
            take_x(2)
            copy_probT(0, 0)
            take_x(3)
            split_high(0, 0)
            split_high(0, 1)
            norm1(0, 0)
            for m in range(2, MT - 3):
                split_high(0, m)
            with act.Fori(0, L - 1) as l:
                for c in range(NCH):
                    step(l, c)
            decay_rate()

            def extra(c, m):
                if c == NCH - 1 and m % 2 == 0:
                    n = m // 2
                    act.wait_ge(n_bias, 1)
                    nc.scalar.activation(hn0[:, n, :], h[:, n, :], ACT.Identity, bias=bias0[:, n:n + 1],
                                         scale=rstd0[:, n:n + 1]).then_inc(n_out, 1)
                if m % 2:
                    decay_row(c * (MT // 2) + m // 2)
                elif 3 * c + m // 2 < 5 and m < 6:
                    mixw_high(3 * c + m // 2)
            for c in range(NCH):
                step(L - 1, c, attend=c < NCH - 1, refresh=False, extra=extra)
            act.wait_ge(n_turned, 1)
            for kt in range(KT):
                nc.scalar.copy(hnT[:, kt, :, 1:T + 1], (A, S)[kt][:].rearrange("p (n t) -> p n t", n=CHUNK)).then_inc(n_taken, 1)
            act.wait_ge(n_taken, KT)

        @block.vector
        def _(dve):
            def turn_qv(l, c):
                a = NCH * l + c
                dve.wait_ge(s_qkv, a + 1)
                nc.vector.tensor_scalar(qT[:], A[QROW:QROW + DK, :], qkvb[QROW:QROW + DK, :], None, ALU.add).then_inc(s_q, 1)
                nc.vector.tensor_scalar(vT[:], A[VROW:VROW + DK, :], qkvb[VROW:VROW + DK, :], None, ALU.add).then_inc(s_v, 1)

            def softmax_max(l, c):
                a = NCH * l + c
                dve.wait_ge(s_sc, a + 1)
                nc.vector.reduce_max(smax[:], S[:].rearrange("p (n t) -> p n t", n=CHUNK), AX.X).then_inc(s_max, 1)
                dve.wait_ge(s_max, a + 1)
                nc.vector.tensor_scalar(nbias[:], smax[:], -DK ** -0.5, None, ALU.mult).then_inc(s_nb, 1)
                dve.wait_ge(s_vt, a + 1)
                nc.vector.tensor_copy(vtok[:].rearrange("p n (j d) -> p n j d", j=3)[:, :, :, 0:DK],
                                      A[:, 0:CHUNK * DK].rearrange("p (n d) -> p n d", n=CHUNK).unsqueeze(2)
                                      .to_broadcast([P, CHUNK, 3, DK])).then_inc(s_vtok, 1)

            def softmax_norm(l, c):
                a = NCH * l + c
                dve.wait_ge(s_exp, a + 1)
                nc.vector.reciprocal(rsum[:], ssum[:]).then_inc(s_rs, 1)
                dve.wait_ge(s_rs, a + 1)
                nc.vector.tensor_tensor(prob[:], prob[:], rsum[:].unsqueeze(2).to_broadcast([P, CHUNK, T]),
                                        ALU.mult).then_inc(s_prob, 1)

            def turn_head(l, c):
                dve.wait_ge(s_pv, NCH * l + c + 1)
                nc.vector.tensor_copy(headT[:], S[0:STACK, :]).then_inc(s_head_hi, 1)
                dve.wait_ge(s_head_hi, NCH * l + c + 1)
                low = headT[32:32 + DK, :]
                nc.vector.tensor_tensor(low, S[32:32 + DK, :], low.bitcast(fp32), ALU.subtract).then_inc(s_head, 1)

            def residual1(l, c):
                a = NCH * l + c
                dve.wait_ge(s_wo, a + 1)
                wait_after(dve, s_x1, KT * a)
                for kt in range(KT):
                    nc.vector.tensor_tensor(z1[:, kt, :], O[kt][:], xT[:, kt, c * CT:(c + 1) * CT], ALU.add).then_inc(s_z1, 1)

            def split_x1(l, c):
                for kt in range(KT):
                    dve.wait_ge(s_x1hi, KT * (NCH * l + c) + kt + 1)
                    nc.vector.tensor_tensor(x1_lo[:, c % 2, kt, :], x1[:, c % 2, kt, :], x1_hi[:, c % 2, kt, :].bitcast(fp32),
                                            ALU.subtract).then_inc(s_x1lo, 1)

            def split_hidden(l, c, m):
                dve.wait_ge(s_hhi, MT * (NCH * l + c) + m + 1)
                nc.vector.tensor_tensor(hid_lo[:, m % RING, :], hid[:, m % 2, :], hid_hi[:, m % RING, :].bitcast(fp32),
                                        ALU.subtract).then_inc(s_hlo, 1)

            def residual2(l, c):
                s = NCH * l + c
                dve.wait_ge(s_y, after(s_y, MT * (s + 1)))
                dve.wait_ge(s_x, KT * (NCH + s))
                for kt in range(KT):
                    nc.vector.tensor_tensor(z2[:, kt, :], Y[kt][:], x1[:, c % 2, kt, :], ALU.add).then_inc(s_z2, 1)

            def split_low(l, m):
                dve.wait_ge(s_w_hi, MT * l + m + 1)
                nc.vector.tensor_tensor(w_lo[:, m, :], w_raw[:, m, :], w_hi[:, m, :].bitcast(fp32),
                                        ALU.subtract).then_inc(s_w_lo, 1)

            def layer(t, l):
                return t[:, bass.ds(l, 1), :]

            def place_qkv(l):
                if not isinstance(l, int):
                    dve.wait_ge(s_qkv, NCH * l)
                    dve.wait_ge(s_k, NCH * l)
                    dve.wait_ge(s_v, NCH * l)
                nc.vector.tensor_copy(qkvb[:], qkvb_all[:, bass.ds(l, 1)])
                nc.vector.tensor_copy(qkv_w[:].unsqueeze(1), layer(qkv_all, l)).then_inc(s_attw, 1)

            def place_attention(l):
                if not isinstance(l, int):
                    dve.wait_ge(s_x1, KT * NCH * l)
                nc.vector.tensor_copy(wo_w[:].unsqueeze(1), layer(wo_all, l)).then_inc(s_wo_hi, 1)
                dve.wait_ge(s_wo_hi, l + 1)
                low = wo_w[64:64 + DK, :]
                nc.vector.tensor_tensor(low.unsqueeze(1), wo_all[64:64 + DK, bass.ds(l, 1), :], low.bitcast(fp32).unsqueeze(1), ALU.subtract)
                nc.vector.tensor_copy(bn1[:].rearrange("p k t -> p (k t)").unsqueeze(1), layer(norm1_all, l)).then_inc(s_attv, 1)

            def place_ffb(l):
                if not isinstance(l, int):
                    dve.wait_ge(s_relu, after(s_relu, MT * NCH * l))
                nc.vector.tensor_copy(ffb[:].unsqueeze(1), layer(ffb_all, l)).then_inc(s_ffb, 1)

            def place_bn2(l):
                dve.wait_ge(s_x, KT * NCH * (l + 1))
                nc.vector.tensor_copy(bn2[:].rearrange("p k t -> p (k t)").unsqueeze(1), layer(norm2_all, l)).then_inc(s_bn2, 1)

            def mixw_low(i):
                dve.wait_ge(s_mixw_hi, i + 1)
                hi, lo = [t[:, :, i * D:(i + 1) * D] for t in mixw]
                nc.vector.tensor_tensor(lo, mixw_raw[:, :, i * D:(i + 1) * D], hi.bitcast(fp32), ALU.subtract).then_inc(s_mixw_lo, 1)

            def take_h(c):
                if c == 1:
                    dve.wait_ge(s_mixw_lo, 5)
                for i in range(2):
                    dve.wait_ge(s_hturn, 2 * c + i + 1)
                    nc.vector.tensor_copy(h[:, c * CHUNK + 2 * i:c * CHUNK + 2 * i + 2, :].rearrange("p n d -> p (n d)"),
                                          O[i][:]).then_inc(s_hout, 1)

            def decay_mask(i):
                dve.wait_ge(s_decay, i + 1)
                nc.vector.tensor_tensor(decays[:, i, :], decays[:, i, :], later_sb[:], ALU.mult).then_inc(s_masked, 1)
                dve.wait_ge(s_masked, i + 1)
                nc.vector.scalar_tensor_tensor(decays[:, i, :], ident[:], bonus_sb[:, i:i + 1], decays[:, i, :],
                                               ALU.mult, ALU.add)

            norm1_all = norm_all[:, 0, :, :, :].rearrange("p l k t -> p l (k t)")
            norm2_all = norm_all[:, 1, :, :, :].rearrange("p l k t -> p l (k t)")

            def step(l, c, attend=True, refresh=True, extra=None):
                nxt = following(l, c)
                if refresh and c == NCH - 1:
                    place_attention(l + 1)
                for m in range(MT):
                    if attend and m == 0:
                        turn_qv(*nxt)
                    if c == 0 and m == 2:
                        place_bn2(l)
                    if attend and m == 4:
                        softmax_norm(*nxt)
                    if attend and m == 6:
                        turn_head(*nxt)
                    if attend and m == 7:
                        residual1(*nxt)
                    split_hidden(l, c, m)
                    if extra:
                        extra(c, m)
                    if attend and m == 1:
                        softmax_max(*nxt)
                    if c == 0 and m < 3:
                        split_low(l, MT - 3 + m)
                    if refresh and c == NCH - 1 and m >= 3:
                        split_low(l + 1, m - 3)
                if attend:
                    split_x1(*nxt)
                if refresh and c == NCH - 1:
                    place_ffb(l + 1)
                if refresh and c == NCH - 2:
                    place_qkv(l + 1)
                residual2(l, c)

            for s in (s_hlo, s_z2):
                dve.sem_inc(s, CREDIT[s])
            nc.vector.memset(hnT[:, :, :, 0:1], 0.0)
            nc.vector.memset(vtok[:], 0.0).then_inc(s_zero, 1)
            dve.wait_ge(s_zero, 1)
            dve.wait_ge(s_ids, 16)
            nc.vector.tensor_scalar(id_wrap[:], ids_sb[:], 0, V, ALU.is_lt, ALU.mult).then_inc(s_idx, 1)
            dve.wait_ge(s_idx, 1)
            nc.vector.tensor_tensor(id_wrap[:], id_wrap[:], ids_sb[:], ALU.add).then_inc(s_idx, 1)
            dve.wait_ge(s_idx, 2)
            nc.vector.tensor_scalar(id_row[:], id_wrap[:], 0, V - 1, ALU.max, ALU.min).then_inc(s_idx, 1)

            def add_position(c):
                dve.wait_ge(s_gather[c], 16 * CHUNK)
                rows = tok[:, c * CHUNK:(c + 1) * CHUNK, :]
                nc.vector.tensor_scalar(rows, rows, pes_sb[:, 0:1], None, ALU.add).then_inc(s_emb, 1)

            def batch_norms():
                dve.wait_ge(s_pow, 1)
                for w in range(2):
                    nc.vector.tensor_tensor(norm_all[:, w, :, 0, :], raw[:, 0, w], norm_tmp[:, w], ALU.mult)
                nc.vector.tensor_tensor(raw[:, 4], raw[:, 4], raw[:, 2], ALU.subtract).then_inc(s_pre, 1)
                dve.wait_ge(s_pre, 3)
                for w in range(2):
                    last = nc.vector.tensor_tensor(raw[:, 4, w], raw[:, 4, w], norm_all[:, w, :, 0, :], ALU.mult)
                last.then_inc(s_pre, 1)
                dve.wait_ge(s_pre, 4)
                for w in range(2):
                    last = nc.vector.tensor_tensor(norm_all[:, w, :, 1, :], raw[:, 4, w], raw[:, 1, w], ALU.add)
                last.then_inc(s_pre, 1)
                dve.wait_ge(s_pre, 5)

            dve.wait_ge(s_bn, 16)
            nc.vector.memset(minus_half[:], -0.5).then_inc(s_pre, 1)
            nc.vector.tensor_scalar(norm_tmp[:], raw[:, 3], BN_EPS, None, ALU.add).then_inc(s_pre, 1)
            dve.wait_ge(s_pes, 16)
            add_position(0)
            add_position(1)
            dve.wait_ge(s_attn_in, 2 * 16)
            place_qkv(0)
            turn_qv(0, 0)
            softmax_max(0, 0)
            add_position(2)
            softmax_norm(0, 0)
            add_position(3)
            batch_norms()
            dve.wait_ge(s_wo_in, 16)
            place_attention(0)
            dve.wait_ge(s_ffb_in, 16)
            place_ffb(0)
            turn_head(0, 0)
            split_low(0, 0)
            residual1(0, 0)
            split_low(0, 1)
            split_x1(0, 0)
            for m in range(2, MT - 3):
                split_low(0, m)
            with dve.Fori(0, L - 1) as l:
                for c in range(NCH):
                    step(l, c)
            dve.wait_ge(s_rate, 1)
            nc.vector.tensor_scalar(rate[:], rate[:], RATE_MAX, -1.0, ALU.min, ALU.mult).then_inc(s_rate, 1)

            def extra(c, m):
                if c == NCH - 2 and m == 2:
                    dve.wait_ge(n_root, 1)
                    nc.vector.scalar_tensor_tensor(bias0[:], mv0[:, :, 0], -1.0, rstd0[:], ALU.mult, ALU.mult).then_inc(n_bias, 1)
                if m % 2:
                    decay_mask(c * (MT // 2) + m // 2)
                elif 3 * c + m // 2 < 5 and m < 6:
                    mixw_low(3 * c + m // 2)
            for c in range(NCH):
                step(L - 1, c, attend=c < NCH - 1, refresh=False, extra=extra)
                if c >= 1:
                    take_h(c - 1)
                if c == 1:
                    dve.wait_ge(s_hout, KT)
                    for n in range(CHUNK):
                        last = nc.vector.bn_stats(stats0[:, n, :], h[:, n, :])
                    last.then_inc(n_stats, 1)
                    dve.wait_ge(n_stats, 1)
                    for n in range(CHUNK):
                        last = nc.vector.bn_aggr(mv0[:, n, :], stats0[:, n, :])
                    last.then_inc(n_mean, 1)
            take_h(NCH - 1)


EVENTS = dict(
    hnT=2, mix_hi=4, r=4, k=2, tanh=4, vg=4, sq=2, yT_hi=2, h2T_hi=2, lgT=1, rexp=1, hn=4, hn2=2,
    hnT_t=2, r_t=2, k_t=2, vg_t=4, s_t=16, y_t=4, yT_t=2, o_t=2, h2T_t=2, lgT_t=1, lg_t=1, moe_t=16,
    st1=4, mv1=4, wide=16, gsum=2, gmean=2, yc=2, gsq=2, yn=4, yg=2,
    xx=2, mix=4, last_lo=1, hn2_v=2, bias1=1, bias2=1, yT_lo=2, h2T_lo=2, h2=2, st2=4, mv2=4, rt=14, acc0=4, moe=32,
    v1=1, rstd1=1, v2=1, rstd2=1, gv=2, grstd=2, mix_lo=3, silu=4, goff=2, gates=2,
)


def mixer_and_experts(nc, bank, h, ident, mixw, decays, hnT, maa, w_exp, w_router, ln_affine, even_odd, expert_no, out):
    fp32, fp32r, u32 = mybir.dt.float32, mybir.dt.float32r, mybir.dt.uint32
    ALU, ACT, AX = mybir.AluOpType, mybir.ActivationFunctionType, mybir.AxisListType
    R, K, VV, G, O = range(5)
    PAIR = 2
    UNITS = CHUNK * NE // 2

    ctx = ExitStack()
    with ctx:
        def sb(name, shape, dt=fp32):
            return ctx.enter_context(nc.sbuf_tensor(name, shape, dt))

        E = {name: ctx.enter_context(nc.semaphore("e_" + name)) for name in EVENTS}
        s_in, s_const, s_halved, s_out, s_exp_in, s_e_hi, s_e_lo, s_router_hi, s_router_lo = [ctx.enter_context(nc.semaphore(n)) for n in (
            "s_in", "s_const", "s_halved", "s_out", "s_exp_in", "s_e_hi", "s_e_lo", "s_router_hi", "s_router_lo")]

        def wait(eng, name, c, k):
            n = EVENTS[name] * c + k
            if not (isinstance(n, int) and n <= 0):
                eng.wait_ge(E[name], n)

        experts = [sb(f"experts_{part}", [P, KT, NE * D], fp32r) for part in ("hi", "lo")]
        router = [sb(f"router_{part}", [P, KT, NE], fp32r) for part in ("hi", "lo")]
        router_raw = sb("router_raw", [P, KT, NE])
        affine = sb("affine", [P, 2, D])
        parity = sb("parity", [P, 2])
        expno = sb("expno", [P, NE])
        minus_half = sb("minus_half2", [P, PAIR * NH])
        ln_eps = sb("ln_eps", [P, CHUNK])
        gn_eps = sb("gn_eps", [P, PAIR * NH])
        held = sb("held", [P, 1])

        stats = sb("stats", [P, 2, CHUNK, 6])
        mv = sb("mv", [P, 2, CHUNK, 2])
        var = sb("var", [P, 2, CHUNK])
        rstd = sb("rstd", [P, 2, CHUNK])
        hn = sb("hn", [P, CHUNK, D])
        xx = sb("xx", [P, KT, CHUNK, T])
        mix_whole = sb("mix_whole", [P, 2, KT, CT])
        mix = [sb(f"mix_{part}", [P, 4, KT, CT], fp32r) for part in ("hi", "lo")]
        r_eo = sb("r_eo", [P, KT, 2, CT])
        kT = sb("kT2", [P, KT, CT])
        vg = sb("vg", [P, CHUNK, 2, D])
        gate = sb("gate", [P, CHUNK, D])
        offs = sb("offs", [P, CHUNK, D])
        weighed = sb("weighed", [P, 2, NH, T])
        experts_raw = weighed[:].rearrange("p b h t -> p (b h t)").rearrange("p (k e) -> p k e", k=KT)
        gsum = sb("gsum", [P, 2, PAIR * NH])
        gmean = sb("gmean", [P, 2, PAIR * NH])
        gvar = sb("gvar", [P, 2, PAIR * NH])
        grstd = sb("grstd", [P, 2, PAIR * NH])
        yc = sb("yc", [P, CHUNK, D])
        yT = [sb(f"yT_{part}", [P, KT, CT], fp32r) for part in ("hi", "lo")]
        hn2 = sb("hn2", [P, CHUNK, D])
        ysq = hn2
        nbias = sb("nbias2", [P, 2, CHUNK])
        h2T = [sb(f"h2T_{part}", [P, KT, CT], fp32r) for part in ("hi", "lo")]
        lgT = sb("lgT", [NE, CT])
        lg = sb("lg", [P, CHUNK, NE])
        lmax = sb("lmax", [P, CHUNK])
        psm = sb("psm", [P, CHUNK, NE])
        psum_ = sb("psum_", [P, CHUNK])
        top = sb("top", [P, CHUNK, NE])
        topi = sb("topi", [P, CHUNK, NE], u32)
        topf = sb("topf", [P, CHUNK, TOPK])
        tsum = sb("tsum", [P, CHUNK])
        wtop = sb("wtop", [P, CHUNK, TOPK])
        wprod = sb("wprod", [P, CHUNK, TOPK])
        ebias = sb("ebias", [P, CHUNK])
        pick = sb("pick", [P, TOPK, CHUNK, NE])
        coef = sb("coef", [P, CHUNK, NE])

        UNITS_BETWEEN = (2, 4, 5, 6, 7, 8, 9, 10, 11, 12, 13, UNITS)
        LATE_UNITS_BETWEEN = (2, 4, 5, 5, 6, 7, 8, 8, 9, 10, 11, UNITS)

        M = [bank[0], bank[1]]
        B = bank[2:8]
        R_BANKS = B[0:2]
        K_BANKS = B[4:6]
        Y_BANKS = B[2:4]
        SC = [B[0], B[1], B[4], B[5]]
        VG = [M[0], M[1], B[2], B[3]]
        LG = M[0]

        def credit(eng, *names):
            for name in names:
                eng.sem_inc(E[name], EVENTS[name])

        def seq(t, n):
            return t[..., n * T:(n + 1) * T]

        def rows(c, n, count=1):
            return h[:, bass.ds(c * CHUNK + n, count), :]

        def of_pair(t, p):
            return t[:, PAIR * p:PAIR * (p + 1), :]

        block = ctx.enter_context(nc.Block())

        @block.sync
        def _(sp):
            for dst, src in ((affine[:], ln_affine), (parity[:], even_odd), (expno[:], expert_no),
                             (router_raw[:], w_router)):
                sp.dma_start(dst, src).then_inc(s_in, 16)
            sp.dma_start(experts_raw, w_exp).then_inc(s_exp_in, 16)

            def store(c):
                for n in range(CHUNK):
                    wait(sp, "moe", c, NE * (n + 1))
                    sp.dma_start(out[bass.ds(c * CHUNK + n, 1), :, :].rearrange("s t d -> (s t) d"),
                                 rows(c, n).rearrange("p n d -> p (n d)")).then_inc(s_out, 16)

            with sp.Fori(0, NCH) as c:
                store(c)
            sp.wait_ge(s_out, 16 * NSEQ)

        @block.gpsimd
        def _(pool):
            def root(c, which):
                w = which - 1
                wait(pool, f"mv{which}", c, CHUNK)
                nc.gpsimd.tensor_tensor(var[:, w, :], mv[:, w, :, 1], ln_eps[:], ALU.add).then_inc(E[f"v{which}"], 1)
                wait(pool, f"v{which}", c, 1)
                nc.gpsimd.tensor_tensor(rstd[:, w, :], var[:, w, :], minus_half[:, 0:CHUNK], ALU.pow).then_inc(E[f"rstd{which}"], 1)

            def gates(c):
                for p in range(2):
                    wait(pool, "vg", c, PAIR * (p + 1))
                    wait(pool, "tanh", c, PAIR * (p + 1))
                    g, t, o = vg[:, PAIR * p:PAIR * (p + 1), 1, :], of_pair(gate, p), of_pair(offs, p)
                    nc.gpsimd.tensor_tensor(o, t, g, ALU.mult).then_inc(E["silu"], 1)
                    wait(pool, "silu", c, 2 * p + 1)
                    nc.gpsimd.tensor_tensor(t, o, g, ALU.add).then_inc(E["silu"], 1)
                    wait(pool, "silu", c, 2 * p + 2)
                    nc.gpsimd.tensor_tensor(o, t, affine[:, 1, :].unsqueeze(1).to_broadcast([P, PAIR, D]), ALU.mult).then_inc(E["goff"], 1)
                    wait(pool, "goff", c, p + 1)
                    nc.gpsimd.tensor_tensor(t, t, affine[:, 0, :].unsqueeze(1).to_broadcast([P, PAIR, D]), ALU.mult).then_inc(E["gates"], 1)

            def group_root(c, p):
                wait(pool, "gsq", c, p + 1)
                nc.gpsimd.tensor_tensor(gvar[:, p, :], gvar[:, p, :], gn_eps[:], ALU.add).then_inc(E["gv"], 1)
                wait(pool, "gv", c, p + 1)
                nc.gpsimd.tensor_tensor(grstd[:, p, :], gvar[:, p, :], minus_half[:], ALU.pow).then_inc(E["grstd"], 1)

            def mix_low(c, i):
                wait(pool, "mix_hi", c, i + 1)
                hi, lo = [t[:, i] for t in mix]
                nc.gpsimd.tensor_tensor(lo, mix_whole[:, i % 2], hi.bitcast(fp32), ALU.subtract).then_inc(E["mix_lo"], 1)

            def step(c, front=True, back=True, more=True):
                if front and more:
                    root(c + 1, 1)
                if back:
                    root(c - 1, 2)
                if front:
                    gates(c)
                    if more:
                        mix_low(c + 1, 0)
                    group_root(c, 0)
                    if more:
                        mix_low(c + 1, 1)
                        mix_low(c + 1, 2)
                    group_root(c, 1)

            pool.memset(ln_eps[:], LN_EPS)
            pool.memset(gn_eps[:], GN_EPS)
            pool.memset(minus_half[:], -0.5).then_inc(s_const, 1)
            pool.wait_ge(s_const, 1)
            credit(pool, "v1", "rstd1")
            for i in range(3):
                mix_low(0, i)
            pool.wait_ge(s_halved, 1)
            step(0, back=False)
            with pool.Fori(1, NCH - 1) as c:
                step(c)
            step(NCH - 1, more=False)
            step(NCH, front=False)

        @block.tensor
        def _(pe):
            def turn_tokens(c, src, ready, banks, done):
                for n in range(CHUNK):
                    if ready:
                        name, base = ready[n * len(ready) // CHUNK]
                        wait(pe, name, c, n + 1 - base)
                    for kt in range(KT):
                        last = nc.tensor.transpose(seq(banks[kt], n), src[:, n, kt * P:(kt + 1) * P], ident[:])
                        if n == CHUNK - 1:
                            last.then_inc(E[done], 1)

            def turn_normed(c):
                wait(pe, "vg", c - 1, 2)
                turn_tokens(c, hn, [("hn", 0)], M, "hnT_t")

            def weights(i, cols):
                return lambda kt: [t[:, kt, i * D + cols.start:i * D + cols.stop] for t in mixw]

            def project_rk(c):
                wait(pe, "wide", c, 0)
                for i, banks, done in ((R, R_BANKS, "r_t"), (K, K_BANKS, "k_t")):
                    wait(pe, "mix_lo", c, i + 1)
                    for mt in range(KT):
                        w = weights(i, slice(mt * P, (mt + 1) * P))
                        for kt in range(KT):
                            last = three(nc, banks[mt][:], w(kt), [t[:, i, kt, :] for t in mix], kt == 0, kt == KT - 1)
                        last.then_inc(E[done], 1)

            def project_vg(c, n):
                if n < 2:
                    wait(pe, "moe", c - 1, 0)
                else:
                    wait(pe, "yc", c, 0)
                for j, i in enumerate((VV, G)):
                    wait(pe, *(("last_lo", c, 1) if i == G else ("mix_lo", c, i + 1)))
                    for kt in range(KT):
                        last = three(nc, VG[n][:, j * D:(j + 1) * D], [seq(t[:, i, kt, :], n) for t in mix],
                                     weights(i, slice(0, D))(kt), kt == 0, kt == KT - 1)
                last.then_inc(E["vg_t"], 1)

            def scores(c, n, mt):
                if n == 0 and mt == 0:
                    wait(pe, "r", c, 4)
                    wait(pe, "k", c, 2)
                    wait(pe, "yT_lo", c - 1, 2)
                    wait(pe, "h2", c - 1, 2)
                elif mt == 0:
                    wait(pe, "wide", c, QUAD * n)
                for q in range(QUAD):
                    at = slice(32 * q, 32 * q + 32)
                    last = nc.tensor.matmul(SC[q][:, mt * 2 * T:(mt + 1) * 2 * T], seq(kT[at, mt, :], n),
                                            seq(r_eo[at, mt, :, :], n), start=True, stop=True)
                    if mt == KT - 1:
                        last.then_inc(E["s_t"], 1)

            def values(c, n, half):
                if half == 0:
                    wait(pe, "wide", c, QUAD * (n + 1))
                if n == 0:
                    wait(pe, "vg", c, CHUNK)
                for head in range(half * NH // 2, (half + 1) * NH // 2):
                    mt, q, e = head // 8, head % 8 // 2, head % 2
                    at = (n % PAIR) * D + head * DH
                    last = nc.tensor.matmul(Y_BANKS[n // PAIR][:, at:at + DH], weighed[:, n % 2, q * 4 + mt * 2 + e, :],
                                            vg[:, n, 0, head * DH:(head + 1) * DH], start=True, stop=True)
                if half:
                    last.then_inc(E["y_t"], 1)

            def turn_y(c):
                wait(pe, "yg", c, 2)
                turn_tokens(c, yc, None, R_BANKS, "yT_t")

            def project_out(c):
                wait(pe, "yT_lo", c, 2)
                for n in range(CHUNK):
                    at = (n % PAIR) * D
                    for kt in range(KT):
                        last = three(nc, K_BANKS[n // PAIR][:, at:at + D], [seq(t[:, kt, :], n) for t in yT],
                                     weights(O, slice(0, D))(kt), kt == 0, kt == KT - 1)
                    if n % PAIR == 1:
                        last.then_inc(E["o_t"], 1)

            def turn_h2(c):
                turn_tokens(c, hn2, [("hn2", 0), ("hn2_v", 2)], M, "h2T_t")

            def route(c):
                for kt in range(KT):
                    wait(pe, "h2T_lo", c, kt + 1)
                    last = three(nc, LG[0:NE, :], [t[:, kt, :] for t in router], [t[:, kt, :] for t in h2T],
                                 kt == 0, kt == KT - 1)
                last.then_inc(E["lgT_t"], 1)

            def turn_logits(c):
                for n in range(CHUNK):
                    last = nc.tensor.transpose(LG[:, n * NE:(n + 1) * NE], lgT[:, n * T:(n + 1) * T], ident[0:NE, 0:NE])
                last.then_inc(E["lg_t"], 1)

            def moe(c, first, last_):
                for u in range(first, last_):
                    n, pair = divmod(u, NE // 2)
                    if u == 0:
                        wait(pe, "rt", c, 2)
                    if u >= 2:
                        wait(pe, "moe", c, 2 * (u - 1))
                    for kt in range(KT):
                        last = three(nc, M[u % 2][:], [seq(t[:, kt, :], n) for t in h2T],
                                     [t[:, kt, pair * 2 * D:(pair + 1) * 2 * D] for t in experts], kt == 0, kt == KT - 1)
                    last.then_inc(E["moe_t"], 1)

            def step(c, front=True, back=True, more=True):
                p = c - 1
                if front:
                    project_rk(c)
                    project_vg(c, 0)
                    project_vg(c, 1)
                if back:
                    if front:
                        wait(pe, "r", c, 4)
                    turn_y(p)
                if front:
                    project_vg(c, 2)
                if back:
                    if front:
                        wait(pe, "k", c, 2)
                    project_out(p)
                if front:
                    project_vg(c, 3)
                    if more:
                        turn_normed(c + 1)
                    scores(c, 0, 0)
                    scores(c, 0, 1)
                if back:
                    if front:
                        wait(pe, *(("hnT", c + 1, KT) if more else ("vg", c, 2)))
                    turn_h2(p)
                    route(p)

                if not front:
                    wait(pe, "lgT", p, 1)
                    turn_logits(p)
                    moe(p, 0, UNITS)
                    return
                ends = iter((0,) + (UNITS_BETWEEN if more else LATE_UNITS_BETWEEN))
                first = next(ends)

                def fill():
                    nonlocal first
                    end = next(ends)
                    if back:
                        moe(p, first, end)
                    first = end
                for n in range(1, CHUNK):
                    scores(c, n, 0)
                    if n > 1:
                        fill()
                    elif back:
                        wait(pe, "lgT", p, 1)
                    scores(c, n, 1)
                    if n > 1:
                        fill()
                    elif back:
                        turn_logits(p)
                    for half in range(2):
                        values(c, n - 1, half)
                        fill()
                for half in range(2):
                    values(c, CHUNK - 1, half)
                    fill()

            credit(pe, "hnT_t")
            step(0, back=False)
            pe.wait_ge(s_router_lo, 1)
            pe.wait_ge(s_e_lo, NE)
            with pe.Fori(1, NCH - 1) as c:
                step(c)
            step(NCH - 1, more=False)
            step(NCH, front=False)

        @block.scalar
        def _(act):
            def turned(c, name, dst, banks):
                for kt in range(KT):
                    wait(act, name.removesuffix("_hi") + "_t", c, kt + 1)
                    nc.scalar.copy(dst[:, kt, :], banks[kt][:]).then_inc(E[name], 1)

            def vg_out(c, n):
                wait(act, "vg_t", c, n + 1)
                if n == 0:
                    wait(act, "yg", c - 1, 2)
                    wait(act, "gates", c - 1, 2)
                nc.scalar.activation(gate[:, n, :], VG[n][:, D:2 * D], ACT.Tanh, scale=0.5).then_inc(E["tanh"], 1)
                nc.scalar.copy(vg[:, n].rearrange("p j d -> p (j d)"), VG[n][:]).then_inc(E["vg"], 1)

            def normed(c, dst, which, done):
                w = which - 1
                wait(act, f"bias{which}", c, 1)
                for n in range(EVENTS[done]):
                    nc.scalar.activation(dst[:, n, :], rows(c, n).rearrange("p n d -> p (n d)"), ACT.Identity,
                                         bias=nbias[:, w, n:n + 1], scale=rstd[:, w, n:n + 1]).then_inc(E[done], 1)

            def normed_out(c):
                for kt in range(KT):
                    wait(act, "hnT_t", c, kt + 1)
                    nc.scalar.copy(hnT[:, kt, :, 1:T + 1], M[kt][:].rearrange("p (n t) -> p n t", n=CHUNK)).then_inc(E["hnT"], 1)

            def mix_high(c, i):
                wait(act, "mix", c, i + 1)
                nc.scalar.copy(mix[0][:, i], mix_whole[:, i % 2]).then_inc(E["mix_hi"], 1)

            def step(c, front=True, back=True, more=True):
                p = c - 1
                if front:
                    for mt in range(KT):
                        wait(act, "r_t", c, mt + 1)
                        for e in range(2):
                            nc.scalar.mul(r_eo[:, mt, e, :], R_BANKS[mt][:], parity[:, e:e + 1]).then_inc(E["r"], 1)
                    turned(c, "k", kT, K_BANKS)
                    if more:
                        normed(c + 1, hn, 1, "hn")
                    vg_out(c, 0)
                    vg_out(c, 1)
                if back:
                    turned(p, "yT_hi", yT[0], R_BANKS)
                if front:
                    vg_out(c, 2)
                    vg_out(c, 3)
                    if more:
                        normed_out(c + 1)
                if back:
                    normed(p, hn2, 2, "hn2")
                    turned(p, "h2T_hi", h2T[0], M)
                    wait(act, "lgT_t", p, 1)
                    nc.scalar.copy(lgT[:], LG[0:NE, :]).then_inc(E["lgT"], 1)
                    wait(act, "rt", p, 2)
                    nc.scalar.activation(psm[:], lg[:], ACT.Exp).then_inc(E["rexp"], 1)

                def square(q):
                    wait(act, "yc", c, q + 1)
                    nc.scalar.activation(of_pair(ysq, q), of_pair(yc, q), ACT.Square, scale=DH ** -0.5).then_inc(E["sq"], 1)
                if front:
                    if more:
                        mix_high(c + 1, 0)
                    square(0)
                    if more:
                        mix_high(c + 1, 1)
                        mix_high(c + 1, 2)
                    square(1)
                    if more:
                        mix_high(c + 1, 3)

            credit(act, "hn", "hnT")
            for i in range(4):
                mix_high(0, i)
            act.wait_ge(s_in, 4 * 16)
            nc.scalar.copy(router[0][:], router_raw[:]).then_inc(s_router_hi, 1)
            act.wait_ge(s_exp_in, 16)
            for i in range(NE):
                cols = slice(i * D, (i + 1) * D)
                nc.scalar.copy(experts[0][:, :, cols], experts_raw[:, :, cols]).then_inc(s_e_hi, 1)
            step(0, back=False)
            with act.Fori(1, NCH - 1) as c:
                step(c)
            step(NCH - 1, more=False)
            step(NCH, front=False)

        @block.vector
        def _(dve):
            def hold():
                nc.vector.memset(held[:], 0.0)

            def low(c, name, banks, parts):
                for kt in range(KT):
                    wait(dve, name + "_hi", c, kt + 1)
                    hi, lo = [t[:, kt] for t in parts]
                    nc.vector.tensor_tensor(lo, banks[kt][:], hi.bitcast(fp32), ALU.subtract).then_inc(E[name + "_lo"], 1)

            def norm(c, which):
                w = which - 1
                for n in range(CHUNK):
                    nc.vector.bn_stats(stats[:, w, n, :], rows(c, n).rearrange("p n d -> p (n d)")).then_inc(E[f"st{which}"], 1)
                wait(dve, f"st{which}", c, CHUNK)
                hold()
                for n in range(CHUNK):
                    nc.vector.bn_aggr(mv[:, w, n, :], stats[:, w, n, :]).then_inc(E[f"mv{which}"], 1)

            def norm_bias(c, which):
                w = which - 1
                wait(dve, f"rstd{which}", c, 1)
                nc.vector.scalar_tensor_tensor(nbias[:, w, :], mv[:, w, :, 0], -1.0, rstd[:, w, :], ALU.mult,
                                               ALU.mult).then_inc(E[f"bias{which}"], 1)

            def mixes(c):
                for kt in range(KT):
                    wait(dve, "hnT", c, kt + 1)
                    nc.vector.tensor_tensor(xx[:, kt], hnT[:, kt, :, 0:T], hnT[:, kt, :, 1:T + 1], ALU.subtract).then_inc(E["xx"], 1)
                wait(dve, "xx", c, KT)

            def mix_of(c, i):
                if i == 2:
                    wait(dve, "mix_lo", c, 1)
                if i == 3:
                    wait(dve, "mix_lo", c, 2)
                for kt in range(KT):
                    last = nc.vector.scalar_tensor_tensor(
                        mix_whole[:, i % 2, kt].rearrange("p (n t) -> p n t", n=CHUNK), xx[:, kt], maa[:, i, kt:kt + 1],
                        hnT[:, kt, :, 1:T + 1], ALU.mult, ALU.add)
                last.then_inc(E["mix"], 1)

            def mix_low(c, i):
                wait(dve, "mix_hi", c, i + 1)
                hi, lo = [t[:, i] for t in mix]
                nc.vector.tensor_tensor(lo, mix_whole[:, i % 2], hi.bitcast(fp32), ALU.subtract).then_inc(E["last_lo"], 1)

            def weigh(c, n):
                if n >= 2:
                    wait(dve, "y_t", c, n - 1)
                for q in range(QUAD):
                    wait(dve, "s_t", c, QUAD * n + q + 1)
                    nc.vector.tensor_tensor(weighed[:, n % 2, 4 * q:4 * q + 4, :], SC[q][:].rearrange("p (h t) -> p h t", t=T),
                                            decays[:, 4 * q:4 * q + 4, :], ALU.mult).then_inc(E["wide"], 1)

            def heads(t):
                return t.rearrange("p n (h d) -> p (n h) d", d=DH)

            def group_centre(c, p):
                y = Y_BANKS[p][:].rearrange("p (h d) -> p h d", d=DH)
                wait(dve, "y_t", c, PAIR * (p + 1))
                nc.vector.reduce_sum(gsum[:, p, :], y, AX.X).then_inc(E["gsum"], 1)
                wait(dve, "gsum", c, p + 1)
                nc.vector.tensor_scalar(gmean[:, p, :], gsum[:, p, :], 1.0 / DH, None, ALU.mult).then_inc(E["gmean"], 1)
                wait(dve, "gmean", c, p + 1)
                nc.vector.tensor_tensor(heads(of_pair(yc, p)), y, gmean[:, p, :].unsqueeze(2).to_broadcast([P, PAIR * NH, DH]),
                                        ALU.subtract).then_inc(E["yc"], 1)

            def group_var(c, p):
                wait(dve, "sq", c, p + 1)
                nc.vector.reduce_sum(gvar[:, p, :], heads(of_pair(ysq, p)), AX.X).then_inc(E["gsq"], 1)

            def group_out(c, p):
                t = of_pair(yc, p)
                wait(dve, "grstd", c, p + 1)
                nc.vector.tensor_tensor(heads(t), heads(t), grstd[:, p, :].unsqueeze(2).to_broadcast([P, PAIR * NH, DH]),
                                        ALU.mult).then_inc(E["yn"], 1)
                wait(dve, "yn", c, 2 * p + 1)
                wait(dve, "gates", c, p + 1)
                nc.vector.tensor_tensor(t, t, of_pair(gate, p), ALU.mult).then_inc(E["yn"], 1)
                wait(dve, "yn", c, 2 * p + 2)
                nc.vector.tensor_tensor(t, t, of_pair(offs, p), ALU.add).then_inc(E["yg"], 1)

            def residual(c):
                for p in range(2):
                    wait(dve, "o_t", c, p + 1)
                    t = rows(c, PAIR * p, PAIR)
                    nc.vector.tensor_tensor(t, K_BANKS[p][:].rearrange("p (n d) -> p n d", n=PAIR), t, ALU.add).then_inc(E["h2"], 1)
                wait(dve, "h2", c, 2)
                hold()

            def route(c):
                k = [0]

                def did(ins):
                    k[0] += 1
                    ins.then_inc(E["rt"], 1)
                    wait(dve, "rt", c, k[0])
                wait(dve, "lg_t", c, 1)
                logits = LG[:, 0:CHUNK * NE].rearrange("p (n e) -> p n e", n=CHUNK)

                def wide(t):
                    return t.to_broadcast([P, CHUNK, NE])
                did(nc.vector.reduce_max(lmax[:], logits, AX.X))
                did(nc.vector.tensor_tensor(lg[:], logits, wide(lmax[:].unsqueeze(2)), ALU.subtract))
                wait(dve, "rexp", c, 1)
                did(nc.vector.reduce_sum(psum_[:], psm[:], AX.X))
                did(nc.vector.reciprocal(psum_[:], psum_[:]))
                did(nc.vector.tensor_tensor(psm[:], psm[:], wide(psum_[:].unsqueeze(2)), ALU.mult))
                hold()
                for n in range(CHUNK):
                    last = nc.vector.max(top[:, n, :], psm[:, n, :])
                did(last)
                hold()
                for n in range(CHUNK):
                    last = nc.vector.max_index(topi[:, n, :], top[:, n, :], psm[:, n, :])
                did(last)
                nc.vector.tensor_tensor(tsum[:], top[:, :, 0], top[:, :, 1], ALU.add)
                did(nc.vector.tensor_copy(topf[:], topi[:, :, 0:TOPK]))
                did(nc.vector.tensor_scalar(tsum[:], tsum[:], TOP_EPS, None, ALU.add))
                did(nc.vector.reciprocal(tsum[:], tsum[:]))
                did(nc.vector.tensor_tensor(wtop[:], top[:, :, 0:TOPK], tsum[:].unsqueeze(2).to_broadcast([P, CHUNK, TOPK]), ALU.mult))
                for j in range(TOPK):
                    nc.vector.tensor_tensor(pick[:, j], wide(topf[:, :, j:j + 1]), expno[:].unsqueeze(1).to_broadcast([P, CHUNK, NE]),
                                            ALU.is_equal)
                did(nc.vector.tensor_tensor(wprod[:], wtop[:], top[:, :, 0:TOPK], ALU.mult))
                for j in range(TOPK):
                    nc.vector.tensor_tensor(pick[:, j], pick[:, j], wide(wtop[:, :, j:j + 1]), ALU.mult)
                did(nc.vector.tensor_tensor(ebias[:], wprod[:, :, 0], wprod[:, :, 1], ALU.add))
                for n in range(CHUNK):
                    t = rows(c, n).rearrange("p n d -> p (n d)")
                    nc.vector.tensor_scalar(t, t, ebias[:, n:n + 1], None, ALU.add).then_inc(E["acc0"], 1)
                did(nc.vector.tensor_tensor(coef[:], pick[:, 0], pick[:, 1], ALU.add))
                assert k[0] == EVENTS["rt"], k

            def add_experts(c, first, last):
                for u in range(first, last):
                    n, pair = divmod(u, NE // 2)
                    wait(dve, "moe_t", c, u + 1)
                    acc = rows(c, n).rearrange("p n d -> p (n d)")
                    for j in range(2):
                        if pair + j == 0:
                            wait(dve, "acc0", c, n + 1)
                        else:
                            wait(dve, "moe", c, 2 * u + j)
                        nc.vector.scalar_tensor_tensor(acc, M[u % 2][:, j * D:(j + 1) * D],
                                                       coef[:, n, 2 * pair + j:2 * pair + j + 1], acc,
                                                       ALU.mult, ALU.add).then_inc(E["moe"], 1)

            def normed2(c, first, last):
                for n in range(first, last):
                    nc.vector.tensor_scalar(hn2[:, n, :], rows(c, n).rearrange("p n d -> p (n d)"), mv[:, 1, n, 0:1],
                                            rstd[:, 1, n:n + 1], ALU.subtract, ALU.mult).then_inc(E["hn2_v"], 1)

            def step(c, front=True, back=True, more=True):
                p = c - 1

                def fill(first, last):
                    if back:
                        add_experts(p, first, last)
                if front and more:
                    norm(c + 1, 1)
                if back:
                    group_out(p, 0)
                if front and more:
                    norm_bias(c + 1, 1)
                if back:
                    group_out(p, 1)
                    low(p, "yT", R_BANKS, yT)
                    residual(p)
                    norm(p, 2)
                    norm_bias(p, 2)
                    normed2(p, 2, 4)
                if not back:
                    prepare()
                if front:
                    weigh(c, 0)
                if back:
                    low(p, "h2T", M, h2T)
                    route(p)
                if not front:
                    fill(0, UNITS)
                    return
                if not more:
                    for n, units in ((1, (0, 4)), (2, (4, 7)), (3, (7, 10))):
                        weigh(c, n)
                        fill(*units)
                        if n == 2:
                            group_centre(c, 0)
                    group_var(c, 0)
                    group_centre(c, 1)
                    fill(10, 11)
                    group_var(c, 1)
                    fill(11, UNITS)
                    return
                weigh(c, 1)
                fill(0, 2)
                if more:
                    mixes(c + 1)
                    mix_of(c + 1, 0)
                fill(2, 4)
                weigh(c, 2)
                fill(4, 7)
                group_centre(c, 0)
                fill(7, 8)
                if more:
                    mix_of(c + 1, 1)
                weigh(c, 3)
                group_var(c, 0)
                fill(8, 12)
                if more:
                    mix_of(c + 1, 2)
                fill(12, 13)
                group_centre(c, 1)
                fill(13, 14)
                group_var(c, 1)
                fill(14, 15)
                if more:
                    mix_of(c + 1, 3)
                fill(15, 16)
                if more:
                    mix_low(c + 1, 3)

            def prepare():
                dve.wait_ge(s_router_hi, 1)
                nc.vector.tensor_tensor(router[1][:], router_raw[:], router[0][:].bitcast(fp32), ALU.subtract).then_inc(s_router_lo, 1)
                for i in range(NE):
                    dve.wait_ge(s_e_hi, i + 1)
                    hi, lo = [t[:, :, i * D:(i + 1) * D] for t in experts]
                    nc.vector.tensor_tensor(lo, experts_raw[:, :, i * D:(i + 1) * D], hi.bitcast(fp32), ALU.subtract).then_inc(s_e_lo, 1)
                dve.wait_ge(s_e_lo, NE)

            credit(dve, "st1", "mv1", "bias1")
            mixes(0)
            for i in range(4):
                mix_of(0, i)
            mix_low(0, 3)
            dve.wait_ge(s_in, 4 * 16)
            nc.vector.tensor_scalar(affine[:], affine[:], 0.5, None, ALU.mult).then_inc(s_halved, 1)
            step(0, back=False)
            with dve.Fori(1, NCH - 1) as c:
                step(c)
            step(NCH - 1, more=False)
            step(NCH, front=False)


def kernel(x, L0_tok_emb, L0_tok_pes, L0_tok_wq, L0_tok_bq, L0_tok_wk, L0_tok_bk, L0_tok_wv, L0_tok_bv, L0_tok_wo, L0_tok_bo, L0_tok_att_gamma, L0_tok_att_beta, L0_tok_att_mean, L0_tok_att_var, L0_tok_w1, L0_tok_bff1, L0_tok_w2, L0_tok_bff2, L0_tok_ffn_gamma, L0_tok_ffn_beta, L0_tok_ffn_mean, L0_tok_ffn_var,
           L0_attn_w_r, L0_attn_w_k, L0_attn_w_v, L0_attn_w_g, L0_attn_w_o, L0_attn_time_maa_k, L0_attn_time_maa_v,
           L0_attn_time_maa_r, L0_attn_time_maa_g, L0_attn_time_decay, L0_attn_time_faaaa, L0_attn_ln_g, L0_attn_ln_b,
           L0_ffn_router_w, L0_ffn_expert_weights):
    import numpy as np
    import concourse.bacc as bacc
    from concourse.bass_utils import run_bass_kernel_spmd
    A = np.asarray
    w1 = A(L0_tok_w1).reshape(L, KT, P, MT, P).transpose(0, 2, 3, 1, 4).reshape(L, P, MT, KT * P)
    w2 = A(L0_tok_w2).reshape(L, MT, P, D).transpose(0, 2, 1, 3)
    w_ffn = np.concatenate([w1, w2], axis=3)
    w_qkv = np.zeros((P, L, KT, QKVROWS), np.float32)
    qkv_bias = np.zeros((QKVROWS, L), np.float32)
    for row, w, b in ((QROW, L0_tok_wq, L0_tok_bq), (KROW, L0_tok_wk, L0_tok_bk), (VROW, L0_tok_wv, L0_tok_bv)):
        w_qkv[:, :, :, row:row + DK] = A(w).reshape(L, KT, P, DK).transpose(2, 0, 1, 3)
        qkv_bias[row:row + DK] = A(b).T
    w_o = np.zeros((STACK, L, D), np.float32)
    for row in range(0, STACK, 32):
        w_o[row:row + DK] = A(L0_tok_wo).transpose(1, 0, 2)
    kinds = [(L0_tok_att_gamma, L0_tok_ffn_gamma), (L0_tok_att_beta, L0_tok_ffn_beta), (L0_tok_att_mean, L0_tok_ffn_mean),
             (L0_tok_att_var, L0_tok_ffn_var), (L0_tok_bo, L0_tok_bff2)]
    bn_raw = np.stack([np.stack([A(v).reshape(L, KT, P).transpose(2, 0, 1) for v in two], 1) for two in kinds], 1)
    ins = dict(ids=A(x).T, emb=A(L0_tok_emb), pes=A(L0_tok_pes)[:T, 0:1], w_ffn=w_ffn,
               w_qkv=w_qkv.reshape(P, L, KT * QKVROWS), w_o=w_o, bn_raw=bn_raw, qkv_bias=qkv_bias,
               ff_bias=A(L0_tok_bff1).reshape(L, MT, P).transpose(2, 0, 1), ident_in=np.eye(P, dtype=np.float32))

    def feature_rows(w):
        return A(w).T.reshape(KT, P, -1).transpose(1, 0, 2)

    def to_all(v):
        return np.broadcast_to(A(v), (P,) + A(v).shape)

    order = [mt * 8 + q * 2 + e for q in range(QUAD) for mt in range(KT) for e in range(2)]
    key, query = np.arange(T)[:, None], np.arange(T)[None, :]
    ins.update(
        w_exp=A(L0_ffn_expert_weights).reshape(NE, KT, P, D).transpose(2, 1, 0, 3).reshape(P, KT, NE * D),
        w_mix=np.concatenate([feature_rows(w) for w in (L0_attn_w_r, L0_attn_w_k, L0_attn_w_v, L0_attn_w_g, L0_attn_w_o)], 2),
        w_router=feature_rows(L0_ffn_router_w),
        maa_in=np.stack([A(m).reshape(KT, P).T for m in (L0_attn_time_maa_r, L0_attn_time_maa_k, L0_attn_time_maa_v,
                                                         L0_attn_time_maa_g)], 1),
        decay=to_all(A(L0_attn_time_decay)[order]), bonus=to_all(A(L0_attn_time_faaaa)[order]),
        ln_affine=to_all(np.stack([A(L0_attn_ln_g), A(L0_attn_ln_b)])),
        gap=np.maximum(query - key - 1, 0).astype(np.float32), later=(query > key).astype(np.float32),
        even_odd=np.stack([np.arange(P) // DH % 2 == e for e in range(2)], 1).astype(np.float32),
        expert_no=to_all(np.arange(NE, dtype=np.float32)))
    nc = bacc.Bacc("TRN2", target_bir_lowering=False, num_devices=1)
    arrays = {k: np.ascontiguousarray(v) for k, v in ins.items()}
    args = {k: nc.dram_tensor(k, v.shape, mybir.dt.from_np(v.dtype), kind="ExternalInput").ap() for k, v in arrays.items()}
    args["out"] = nc.dram_tensor("out", [NSEQ, T, D], mybir.dt.float32, kind="ExternalOutput").ap()
    tower(nc, **args)
    return run_bass_kernel_spmd(nc, [arrays], core_ids=[0]).results[0]["out"]
```
